# Optimizing a Trainium2 kernel written in Bass

```python
import numpy as np
import jax
import jax.numpy as jnp

def _softmax(x, axis=-1):
    return jax.nn.softmax(x, axis=axis)

def _gelu(x):
    return jax.nn.gelu(x, approximate=True)

def _silu(x):
    return jax.nn.silu(x)

def _sigmoid(x):
    return jax.nn.sigmoid(x)

def _layernorm(x, axis=-1, eps=1e-05):
    m = jnp.mean(x, axis=axis, keepdims=True)
    v = jnp.var(x, axis=axis, keepdims=True)
    return (x - m) / jnp.sqrt(v + eps)

def _scatter_add(tgt, idx, src, axis=0):
    return tgt.at[idx].add(src)

def _segment_sum(src, seg, n):
    return jax.ops.segment_sum(src, seg, n)
kernel_name = 'mk_hybrid_d2_jaxref_r8_54d479'

def setup_inputs(seed: int=0):
    np.random.seed(seed)
    _w = jnp.asarray

    def _L0_attn_a_setup():
        import jax, jax.numpy as jnp
        import numpy as np
        B, N, C, H = (8, 512, 128, 16)
        D = C // H
        EPS = 1e-12

        def _l2norm(x):
            n = jnp.sqrt(jnp.sum(x * x, axis=-1, keepdims=True))
            return x / jnp.maximum(n, EPS)
        key = jax.random.key(seed)
        ks = jax.random.split(key, 5)
        return {'x': jax.random.normal(ks[0], (B, N, C), dtype=jnp.float32), 'qkv_w': jax.random.normal(ks[1], (C, 3 * C), dtype=jnp.float32) * 0.02, 'qkv_b': jax.random.normal(ks[2], (3 * C,), dtype=jnp.float32) * 0.02, 'proj_w': jax.random.normal(ks[3], (C, C), dtype=jnp.float32) * 0.02, 'proj_b': jax.random.normal(ks[4], (C,), dtype=jnp.float32) * 0.02}
    _L0_attn_a_in = _L0_attn_a_setup()

    def _L0_attn_b_setup():
        import jax, jax.numpy as jnp
        import numpy as np
        N_POWER_ITERS = 10

        def _spectral_normalize(W):
            u = jnp.ones((W.shape[0],), W.dtype) / jnp.sqrt(jnp.asarray(W.shape[0], W.dtype))

            def body(u, _):
                v = W.T @ u
                v = v / (jnp.linalg.norm(v) + 1e-12)
                u = W @ v
                u = u / (jnp.linalg.norm(u) + 1e-12)
                return (u, None)
            u, _ = jax.lax.scan(body, u, None, length=N_POWER_ITERS)
            u = jax.lax.stop_gradient(u)
            v = W.T @ u
            v = jax.lax.stop_gradient(v / (jnp.linalg.norm(v) + 1e-12))
            sigma = u @ (W @ v)
            return W / sigma

        def _reference_tuple_inner(x, W_A, W_B, W_C):
            A = _spectral_normalize(W_A)
            Bw = _spectral_normalize(W_B)
            C = _spectral_normalize(W_C)
            xb = jnp.einsum('bti,hi->bth', x, Bw)
            h0 = jnp.zeros((x.shape[0], A.shape[0]), x.dtype)

            def step(h, xb_t):
                h = h @ A.T + xb_t
                return (h, h)
            _, hs = jax.lax.scan(step, h0, jnp.swapaxes(xb, 0, 1))
            hs = jnp.swapaxes(hs, 0, 1)
            ys = jnp.einsum('bth,oh->bto', hs, C)
            return (ys, hs)
        key = jax.random.key(seed)
        k1, k2, k3, k4 = jax.random.split(key, 4)
        B, T, D_in, H, D_out = (32, 128, 128, 128, 128)
        x = jax.random.normal(k1, (B, T, D_in), dtype=jnp.float32)
        W_A = jax.random.normal(k2, (H, H), dtype=jnp.float32) * (1.0 / np.sqrt(H))
        W_B = jax.random.normal(k3, (H, D_in), dtype=jnp.float32) * (1.0 / np.sqrt(D_in))
        W_C = jax.random.normal(k4, (D_out, H), dtype=jnp.float32) * (1.0 / np.sqrt(H))
        return {'x': x, 'W_A': W_A, 'W_B': W_B, 'W_C': W_C}
    _L0_attn_b_in = _L0_attn_b_setup()

    def _L0_ffn_setup():
        import jax, jax.numpy as jnp
        import numpy as np
        H, I, E, K = (128, 64, 32, 8)
        B, S = (4, 128)

        def silu(x):
            return x * jax.nn.sigmoid(x)
        key = jax.random.key(seed)
        ks = jax.random.split(key, 14)

        def w(k, shape, fan_in):
            return jax.random.normal(k, shape, jnp.float32) / np.float32(np.sqrt(fan_in))
        return {'hidden_states': jax.random.normal(ks[0], (B, S, H), jnp.float32), 'Wr': w(ks[1], (H, E), H), 'br': jnp.zeros((E,), jnp.float32), 'Wg_s': w(ks[2], (H, I), H), 'bg_s': jnp.zeros((I,), jnp.float32), 'Wu_s': w(ks[3], (H, I), H), 'bu_s': jnp.zeros((I,), jnp.float32), 'Wd_s': w(ks[4], (I, H), I), 'bd_s': jnp.zeros((H,), jnp.float32), 'Wg': w(ks[5], (E, H, I), H), 'bg': jnp.zeros((E, I), jnp.float32), 'Wu': w(ks[6], (E, H, I), H), 'bu': jnp.zeros((E, I), jnp.float32), 'Wd': w(ks[7], (E, I, H), I), 'bd': jnp.zeros((E, H), jnp.float32)}
    _L0_ffn_in = _L0_ffn_setup()

    def _L1_attn_a_setup():
        import jax, jax.numpy as jnp
        import numpy as np
        B, T, H = (2, 256, 128)
        I, N, R, K = (256, 16, 64, 4)
        EPS = 1e-06
        key = jax.random.key(seed)
        ks = jax.random.split(key, 8)
        s = lambda k, shape, sc=0.02: jax.random.normal(k, shape, dtype=jnp.float32) * sc
        return dict(x=jax.random.normal(ks[0], (B, T, H), dtype=jnp.float32), norm_scale=jnp.ones((H,), jnp.float32), in_w=s(ks[1], (H, 2 * I)), in_b=jnp.zeros((2 * I,), jnp.float32), conv_w=jax.random.normal(ks[2], (K, I), dtype=jnp.float32) / np.float32(np.sqrt(K * I)), conv_b=jnp.zeros((I,), jnp.float32), xproj_w=s(ks[3], (I, R + 2 * N)), dt_w=s(ks[4], (R, I)), dt_b=s(ks[5], (I,), 0.1), A_log=jnp.tile(jnp.log(jnp.arange(1, N + 1, dtype=jnp.float32))[None, :], (I, 1)), D=jnp.ones((I,), jnp.float32), out_w=s(ks[6], (I, H)), out_b=jnp.zeros((H,), jnp.float32))
    _L1_attn_a_in = _L1_attn_a_setup()

    def _L1_attn_b_setup():
        import jax, jax.numpy as jnp
        import numpy as np
        B, S, D, H = (2, 256, 128, 8)
        DQK = D // 2
        DV = D
        DHQK = DQK // H
        DHV = DV // H
        EPS = 1e-06
        GATE_CAP = 15.0

        def soft_cap(x, cap):
            return cap * jnp.tanh(x / cap)

        def _mlstm_parallel_stabilized(q, k, v, i_pre, f_pre):
            s = q.shape[2]
            log_fg = jax.nn.log_sigmoid(f_pre)
            lfc = jnp.cumsum(log_fg, axis=-1)
            log_D = lfc[..., :, None] - lfc[..., None, :] + i_pre[..., None, :]
            causal = jnp.tril(jnp.ones((s, s), dtype=bool))
            log_D = jnp.where(causal, log_D, -jnp.inf)
            m = jnp.max(log_D, axis=-1, keepdims=True)
            Dmat = jnp.exp(log_D - m)
            scores = jnp.einsum('bhsd,bhtd->bhst', q, k) / jnp.sqrt(jnp.float32(q.shape[-1]))
            C = scores * Dmat
            n = jnp.maximum(jnp.abs(jnp.sum(C, axis=-1, keepdims=True)), jnp.exp(-m))
            return jnp.einsum('bhst,bhtd->bhsd', C / (n + EPS), v)
        key = jax.random.key(seed)
        ks = jax.random.split(key, 9)
        std = float(np.sqrt(2.0 / (5.0 * D)))
        return {'x': jax.random.normal(ks[0], (B, S, D), jnp.float32), 'Wq': jax.random.normal(ks[1], (D, DQK), jnp.float32) * std, 'Wk': jax.random.normal(ks[2], (D, DQK), jnp.float32) * std, 'Wv': jax.random.normal(ks[3], (D, DV), jnp.float32) * std, 'Wo': jax.random.normal(ks[4], (D, DV), jnp.float32) * std, 'Wi': jax.random.normal(ks[5], (D, H), jnp.float32) * 0.01, 'bi': jax.random.normal(ks[6], (H,), jnp.float32) * 0.1, 'Wf': jax.random.normal(ks[7], (D, H), jnp.float32) * 0.01, 'bf': jnp.linspace(3.0, 6.0, H, dtype=jnp.float32), 'outnorm_w': jnp.ones((H, DHV), jnp.float32), 'Wdown': jax.random.normal(ks[8], (DV, D), jnp.float32) * std}
    _L1_attn_b_in = _L1_attn_b_setup()

    def _L1_ffn_setup():
        import jax, jax.numpy as jnp
        import numpy as np
        DIM = 128
        HIDDEN = 128
        NUM_EXPERTS = 8
        TOP_K = 2
        key = jax.random.key(seed)
        ks = jax.random.split(key, 8)
        std = 0.02
        x = jax.random.normal(ks[0], (2, 128, DIM), dtype=jnp.float32)
        gate_w = jax.random.normal(ks[1], (NUM_EXPERTS, DIM), dtype=jnp.float32) * std
        w1 = jax.random.normal(ks[2], (NUM_EXPERTS, DIM, HIDDEN), dtype=jnp.float32) * std
        w2 = jax.random.normal(ks[3], (NUM_EXPERTS, HIDDEN, DIM), dtype=jnp.float32) * std
        w3 = jax.random.normal(ks[4], (NUM_EXPERTS, DIM, HIDDEN), dtype=jnp.float32) * std
        w1s = jax.random.normal(ks[5], (1, DIM, HIDDEN), dtype=jnp.float32) * std
        w2s = jax.random.normal(ks[6], (1, HIDDEN, DIM), dtype=jnp.float32) * std
        w3s = jax.random.normal(ks[7], (1, DIM, HIDDEN), dtype=jnp.float32) * std
        return {'x': x, 'gate_w': gate_w, 'w1': w1, 'w2': w2, 'w3': w3, 'w1s': w1s, 'w2s': w2s, 'w3s': w3s}
    _L1_ffn_in = _L1_ffn_setup()
    _d = {'L0_attn_a_x': _L0_attn_a_in['x'], 'L0_attn_a_qkv_w': _L0_attn_a_in['qkv_w'], 'L0_attn_a_qkv_b': _L0_attn_a_in['qkv_b'], 'L0_attn_a_proj_w': _L0_attn_a_in['proj_w'], 'L0_attn_a_proj_b': _L0_attn_a_in['proj_b'], 'L0_attn_b_W_A': _L0_attn_b_in['W_A'], 'L0_attn_b_W_B': _L0_attn_b_in['W_B'], 'L0_attn_b_W_C': _L0_attn_b_in['W_C'], 'L0_ffn_Wr': _L0_ffn_in['Wr'], 'L0_ffn_br': _L0_ffn_in['br'], 'L0_ffn_Wg_s': _L0_ffn_in['Wg_s'], 'L0_ffn_bg_s': _L0_ffn_in['bg_s'], 'L0_ffn_Wu_s': _L0_ffn_in['Wu_s'], 'L0_ffn_bu_s': _L0_ffn_in['bu_s'], 'L0_ffn_Wd_s': _L0_ffn_in['Wd_s'], 'L0_ffn_bd_s': _L0_ffn_in['bd_s'], 'L0_ffn_Wg': _L0_ffn_in['Wg'], 'L0_ffn_bg': _L0_ffn_in['bg'], 'L0_ffn_Wu': _L0_ffn_in['Wu'], 'L0_ffn_bu': _L0_ffn_in['bu'], 'L0_ffn_Wd': _L0_ffn_in['Wd'], 'L0_ffn_bd': _L0_ffn_in['bd'], 'L1_attn_a_norm_scale': _L1_attn_a_in['norm_scale'], 'L1_attn_a_in_w': _L1_attn_a_in['in_w'], 'L1_attn_a_in_b': _L1_attn_a_in['in_b'], 'L1_attn_a_conv_w': _L1_attn_a_in['conv_w'], 'L1_attn_a_conv_b': _L1_attn_a_in['conv_b'], 'L1_attn_a_xproj_w': _L1_attn_a_in['xproj_w'], 'L1_attn_a_dt_w': _L1_attn_a_in['dt_w'], 'L1_attn_a_dt_b': _L1_attn_a_in['dt_b'], 'L1_attn_a_A_log': _L1_attn_a_in['A_log'], 'L1_attn_a_D': _L1_attn_a_in['D'], 'L1_attn_a_out_w': _L1_attn_a_in['out_w'], 'L1_attn_a_out_b': _L1_attn_a_in['out_b'], 'L1_attn_b_Wq': _L1_attn_b_in['Wq'], 'L1_attn_b_Wk': _L1_attn_b_in['Wk'], 'L1_attn_b_Wv': _L1_attn_b_in['Wv'], 'L1_attn_b_Wo': _L1_attn_b_in['Wo'], 'L1_attn_b_Wi': _L1_attn_b_in['Wi'], 'L1_attn_b_bi': _L1_attn_b_in['bi'], 'L1_attn_b_Wf': _L1_attn_b_in['Wf'], 'L1_attn_b_bf': _L1_attn_b_in['bf'], 'L1_attn_b_outnorm_w': _L1_attn_b_in['outnorm_w'], 'L1_attn_b_Wdown': _L1_attn_b_in['Wdown'], 'L1_ffn_gate_w': _L1_ffn_in['gate_w'], 'L1_ffn_w1': _L1_ffn_in['w1'], 'L1_ffn_w2': _L1_ffn_in['w2'], 'L1_ffn_w3': _L1_ffn_in['w3'], 'L1_ffn_w1s': _L1_ffn_in['w1s'], 'L1_ffn_w2s': _L1_ffn_in['w2s'], 'L1_ffn_w3s': _L1_ffn_in['w3s']}
    _x0 = _d['L0_attn_a_x']
    _d['L0_attn_a_x'] = jax.random.normal(jax.random.fold_in(jax.random.key(seed), 1), (4, 1024, 128), dtype=_x0.dtype)
    del _x0
    return _d

def reference(L0_attn_a_x, L0_attn_a_qkv_w, L0_attn_a_qkv_b, L0_attn_a_proj_w, L0_attn_a_proj_b, L0_attn_b_W_A, L0_attn_b_W_B, L0_attn_b_W_C, L0_ffn_Wr, L0_ffn_br, L0_ffn_Wg_s, L0_ffn_bg_s, L0_ffn_Wu_s, L0_ffn_bu_s, L0_ffn_Wd_s, L0_ffn_bd_s, L0_ffn_Wg, L0_ffn_bg, L0_ffn_Wu, L0_ffn_bu, L0_ffn_Wd, L0_ffn_bd, L1_attn_a_norm_scale, L1_attn_a_in_w, L1_attn_a_in_b, L1_attn_a_conv_w, L1_attn_a_conv_b, L1_attn_a_xproj_w, L1_attn_a_dt_w, L1_attn_a_dt_b, L1_attn_a_A_log, L1_attn_a_D, L1_attn_a_out_w, L1_attn_a_out_b, L1_attn_b_Wq, L1_attn_b_Wk, L1_attn_b_Wv, L1_attn_b_Wo, L1_attn_b_Wi, L1_attn_b_bi, L1_attn_b_Wf, L1_attn_b_bf, L1_attn_b_outnorm_w, L1_attn_b_Wdown, L1_ffn_gate_w, L1_ffn_w1, L1_ffn_w2, L1_ffn_w3, L1_ffn_w1s, L1_ffn_w2s, L1_ffn_w3s):

    def _L0_attn_a_ref(x, qkv_w, qkv_b, proj_w, proj_b):
        import jax, jax.numpy as jnp
        import numpy as np
        B, N, C, H = (8, 512, 128, 16)
        D = C // H
        EPS = 1e-12

        def _l2norm(x):
            n = jnp.sqrt(jnp.sum(x * x, axis=-1, keepdims=True))
            return x / jnp.maximum(n, EPS)
        b, n, c = x.shape
        qkv = (x @ qkv_w + qkv_b).reshape(b, n, 3, H, D)
        qkv = jnp.transpose(qkv, (2, 0, 3, 1, 4))
        q, k, v = (qkv[0], qkv[1], qkv[2])
        q = _l2norm(q)
        k = _l2norm(k)
        kv = jnp.einsum('bhnd,bhne->bhde', k, v)
        out = jnp.einsum('bhnd,bhde->bhne', q, kv)
        out = jnp.transpose(out, (0, 2, 1, 3)).reshape(b, n, c)
        return out @ proj_w + proj_b

    def _L0_attn_b_ref(x, W_A, W_B, W_C):
        import jax, jax.numpy as jnp
        import numpy as np
        N_POWER_ITERS = 10

        def _spectral_normalize(W):
            u = jnp.ones((W.shape[0],), W.dtype) / jnp.sqrt(jnp.asarray(W.shape[0], W.dtype))

            def body(u, _):
                v = W.T @ u
                v = v / (jnp.linalg.norm(v) + 1e-12)
                u = W @ v
                u = u / (jnp.linalg.norm(u) + 1e-12)
                return (u, None)
            u, _ = jax.lax.scan(body, u, None, length=N_POWER_ITERS)
            u = jax.lax.stop_gradient(u)
            v = W.T @ u
            v = jax.lax.stop_gradient(v / (jnp.linalg.norm(v) + 1e-12))
            sigma = u @ (W @ v)
            return W / sigma

        def _reference_tuple_inner(x, W_A, W_B, W_C):
            A = _spectral_normalize(W_A)
            Bw = _spectral_normalize(W_B)
            C = _spectral_normalize(W_C)
            xb = jnp.einsum('bti,hi->bth', x, Bw)
            h0 = jnp.zeros((x.shape[0], A.shape[0]), x.dtype)

            def step(h, xb_t):
                h = h @ A.T + xb_t
                return (h, h)
            _, hs = jax.lax.scan(step, h0, jnp.swapaxes(xb, 0, 1))
            hs = jnp.swapaxes(hs, 0, 1)
            ys = jnp.einsum('bth,oh->bto', hs, C)
            return (ys, hs)
        return _reference_tuple_inner(x, W_A, W_B, W_C)[0]

    def _L0_ffn_ref(hidden_states, Wr, br, Wg_s, bg_s, Wu_s, bu_s, Wd_s, bd_s, Wg, bg, Wu, bu, Wd, bd):
        import jax, jax.numpy as jnp
        import numpy as np
        H, I, E, K = (128, 64, 32, 8)
        B, S = (4, 128)

        def silu(x):
            return x * jax.nn.sigmoid(x)
        b, s, h = hidden_states.shape
        T = b * s
        x = hidden_states.reshape(T, h)
        logits = jnp.dot(x.astype(jnp.float32), Wr) + br
        aff = jax.nn.sigmoid(logits)
        top_v, top_i = jax.lax.top_k(aff, K)
        top_w = top_v / (jnp.sum(top_v, axis=-1, keepdims=True) + 1e-09)
        top_w = top_w.astype(hidden_states.dtype)
        e_total = Wr.shape[1]
        w_full = jnp.zeros((T, e_total), hidden_states.dtype)
        w_full = w_full.at[jnp.arange(T)[:, None], top_i].set(top_w)
        shared = jnp.dot(silu(jnp.dot(x, Wg_s) + bg_s) * (jnp.dot(x, Wu_s) + bu_s), Wd_s) + bd_s
        gate = silu(jnp.einsum('th,ehi->eti', x, Wg) + bg[:, None, :])
        up = jnp.einsum('th,ehi->eti', x, Wu) + bu[:, None, :]
        down = jnp.einsum('eti,eih->eth', gate * up, Wd) + bd[:, None, :]
        routed = jnp.einsum('te,eth->th', w_full, down)
        return (shared + routed).reshape(b, s, h)

    def _L1_attn_a_ref(x, norm_scale, in_w, in_b, conv_w, conv_b, xproj_w, dt_w, dt_b, A_log, D, out_w, out_b):
        import jax, jax.numpy as jnp
        import numpy as np
        B, T, H = (2, 256, 128)
        I, N, R, K = (256, 16, 64, 4)
        EPS = 1e-06
        Bsz, Tlen, Hd = x.shape
        Kk, Ii = conv_w.shape
        Nn = A_log.shape[1]
        Rr = dt_w.shape[0]
        xn = x * jax.lax.rsqrt(jnp.mean(x * x, axis=-1, keepdims=True) + EPS) * norm_scale
        proj = xn @ in_w + in_b
        hidden, gate = jnp.split(proj, 2, axis=-1)
        xp = jnp.pad(hidden, ((0, 0), (Kk - 1, 0), (0, 0)))
        conv = sum((conv_w[k] * xp[:, k:k + Tlen, :] for k in range(Kk))) + conv_b
        conv = jax.nn.silu(conv)
        xpj = conv @ xproj_w
        ts = xpj[..., :Rr]
        Bm = xpj[..., Rr:Rr + Nn]
        Cm = xpj[..., Rr + Nn:]
        delta = jax.nn.softplus(ts @ dt_w + dt_b)
        A = -jnp.exp(A_log)
        gate_a = jax.nn.silu(gate)

        def step(state, inp):
            h_t, d_t, g_t, B_t, C_t = inp
            dA = jnp.exp(A[None, :, :] * d_t[:, :, None])
            new = dA * state + d_t[:, :, None] * B_t[:, None, :] * h_t[:, :, None]
            y = jnp.einsum('bin,bn->bi', new, C_t) + D * h_t
            return (new, y * g_t)
        tm = lambda a: jnp.swapaxes(a, 0, 1)
        init = jnp.zeros((Bsz, Ii, Nn), x.dtype)
        _, ys = jax.lax.scan(step, init, (tm(conv), tm(delta), tm(gate_a), tm(Bm), tm(Cm)))
        ssm = jnp.swapaxes(ys, 0, 1)
        return ssm @ out_w + out_b

    def _L1_attn_b_ref(x, Wq, Wk, Wv, Wo, Wi, bi, Wf, bf, outnorm_w, Wdown):
        import jax, jax.numpy as jnp
        import numpy as np
        B, S, D, H = (2, 256, 128, 8)
        DQK = D // 2
        DV = D
        DHQK = DQK // H
        DHV = DV // H
        EPS = 1e-06
        GATE_CAP = 15.0

        def soft_cap(x, cap):
            return cap * jnp.tanh(x / cap)

        def _mlstm_parallel_stabilized(q, k, v, i_pre, f_pre):
            s = q.shape[2]
            log_fg = jax.nn.log_sigmoid(f_pre)
            lfc = jnp.cumsum(log_fg, axis=-1)
            log_D = lfc[..., :, None] - lfc[..., None, :] + i_pre[..., None, :]
            causal = jnp.tril(jnp.ones((s, s), dtype=bool))
            log_D = jnp.where(causal, log_D, -jnp.inf)
            m = jnp.max(log_D, axis=-1, keepdims=True)
            Dmat = jnp.exp(log_D - m)
            scores = jnp.einsum('bhsd,bhtd->bhst', q, k) / jnp.sqrt(jnp.float32(q.shape[-1]))
            C = scores * Dmat
            n = jnp.maximum(jnp.abs(jnp.sum(C, axis=-1, keepdims=True)), jnp.exp(-m))
            return jnp.einsum('bhst,bhtd->bhsd', C / (n + EPS), v)
        b, s, _ = x.shape
        q = (x @ Wq).reshape(b, s, H, DHQK).transpose(0, 2, 1, 3)
        k = (x @ Wk).reshape(b, s, H, DHQK).transpose(0, 2, 1, 3)
        v = (x @ Wv).reshape(b, s, H, DHV).transpose(0, 2, 1, 3)
        o = x @ Wo
        i_pre = soft_cap(x @ Wi + bi, GATE_CAP).transpose(0, 2, 1)
        f_pre = soft_cap(x @ Wf + bf, GATE_CAP).transpose(0, 2, 1)
        h = _mlstm_parallel_stabilized(q, k, v, i_pre, f_pre)
        h = h.transpose(0, 2, 1, 3)
        mu = jnp.mean(h, axis=-1, keepdims=True)
        var = jnp.var(h, axis=-1, keepdims=True)
        h_norm = (h - mu) / jnp.sqrt(var + EPS) * outnorm_w
        h_norm = h_norm.reshape(b, s, -1)
        h_out = jax.nn.sigmoid(o) * h_norm
        return h_out @ Wdown

    def _L1_ffn_ref(x, gate_w, w1, w2, w3, w1s, w2s, w3s):
        import jax, jax.numpy as jnp
        import numpy as np
        DIM = 128
        HIDDEN = 128
        NUM_EXPERTS = 8
        TOP_K = 2
        bs, slen, dim = x.shape
        xt = x.reshape(bs * slen, dim)
        logits = xt @ gate_w.T
        scores = jax.nn.softmax(logits.astype(jnp.float32), axis=1).astype(x.dtype)
        top_scores, sel = jax.lax.top_k(scores, TOP_K)
        sel_flat = sel.reshape(-1)
        order = jnp.argsort(sel_flat, stable=True)
        top_scores_sorted = top_scores.reshape(-1)[order]
        token_idx = order // TOP_K
        eid = sel_flat[order]
        routed_in = xt[token_idx] * top_scores_sorted[:, None]
        out_routed = jnp.zeros_like(routed_in)
        for e in range(NUM_EXPERTS):
            m = (eid == e)[:, None]
            xe = jnp.where(m, routed_in, 0.0)
            h = jax.nn.silu(xe @ w1[e]) * (xe @ w3[e])
            out_routed = out_routed + jnp.where(m, h @ w2[e], 0.0)
        hs = jax.nn.silu(xt @ w1s[0]) * (xt @ w3s[0])
        out = hs @ w2s[0]
        out = out.at[token_idx].add(out_routed)
        return out.reshape(bs, slen, dim)
    x = L0_attn_a_x
    x = x + _L0_attn_a_ref(_layernorm(x, axis=-1), L0_attn_a_qkv_w, L0_attn_a_qkv_b, L0_attn_a_proj_w, L0_attn_a_proj_b)
    x = x + _L0_ffn_ref(_layernorm(x, axis=-1), L0_ffn_Wr, L0_ffn_br, L0_ffn_Wg_s, L0_ffn_bg_s, L0_ffn_Wu_s, L0_ffn_bu_s, L0_ffn_Wd_s, L0_ffn_bd_s, L0_ffn_Wg, L0_ffn_bg, L0_ffn_Wu, L0_ffn_bu, L0_ffn_Wd, L0_ffn_bd)
    x = x + _L0_attn_b_ref(_layernorm(x, axis=-1), L0_attn_b_W_A, L0_attn_b_W_B, L0_attn_b_W_C)
    x = x + _L0_ffn_ref(_layernorm(x, axis=-1), L0_ffn_Wr, L0_ffn_br, L0_ffn_Wg_s, L0_ffn_bg_s, L0_ffn_Wu_s, L0_ffn_bu_s, L0_ffn_Wd_s, L0_ffn_bd_s, L0_ffn_Wg, L0_ffn_bg, L0_ffn_Wu, L0_ffn_bu, L0_ffn_Wd, L0_ffn_bd)
    x = x + _L1_attn_a_ref(_layernorm(x, axis=-1), L1_attn_a_norm_scale, L1_attn_a_in_w, L1_attn_a_in_b, L1_attn_a_conv_w, L1_attn_a_conv_b, L1_attn_a_xproj_w, L1_attn_a_dt_w, L1_attn_a_dt_b, L1_attn_a_A_log, L1_attn_a_D, L1_attn_a_out_w, L1_attn_a_out_b)
    x = x + _L1_ffn_ref(_layernorm(x, axis=-1), L1_ffn_gate_w, L1_ffn_w1, L1_ffn_w2, L1_ffn_w3, L1_ffn_w1s, L1_ffn_w2s, L1_ffn_w3s)
    x = x + _L1_attn_b_ref(_layernorm(x, axis=-1), L1_attn_b_Wq, L1_attn_b_Wk, L1_attn_b_Wv, L1_attn_b_Wo, L1_attn_b_Wi, L1_attn_b_bi, L1_attn_b_Wf, L1_attn_b_bf, L1_attn_b_outnorm_w, L1_attn_b_Wdown)
    x = x + _L1_ffn_ref(_layernorm(x, axis=-1), L1_ffn_gate_w, L1_ffn_w1, L1_ffn_w2, L1_ffn_w3, L1_ffn_w1s, L1_ffn_w2s, L1_ffn_w3s)
    return x

_drawn_inputs = setup_inputs


def setup_inputs(seed=0):
    import zlib

    import numpy as np

    out = dict(_drawn_inputs(seed))
    spreads = {'L0_ffn_br': (0.0, 0.1),
     'L0_ffn_bg_s': (0.0, 0.1),
     'L0_ffn_bu_s': (0.0, 0.1),
     'L0_ffn_bd_s': (0.0, 0.1),
     'L0_ffn_bg': (0.0, 0.387),
     'L0_ffn_bu': (0.0, 0.392),
     'L0_ffn_bd': (0.0, 0.1),
     'L1_attn_a_norm_scale': (1.0, 0.6),
     'L1_attn_a_in_b': (0.0, 0.8),
     'L1_attn_a_conv_b': (0.0, 0.8),
     'L1_attn_a_D': (1.0, 0.6),
     'L1_attn_a_out_b': (0.0, 0.8),
     'L1_attn_b_outnorm_w': (1.0, 0.6)}
    factors = {'L0_attn_a_proj_b': 3.164,
     'L1_attn_a_in_w': 8.0,
     'L1_attn_a_conv_w': 8.0,
     'L1_attn_a_xproj_w': 8.0,
     'L1_attn_a_dt_w': 8.0,
     'L1_attn_a_dt_b': 8.0,
     'L1_attn_a_A_log': 8.0,
     'L1_attn_a_out_w': 8.0,
     'L1_attn_b_Wi': 200.0,
     'L1_attn_b_bi': 200.0,
     'L1_attn_b_Wf': 200.0,
     'L1_ffn_gate_w': 60.708,
     'L1_ffn_w1': 62.233,
     'L1_ffn_w2': 58.377,
     'L1_ffn_w3': 59.109,
     'L1_ffn_w1s': 26.589,
     'L1_ffn_w2s': 23.781,
     'L1_ffn_w3s': 23.51,
     'L1_attn_b_Wq': 58.068,
     'L1_attn_b_Wk': 56.958,
     'L1_attn_b_Wv': 52.785,
     'L1_attn_b_Wo': 64.0,
     'L1_attn_b_bf': 64.0,
     'L1_attn_b_Wdown': 53.897}
    for name, (base, spread) in spreads.items():
        noise = np.random.default_rng([zlib.crc32(name.encode()), seed]).standard_normal(out[name].shape)
        drawn = base * np.exp(spread * noise) if base else spread * noise
        out[name] = jnp.asarray(drawn.astype(out[name].dtype))
    for name, factor in factors.items():
        out[name] = (out[name] * factor).astype(out[name].dtype)
    return out
```

```python
import concourse.bass as bass
from concourse import mybir
from contextlib import ExitStack

FP32 = mybir.dt.float32
FP32R = mybir.dt.float32r
BF16 = mybir.dt.bfloat16
ALU = mybir.AluOpType
ACT = mybir.ActivationFunctionType
AX = mybir.AxisListType

P = 128
NB, NT, C = 4, 1024, 128
SPB = NT // P
TILES = NB * SPB
SUP = 4
NSUP = TILES // SUP
W = SUP * P
LN_EPS = 1e-5

E0, I0, TOP0 = 32, 64, 8
PAIRS = E0 // 2
SLOTS0 = PAIRS + 1
E1, I1, TOP1 = 8, 128, 2
SLOTS1 = E1 + 1
SSM_N, SSM_R, SSM_K = 16, 64, 4
LIN_H, LIN_D = 16, 8
MH, MQK, MV = 8, 8, 16
MV1 = MV + 1
GATE_CAP = 15.0
CHUNKS = NT // P
FAR = -1e30
AHEAD = 3

ORDER = ["setup", "lin", "ffn0", "rnn", "ffn0", "ssm", "ffn1", "mlstm", "ffn1"]


def build(nc, A, out, order=ORDER):
    ctx = ExitStack()
    with ctx:
        def sem(name):
            return ctx.enter_context(nc.semaphore(name))

        def sb(name, shape, dt=FP32, where=ctx):
            return where.enter_context(nc.sbuf_tensor(name, shape, dt))

        X = sb("X", [P, TILES, C])
        ident = sb("ident", [P, P])
        identb = sb("identb", [P, P], BF16)
        settle_cell = sb("settle_cell", [P, 1])
        ln_stats = sb("ln_stats", [P, SUP, 6])
        ln_mv = sb("ln_mv", [P, SUP, 2])
        ln_var = sb("ln_var", [P, SUP])
        ln_rstd = sb("ln_rstd", [P, SUP])
        minus_half = sb("minus_half", [P, P])
        xn = sb("xn", [P, SUP, C])
        f1_hi = sb("f1_hi", [P, 3, SLOTS1, P], FP32R)
        f1_lo = sb("f1_lo", [P, 3, SLOTS1, P], FP32R)
        sel1 = sb("sel1", [3 * E1, E1, P], BF16)
        gate1_w = sb("gate1_w", [P, E1])
        sel0 = sb("sel0", [3 * E0, PAIRS, P], BF16)
        router0_w = sb("router0_w", [P, E0])
        router0_b = sb("router0_b", [E0, 1])
        bg_sb = sb("bg_sb", [P, SLOTS0])
        bu_sb = sb("bu_sb", [P, SLOTS0])
        bd_raw = sb("bd_raw", [3 * E0 + 1, P])
        bd_rest = sb("bd_rest", [3 * E0 + 1, P])
        bd_parts = sb("bd_parts", [3 * E0 + 1, 3, P], BF16)
        lin_qkv_w = sb("lin_qkv_w", [P, 3 * C])
        lin_qkv_b = sb("lin_qkv_b", [P, 3 * C])
        lin_proj_w = sb("lin_proj_w", [P, C])
        lin_proj_b = sb("lin_proj_b", [P, C])
        rnn_w = sb("rnn_w", [P, 3, P])
        ssm_in_w = sb("ssm_in_w", [P, 4 * P])
        ssm_xproj = sb("ssm_xproj", [P, 2, SSM_R])
        ssm_xbc = sb("ssm_xbc", [P, 2, 96])
        ssm_dt_w = sb("ssm_dt_w", [SSM_R, 2 * P])
        ssm_out_w = sb("ssm_out_w", [P, 2, C])
        ssm_out_b = sb("ssm_out_b", [P, C])
        ssm_A_log = sb("ssm_A_log", [P, 2, SSM_N])
        ssm_norm = sb("ssm_norm", [P, 1])
        ssm_in_b = sb("ssm_in_b", [P, 4])
        ssm_conv_w = sb("ssm_conv_w", [P, 2, SSM_K])
        ssm_conv_b = sb("ssm_conv_b", [P, 2])
        ssm_dt_b = sb("ssm_dt_b", [P, 2])
        ssm_D = sb("ssm_D", [P, 2])
        ml_qk_w = sb("ml_qk_w", [P, 2, MH * MQK])
        ml_ovk_w = sb("ml_ovk_w", [P, 2 * C + MH * MQK])
        ml_if_w = sb("ml_if_w", [P, 2, MH])
        ml_if_b = sb("ml_if_b", [2, MH])
        ml_norm_w = sb("ml_norm_w", [P, C])
        ml_down_w = sb("ml_down_w", [P, C])
        turns = []

        def turn(name, rows, width, src, dst):
            turns.append((sb(name, [rows, width])[:, :], dst, src))

        def row(ap):
            return ap.rearrange("(a n) -> a n", a=1)

        for n, dst in (("bg", bg_sb), ("bu", bu_sb)):
            turn(f"{n}_rows", PAIRS, P, A["L0_ffn_" + n].rearrange("(a e) i -> a (e i)", e=2), dst[:, 0:PAIRS])
            turn(f"{n}s_row", 1, I0, row(A[f"L0_ffn_{n}_s"]), dst[0:I0, PAIRS:SLOTS0])
        turn("br_row", 1, E0, row(A["L0_ffn_br"]), router0_b[:, :])
        a = "L1_attn_a_"
        turn("norm_row", 1, P, row(A[a + "norm_scale"]), ssm_norm[:, :])
        turn("in_b_rows", 4, P, A[a + "in_b"].rearrange("(k p) -> k p", p=P), ssm_in_b[:, :])
        for blk in range(2):
            turn(f"conv_w_rows{blk}", SSM_K, P, A[a + "conv_w"][:, blk * P:(blk + 1) * P], ssm_conv_w[:, blk, :])
        turn("conv_b_rows", 2, P, A[a + "conv_b"].rearrange("(k p) -> k p", p=P), ssm_conv_b[:, :])
        turn("dt_b_rows", 2, P, A[a + "dt_b"].rearrange("(k p) -> k p", p=P), ssm_dt_b[:, :])
        turn("D_rows", 2, P, A[a + "D"].rearrange("(k p) -> k p", p=P), ssm_D[:, :])
        turn("gate1_rows", E1, P, A["L1_ffn_gate_w"], gate1_w[:, :])

        banks = [ctx.enter_context(nc.psum_tensor(f"bank{i}", [P, 512], FP32)) for i in range(8)]

        region = ExitStack()
        f0_hi = sb("f0_hi", [P, 3, PAIRS, P], FP32R, region)
        f0_lo = sb("f0_lo", [P, 3, PAIRS, P], FP32R, region)
        f0s_hi = sb("f0s_hi", [P, 3, P], FP32R, region)
        f0s_lo = sb("f0s_lo", [P, 3, P], FP32R, region)
        inner = ExitStack()
        st0 = sb("st0", [P, 3, PAIRS, P], where=inner)
        st0s = sb("st0s", [P, 3, P], where=inner)
        st1 = sb("st1", [P, 3, SLOTS1, P], where=inner)
        inner.close()
        inner = ExitStack()
        mlp = {}
        for n, shape, dt in (("xT", [P, W], FP32), ("xh", [P, 2, W], FP32R), ("xl", [P, 2, W], FP32R),
                             ("aff", [P, W], FP32), ("top", [P, SUP, 8], FP32), ("rep", [P, SUP, E0], FP32), ("rep1", [P, SUP, E1 + 8 - TOP1], FP32),
                             ("sum", [P, SUP], FP32), ("rsum", [P, SUP], FP32), ("mxl", [P, SUP], FP32),
                             ("w", [P, SUP, E0], FP32), ("s", [P, SUP, E1 + 8 - TOP1], FP32), ("rest", [P, SUP, E0], FP32),
                             ("w3", [P, SUP, 3 * E0 + 1], BF16), ("w3_1", [P, SUP, 3 * E1], BF16),
                             ("wT", [P, 2, W], BF16), ("sil", [P, 2, W], FP32), ("gs", [P, 2, W], FP32), ("wb", [P, 2, W], FP32),
                             ("t1", [P, 2, W], FP32), ("h", [P, 2, W], FP32), ("hh", [P, 2, W], FP32R),
                             ("hl", [P, 2, W], FP32R), ("yT", [P, W], FP32)):
            mlp[n] = sb("mlp_" + n, shape, dt, inner)
        inner.close()
        inner = ExitStack()
        lin = {n: sb("lin_" + n, shape, dt, inner) for n, shape, dt in (
            ("xT", [P, W], FP32), ("qkv", [P, 2, SUP, 3 * C], FP32), ("sq", [P, SUP, 2 * C], FP32),
            ("ss", [P, SUP, 2 * LIN_H], FP32), ("rn", [P, SUP, 2 * LIN_H], FP32), ("qT", [P, 2, W], FP32),
            ("kvm", [P, C], FP32), ("m", [P, C], FP32), ("blocks", [P, C], FP32))}
        inner.close()
        inner = ExitStack()
        rnn = {n: sb("rnn_" + n, shape, FP32, inner) for n, shape in (
            ("u", [P, 3]), ("v", [P, 3]), ("raw", [P, 3]), ("sq", [P, 3]), ("norm", [P, 3]), ("norm1", [P, 3]), ("inv", [P, 3]),
            ("isig", [P, 3]), ("ones", [P, P]), ("wT", [P, 3, P]), ("CT", [P, P]), ("xT", [P, 2, W]), ("U", [P, NB, SPB, P]),
            ("carry", [P, NB, P + 1]), ("L", [P, 10, P]), ("R", [P, 13, P]), ("G", [P, SPB, P]))}
        inner.close()
        region.close()
        region = ExitStack()
        ssm = {n: sb("ssm_" + n, shape, dt, region) for n, shape, dt in (
            ("ms", [P, SUP], FP32), ("ms2", [P, SUP], FP32), ("xT", [P, NT], FP32), ("hp", [P, 2, 2, W + SSM_K - 1], FP32),
            ("gs", [P, 2, 2, W], FP32), ("cv", [P, 2, 2, W], FP32), ("ts", [SSM_R, W], FP32), ("v0", [96, W], FP32),
            ("r", [96, W], FP32), ("bc", [96, 2, W], BF16), ("zb", [P, 2, W], FP32), ("ez", [P, 2, W], FP32), ("uz", [P, 2, W], FP32), ("lz", [P, 2, W], FP32),
            ("delta", [P, 2, 2, W], FP32), ("du", [P, 2, 2, W], FP32), ("negA", [P, 2, SSM_N], FP32),
            ("last", [P, 2 * SSM_N], FP32), ("bs", [P, 2, W], FP32), ("da", [P, 4, W], FP32), ("dbu", [P, 4, W], FP32),
            ("st", [P, 4, W], FP32), ("sc", [P, 4, W], FP32), ("y2", [P, 2, W], FP32), ("yb", [P, 2, NT], FP32),
            ("sel", [96, 32, P], BF16), ("diag", [P, 2, SSM_K, P], FP32))}
        region.close()
        region = ExitStack()
        ml = {n: sb("ml_" + n, shape, dt, region) for n, shape, dt in (
            ("brows", [2, P], FP32), ("bcols", [P, 2], FP32), ("if_pad", [P, 2, 32], FP32), ("qk_pad", [P, 2, 2, P], FP32),
            ("ones", [P, P], BF16), ("indf", [P, MH], FP32), ("ind", [P, MH], BF16), ("head", [P, MH], FP32), ("heads", [P, 2, P], FP32), ("blocks", [P, 4], FP32),
            ("causal", [P, P], BF16), ("later", [P, 2], FP32), ("restart", [P, NT], FP32),
            ("xT", [P, NB * NT], FP32),
            ("i", [P, NT], FP32), ("f", [P, NT], FP32), ("e", [P, NT], FP32), ("u", [P, NT], FP32), ("l", [P, NT], FP32),
            ("m", [P, NT], FP32), ("a", [P, NT], FP32), ("b", [P, NT], FP32),
            ("part", [P, NT], BF16), ("a3", [P, NT], BF16), ("b3", [P, NT], BF16), ("mprev", [P, CHUNKS], FP32),
            ("WT", [P, CHUNKS * NB * MH], FP32), ("RT", [P, CHUNKS * NB * MH], FP32), ("eT", [P, CHUNKS * NB * MH], FP32),
            ("decay", [P, CHUNKS * 2 * NB], FP32), ("S", [P, NB, 2, 4 * MV1], FP32),
            ("xc", [P, 2, W], FP32), ("ac", [P, 2, P], BF16), ("bm", [P, 2, MH, P], BF16),
            ("qT", [P, 2, 2, W], FP32), ("kT", [P, 2, 2, W], FP32), ("eo", [P, 2, NB, C], FP32), ("v1", [P, 2, MH, MV1], FP32),
            ("k", [P, 2, MH * MQK], FP32), ("kw", [P, 2, MH, 32], FP32), ("D", [P, 2, MH * P], FP32),
            ("t1", [P, 2, MH * MV1], FP32), ("um", [P, 2, MH * MV1], FP32), ("T", [P, 2, NB, MH, MV1], FP32),
            ("n", [P, NB, MH], FP32), ("h", [P, NB, MH, MV], FP32), ("mu", [P, NB, MH], FP32), ("hc", [P, NB, MH, MV], FP32),
            ("sq", [P, NB, MH, MV], FP32), ("var", [P, NB, MH], FP32), ("rstd", [P, NB, MH], FP32),
            ("hw", [P, NB, MH, MV], FP32), ("eo1", [P, NB, C], FP32), ("y", [P, NB, C], FP32))}
        region.close()
        rnn["w"] = rnn_w
        lin["qkv_w"], lin["qkv_b"], lin["proj_w"], lin["proj_b"] = lin_qkv_w, lin_qkv_b, lin_proj_w, lin_proj_b

        loaded = sem("loaded")
        x_loaded = sem("x_loaded")
        consts_ready = sem("consts_ready")
        consts_step = sem("consts_step")
        hi_split = sem("hi_split")
        lo_split = sem("lo_split")
        bd_step = sem("bd_step")
        rows_turned = sem("rows_turned")
        stored = sem("stored")
        phase_done = sem("phase_done")

        ln_stats_done = sem("ln_stats_done")
        ln_mv_done = sem("ln_mv_done")
        ln_var_done = sem("ln_var_done")
        ln_rstd_done = sem("ln_rstd_done")
        xn_ready = sem("xn_ready")
        xn_turned = sem("xn_turned")
        xT_ready = sem("xT_ready")

        l_const, l_qkv, l_biased, l_sq, l_ss, l_rn, l_unit, l_qt, l_qT, l_kv, l_kvm, l_m, l_mb, l_out, l_add, l_pb = (
            sem("l_" + n) for n in (
                "const",
                "qkv",
                "biased",
                "sq",
                "ss",
                "rn",
                "unit",
                "qt", "qT",
                "kv", "kvm",
                "m", "mb",
                "out", "add",
                "pb"))
        p_turned, p_wT, p_vec, p_raw, p_sq, p_sum, p_norm, p_sigma, p_scaled = (
            sem("p_" + n) for n in (
                "turned", "wT",
                "vec",
                "raw",
                "sq", "sum",
                "norm",
                "sigma",
                "scaled"))
        r_bx, r_u, r_step, r_stepped, r_pow, r_power, r_jump, r_carried, r_out, r_add = (
            sem("r_" + n) for n in (
                "bx", "u",
                "step", "stepped",
                "pow", "power",
                "jump", "carried",
                "out", "add"))

        (s_const, s_diag, s_rms, s_rpow, s_prod, s_evac, s_split, s_soft, s_delta, s_du, s_bb, s_bc, s_bs, s_da, s_dbu, s_scan,
         s_mult, s_acc, s_y, s_y3, s_out, s_oadd, s_pb) = (sem("s_" + n) for n in (
             "const",
             "diag",
             "rms", "rpow",
             "prod", "evac",
             "split",
             "soft",
             "delta", "du",
             "bb", "bc",
             "bs",
             "da",
             "dbu",
             "scan",
             "mult",
             "acc",
             "y", "y3",
             "out", "oadd",
             "pb"))

        (g_const, g_ind, g_pconst, g_bias, g_gate, g_rows, g_turn, g_xc, g_bm, g_b0, g_b0used, g_ovk, g_ovkused, g_kw, g_e, g_D, g_s,
         g_c, g_o, g_t, g_T, g_state, g_post, g_sq, g_pow, g_y, g_down, g_add) = (sem("g_" + n) for n in (
             "const",
             "ind",
             "pconst",
             "bias",
             "gate",
             "rows",
             "turn",
             "xc", "bm",
             "b0", "b0used",
             "ovk", "ovkused",
             "kw",
             "e", "D",
             "s", "c",
             "o",
             "t", "T",
             "state",
             "post",
             "sq", "pow",
             "y",
             "down", "add"))

        consts = []

        n_loads = [0]

        def load(eng, dst, src, s=loaded):
            eng.dma_start(dst, src).then_inc(s, 16)
            if s is loaded:
                n_loads[0] += 1

        def setup_sync(e):
            for b in range(NB):
                load(e, X[:, b * SPB:(b + 1) * SPB, :], A["L0_attn_a_x"][b].rearrange("(j s) c -> j s c", s=SPB), x_loaded)
            for k, n in enumerate(("Wg", "Wu")):
                load(e, st0[:, k, :, :].rearrange("p a (e i) -> p (a e) i", e=2), A["L0_ffn_" + n].rearrange("e h i -> h e i"))
                load(e, st0s[:, k, 0:I0], A[f"L0_ffn_{n}_s"])
            load(e, st0[:, 2, :, :], A["L0_ffn_Wd"].rearrange("(a e) i h -> (e i) a h", e=2))
            load(e, st0s[0:I0, 2, :], A["L0_ffn_Wd_s"])
            for k, n in enumerate(("w1", "w3", "w2")):
                load(e, st1[:, k, 0:E1, :], A["L1_ffn_" + n].rearrange("e d h -> d e h"))
                load(e, st1[:, k, E1, :], A[f"L1_ffn_{n}s"][0])
            load(e, router0_w[:, :], A["L0_ffn_Wr"])
            for raw, _, src in turns:
                load(e, raw, src)
            for j in range(3):
                load(e, bd_raw[j * E0:(j + 1) * E0, :], A["L0_ffn_bd"])
            load(e, bd_raw[3 * E0:3 * E0 + 1, :], A["L0_ffn_bd_s"].rearrange("(a h) -> a h", a=1))
            load_more(e)

        POOL_CONSTS = [0]

        def setup_pool(e):
            n = [0]

            def step(i):
                n[0] += 1
                i.then_inc(consts_step, 1)
                e.wait_ge(consts_step, n[0])

            step(nc.gpsimd.memset(ident[:, :], 0.0))
            step(nc.gpsimd.affine_select(out=ident[:, :], in_=ident[:, :], compare_op=ALU.not_equal, fill=1.0,
                                         base=0, pattern=[[-1, P]], channel_multiplier=1))
            step(nc.gpsimd.tensor_copy(identb[:, :], ident[:, :]))
            step(nc.gpsimd.memset(minus_half[:, :], -0.5))
            step(nc.gpsimd.memset(sel0[:, :, :], 0.0))
            for j in range(3):
                step(nc.gpsimd.affine_select(out=sel0[:, :, :], in_=sel0[:, :, :], compare_op=ALU.not_equal, fill=1.0,
                                             base=-E0 * j, pattern=[[-2, PAIRS], [-1, 2], [0, I0]], channel_multiplier=1))
            step(nc.gpsimd.memset(sel1[:, :, :], 0.0))
            for j in range(3):
                step(nc.gpsimd.affine_select(out=sel1[:, :, :], in_=sel1[:, :, :], compare_op=ALU.not_equal, fill=1.0,
                                             base=-E1 * j, pattern=[[-1, E1], [0, P]], channel_multiplier=1))
            more_consts(step)
            e.sem_inc(consts_ready, 1)

        def setup_scalar(e):
            e.wait_ge(loaded, 16 * n_loads[0])
            for k in range(3):
                nc.scalar.activation(f0_hi[:, k, :, :], st0[:, k, :, :], ACT.Copy).then_inc(hi_split, 1)
                kk = I0 if k == 2 else P
                nn = P if k == 2 else I0
                nc.scalar.activation(f0s_hi[0:kk, k, 0:nn], st0s[0:kk, k, 0:nn], ACT.Copy).then_inc(hi_split, 1)
            for k in range(3):
                nc.scalar.activation(f1_hi[:, k, :, :], st1[:, k, :, :], ACT.Copy).then_inc(hi_split, 1)
            nc.scalar.activation(bd_parts[:, 0, :], bd_raw[:, :], ACT.Copy).then_inc(bd_step, 1)

        def setup_vector(e):
            e.wait_ge(loaded, 16 * n_loads[0])
            for k in range(3):
                e.wait_ge(hi_split, 2 * k + 1)
                nc.vector.tensor_tensor(f0_lo[:, k, :, :], st0[:, k, :, :], f0_hi[:, k, :, :].bitcast(FP32),
                                        ALU.subtract).then_inc(lo_split, 1)
                kk = I0 if k == 2 else P
                nn = P if k == 2 else I0
                e.wait_ge(hi_split, 2 * k + 2)
                nc.vector.tensor_tensor(f0s_lo[0:kk, k, 0:nn], st0s[0:kk, k, 0:nn], f0s_hi[0:kk, k, 0:nn].bitcast(FP32),
                                        ALU.subtract).then_inc(lo_split, 1)
            for k in range(3):
                e.wait_ge(hi_split, 7 + k)
                nc.vector.tensor_tensor(f1_lo[:, k, :, :], st1[:, k, :, :], f1_hi[:, k, :, :].bitcast(FP32),
                                        ALU.subtract).then_inc(lo_split, 1)
            e.wait_ge(bd_step, 1)
            nc.vector.tensor_tensor(bd_rest[:, :], bd_raw[:, :], bd_parts[:, 0, :], ALU.subtract).then_inc(bd_step, 1)
            e.wait_ge(bd_step, 2)
            nc.vector.tensor_copy(bd_parts[:, 1, :], bd_rest[:, :]).then_inc(bd_step, 1)
            e.wait_ge(bd_step, 3)
            nc.vector.tensor_tensor(bd_parts[:, 2, :], bd_rest[:, :], bd_parts[:, 1, :], ALU.subtract).then_inc(bd_step, 1)
            e.wait_ge(rows_turned, 1)
            at = 0
            for raw, dst, _ in turns:
                r, n = raw.shape
                nc.vector.tensor_copy(dst, banks[0][0:n, at:at + r])
                at += r

        def setup_tensor(e):
            e.wait_ge(loaded, 16 * n_loads[0])
            e.wait_ge(consts_ready, 1)
            at = 0
            for raw, _, _ in turns:
                r, n = raw.shape
                last = nc.tensor.transpose(banks[0][0:n, at:at + r], raw, ident[0:r, 0:r])
                at += r
            last.then_inc(rows_turned, 1)

        def load_more(e):
            load(e, lin_qkv_w[:, :], A["L0_attn_a_qkv_w"])
            load(e, lin_qkv_b[:, :], row(A["L0_attn_a_qkv_b"]).to_broadcast([P, 3 * C]))
            load(e, lin_proj_w[:, :], A["L0_attn_a_proj_w"])
            load(e, lin_proj_b[:, :], row(A["L0_attn_a_proj_b"]).to_broadcast([P, C]))
            for k, n in enumerate("ABC"):
                load(e, rnn_w[:, k, :], A["L0_attn_b_W_" + n])
            a = "L1_attn_a_"
            load(e, ssm_in_w[:, :], A[a + "in_w"])
            xw = A[a + "xproj_w"].rearrange("(k p) n -> p k n", p=P)
            load(e, ssm_xproj[:, :, :], xw[:, :, 0:SSM_R])
            for j in range(3):
                load(e, ssm_xbc[:, :, 32 * j:32 * (j + 1)], xw[:, :, SSM_R:SSM_R + 32])
            load(e, ssm_dt_w[:, :], A[a + "dt_w"])
            load(e, ssm_out_w[:, :, :], A[a + "out_w"].rearrange("(k p) n -> p k n", p=P))
            load(e, ssm_out_b[:, :], row(A[a + "out_b"]).to_broadcast([P, C]))
            a2 = "L1_attn_b_"
            for k, n in enumerate(("Wq", "Wk")):
                load(e, ml_qk_w[:, k, :], A[a2 + n])
            for n, at, width in (("Wo", 0, C), ("Wv", C, C), ("Wk", 2 * C, MH * MQK)):
                load(e, ml_ovk_w[:, at:at + width], A[a2 + n])
            for k, n in enumerate("if"):
                load(e, ml_if_w[:, k, :], A[a2 + "W" + n])
                load(e, ml_if_b[k:k + 1, :], row(A[a2 + "b" + n]))
            load(e, ml_norm_w[:, :], A[a2 + "outnorm_w"].rearrange("(a h) d -> a (h d)", a=1).to_broadcast([P, C]))
            load(e, ml_down_w[:, :], A[a2 + "Wdown"])
            load(e, ssm_A_log[:, :, :], A[a + "A_log"].rearrange("(k p) n -> p k n", p=P))

        def more_consts(step):
            pass

        def settle(e):
            nc.vector.memset(settle_cell[:, :], 0.0)

        def ln_vector_stats(e, n, i):
            for k in range(SUP):
                last = nc.vector.bn_stats(ln_stats[:, k, :], X[:, bass.ds(i * SUP + k, 1), :])
            last.then_inc(ln_stats_done, 1)
            e.wait_ge(ln_stats_done, n + 1)
            settle(e)
            for k in range(SUP):
                last = nc.vector.bn_aggr(ln_mv[:, k, :], ln_stats[:, k, :])
            last.then_inc(ln_mv_done, 1)
            e.wait_ge(ln_mv_done, n + 1)
            nc.vector.tensor_scalar(ln_var[:, :], ln_mv[:, :, 1], LN_EPS, None, ALU.add).then_inc(ln_var_done, 1)

        def ln_pool(e, n):
            e.wait_ge(ln_var_done, n + 1)
            nc.gpsimd.tensor_tensor(ln_rstd[:, :], ln_var[:, :], minus_half[:, 0:SUP], ALU.pow).then_inc(ln_rstd_done, 1)

        def ln_vector_norm(e, n, i):
            e.wait_ge(ln_rstd_done, n + 1)
            e.wait_ge(xn_turned, n)
            for k in range(SUP):
                last = nc.vector.tensor_scalar(xn[:, k, :], X[:, bass.ds(i * SUP + k, 1), :], ln_mv[:, k, 0:1],
                                               ln_rstd[:, k:k + 1], ALU.subtract, ALU.mult)
            last.then_inc(xn_ready, 1)

        def ln_tensor(e, n, bank):
            e.wait_ge(xn_ready, n + 1)
            for k in range(SUP):
                last = nc.tensor.transpose(bank[:, k * P:(k + 1) * P], xn[:, k, :], ident[:, :])
            last.then_inc(xn_turned, 1)

        def pipeline(fori, depth, stage):
            def turn_of(tau, b0, first, last):
                for s in reversed(range(depth)):
                    if first <= tau - s <= last:
                        i = tau - s
                        stage(s, b0 * 2 + i, b0 + i // 2, i % 2)

            loops = (NSUP - depth) // 2
            for tau in range(depth):
                turn_of(tau, 0, 0, NSUP)
            with fori(0, loops) as it:
                for tau in range(depth, depth + 2):
                    turn_of(tau, it, 0, NSUP)
            for tau in range(depth + 2 * loops, NSUP + depth):
                turn_of(tau, 0, 0, NSUP - 1)

        m_logits = sem("m_logits")
        m_zeroed = sem("m_zeroed")
        m_aff = sem("m_aff")
        m_affT = sem("m_affT")
        m_top = sem("m_top")
        m_exp = sem("m_exp")
        m_w3 = sem("m_w3")
        m_w3T = sem("m_w3T")
        m_wT = sem("m_wT")
        m_xs = sem("m_xs")
        m_gate = sem("m_gate")
        m_up = sem("m_up")
        m_bc = sem("m_bc")
        m_down = sem("m_down")
        m_silu = sem("m_silu")
        m_gs = sem("m_gs")
        m_wbs = sem("m_wbs")
        m_upused = sem("m_upused")
        m_h = sem("m_h")
        m_hh = sem("m_hh")
        m_hl = sem("m_hl")
        m_yT = sem("m_yT")
        m_yt = sem("m_yt")
        m_xadd = sem("m_xadd")
        GB, UB, WB, YB, MISC = banks[0:2], banks[2:4], banks[4:6], banks[6], banks[7]
        CREDIT = 2

        class Mlp:
            def __init__(self, kind, calls):
                self.kind = kind
                self.slots = SLOTS0 if kind == 0 else SLOTS1
                self.routed = PAIRS if kind == 0 else E1
                self.rows = 3 * (E0 if kind == 0 else E1)
                self.steps = 9 if kind == 0 else 12
                self.slot0 = sum(NSUP * (SLOTS0 if c == 0 else SLOTS1) for c in calls)
                self.routed0 = sum(NSUP * (PAIRS if c == 0 else E1) for c in calls)
                self.spared = NSUP * PAIRS * sum(c == 0 for c in calls)
                self.sup0 = NSUP * len(calls)
                self.exp0 = NSUP * sum(c == 1 for c in calls)
                self.step0 = sum(NSUP * (9 if c == 0 else 12) for c in calls)
                self.stages = ([[0, 2, 4, 6, 8, 9, 12], [17, 19, 21, 23, 25, 27, 29]] if kind == 0 else
                               [[0, 1, 2, 3, 4, 5, 5], [9, 11, 12, 12, 13, 14, 14]])

            def width(self, q):
                return I0 if self.kind == 0 and q == PAIRS else P

        def mlp_order(m, fori, prep, front, back, finish, tail):
            L = m.slots
            for st in range(7):
                prep(0, 0, st)
            for f in range(AHEAD):
                front(0, 0, f, m.slot0 + f, m.routed0 + f)

            def body(it, last):
                for q in range(2 * L):
                    f = q + AHEAD
                    if q == L:
                        finish(it * 2, 0)
                    if not last or f < 2 * L:
                        ahead, fq = divmod(f, L)
                        front(ahead % 2, it * 2 + ahead, fq, it * (2 * L) + (m.slot0 + f),
                              it * (2 * m.routed) + (m.routed0 + ahead * m.routed + fq))
                    elif f == 2 * L:
                        tail()
                    back(q // L, it * 2 + q // L, q % L, it * (2 * L) + (m.slot0 + q))
                    if q == L + 1:
                        finish(it * 2, 1)
                    for half in range(1 if last else 2):
                        for st, at in enumerate(m.stages[half]):
                            if at == q:
                                prep(1 - half, it * 2 + 1 + half, st)
                finish(it * 2 + 1, 0)
                finish(it * 2 + 1, 1)

            with fori(0, NSUP // 2 - 1) as it:
                body(it, False)
            body(NSUP // 2 - 1, True)

        def nothing(*_):
            pass

        def first(j):
            return isinstance(j, int) and j == 0

        def mlp_vector(e, m, ln0):
            D = mlp

            def prep(par, j, st):
                t = j + m.sup0
                if st == 0:
                    ln_vector_stats(e, j + ln0, j)
                elif st == 1:
                    ln_vector_norm(e, j + ln0, j)
                elif st == 2:
                    e.wait_ge(xT_ready, j + (ln0 + 1))
                    if not first(j):
                        e.wait_ge(m_up, (j - 1) * m.slots + m.slot0)
                    nc.vector.tensor_copy(D["xh"][:, par, :], D["xT"][:, :]).then_inc(m_xs, 1)
                    e.wait_ge(m_xs, t * 2 + 1)
                    nc.vector.tensor_tensor(D["xl"][:, par, :], D["xT"][:, :], D["xh"][:, par, :].bitcast(FP32),
                                            ALU.subtract).then_inc(m_xs, 1)
                elif st in (4, 5):
                    count = [0 if st == 4 else 9 if m.kind == 0 else 2]

                    def step(ins):
                        count[0] += 1
                        ins.then_inc(m_top, 1)
                        e.wait_ge(m_top, j * m.steps + (m.step0 + count[0]))

                    def split(w, rest, w3, E):
                        e.wait_ge(m_w3T, t)
                        step(nc.vector.tensor_copy(w3[:, :, 0:E], w))
                        step(nc.vector.tensor_tensor(rest, w, w3[:, :, 0:E], ALU.subtract))
                        step(nc.vector.tensor_copy(w3[:, :, E:2 * E], rest))
                        nc.vector.tensor_tensor(w3[:, :, 2 * E:3 * E], rest, w3[:, :, E:2 * E], ALU.subtract).then_inc(m_w3, 1)

                    if m.kind == 0 and st == 4:
                        e.wait_ge(m_affT, t + 1)
                        aff = MISC[:, :].rearrange("p (k e) -> p k e", k=SUP)[:, :, 0:E0]
                        settle(e)
                        for k in range(SUP):
                            last = nc.vector.max(D["top"][:, k, :], aff[:, k, :])
                        step(last)
                        settle(e)
                        for k in range(SUP):
                            nc.vector.match_replace(D["rep"][:, k, :], D["top"][:, k, :], aff[:, k, :], 0.0)
                        step(nc.vector.reduce_sum(D["sum"][:, :], D["top"][:, :, :], AX.X))
                        step(nc.vector.tensor_scalar(D["rsum"][:, :], D["sum"][:, :], 1e-9, None, ALU.add))
                        step(nc.vector.reciprocal(D["sum"][:, :], D["rsum"][:, :]))
                        step(nc.vector.tensor_tensor(D["w"][:, :, :], aff, D["rep"][:, :, :], ALU.subtract))
                        step(nc.vector.tensor_tensor(D["rest"][:, :, :], D["w"][:, :, :],
                                                     D["sum"][:, :, None].to_broadcast([P, SUP, E0]), ALU.mult))
                        split(D["rest"][:, :, :], D["w"][:, :, :], D["w3"], E0)
                    elif m.kind == 1 and st == 4:
                        e.wait_ge(m_affT, t + 1)
                        lg = MISC[:, :].rearrange("p (k e) -> p k e", k=SUP)[:, :, 0:E1]
                        settle(e)
                        for k in range(SUP):
                            last = nc.vector.max(D["top"][:, k, :], lg[:, k, :])
                        step(last)
                        step(nc.vector.tensor_tensor(D["rep"][:, :, 0:E1], lg, D["top"][:, :, 0:1].to_broadcast([P, SUP, E1]),
                                                     ALU.subtract))
                    elif m.kind == 1 and st == 5:
                        s, real, rest = D["s"], D["s"][:, :, 0:E1], D["rest"][:, :, 0:E1]
                        e.wait_ge(m_exp, j + (m.exp0 + 1))
                        step(nc.vector.reduce_sum(D["sum"][:, :], D["w"][:, :, 0:E1], AX.X))
                        step(nc.vector.reciprocal(D["rsum"][:, :], D["sum"][:, :]))
                        step(nc.vector.tensor_tensor(real, D["w"][:, :, 0:E1],
                                                     D["rsum"][:, :, None].to_broadcast([P, SUP, E1]), ALU.mult))
                        settle(e)
                        for k in range(SUP):
                            last = nc.vector.max(D["top"][:, k, :], s[:, k, 0:E1])
                        step(last)
                        step(nc.vector.tensor_copy(D["top"][:, :, TOP1:8], s[:, :, E1:E1 + 8 - TOP1]))
                        settle(e)
                        for k in range(SUP):
                            last = nc.vector.match_replace(D["rep1"][:, k, :], D["top"][:, k, :], s[:, k, :], 0.0)
                        step(last)
                        step(nc.vector.tensor_tensor(D["w"][:, :, 0:E1], real, D["rep1"][:, :, 0:E1], ALU.subtract))
                        split(D["w"][:, :, 0:E1], rest, D["w3_1"], E1)

            def front(par, j, q, mm, rr):
                b, K, routed = (par * m.slots + q) % 2, m.width(q), q < m.routed
                if m.kind == 1 and routed:
                    e.wait_ge(m_wbs, rr + (CREDIT + 1 - m.spared))
                    e.wait_ge(m_gate, mm + 1)
                    e.wait_ge(m_silu, mm + (CREDIT - 1))
                    nc.vector.tensor_tensor(D["gs"][:, b, :], GB[b][:, :], D["wb"][:, b, :], ALU.mult).then_inc(m_gs, 1)
                e.wait_ge(m_silu, mm + (CREDIT + 1))
                e.wait_ge(m_up, mm + 1)
                if not routed:
                    e.wait_ge(m_hl, mm + (CREDIT - 1))
                dst = (D["t1"] if routed else D["h"])[0:K, b, :]
                if m.kind == 0:
                    ins = nc.vector.scalar_tensor_tensor(dst, UB[b][0:K, :], bu_sb[0:K, q:q + 1], D["sil"][0:K, b, :],
                                                         ALU.add, ALU.mult)
                else:
                    ins = nc.vector.tensor_tensor(dst, UB[b][:, :], D["sil"][:, b, :], ALU.mult)
                ins.then_inc(m_upused, 1)
                e.wait_ge(m_upused, mm + (CREDIT + 1))
                if routed:
                    if m.kind == 0:
                        e.wait_ge(m_bc, rr + 1)
                    e.wait_ge(m_hl, mm + (CREDIT - 1))
                    by = WB[b][:, :] if m.kind == 0 else D["wb"][:, b, :]
                    nc.vector.tensor_tensor(D["h"][:, b, :], D["t1"][:, b, :], by, ALU.mult).then_inc(m_h, 1)
                else:
                    e.sem_inc(m_h, 1)

            def finish(j, st):
                if st == 1:
                    e.wait_ge(m_yt, j + (m.sup0 + 1))
                    at = bass.ds(j * SUP, SUP)
                    nc.vector.tensor_tensor(X[:, at, :], X[:, at, :], MISC[:, :].rearrange("p (k c) -> p k c", k=SUP),
                                            ALU.add).then_inc(m_xadd, 1)

            if m.kind == 0:
                nc.vector.memset(D["w3"][:, :, 3 * E0:3 * E0 + 1], 1.0)
            else:
                nc.vector.memset(D["s"][:, :, E1:E1 + 8 - TOP1], -1.0)
            nc.vector.memset(D["aff"][:, :], 0.0).then_inc(m_zeroed, 1)
            mlp_order(m, e.Fori, prep, front, nothing, finish, nothing)

        def mlp_scalar(e, m, ln0):
            D = mlp

            def prep(par, j, st):
                t = j + m.sup0
                if st == 2:
                    e.wait_ge(xn_turned, j + (ln0 + 1))
                    e.wait_ge(m_xs, t * 2)
                    e.wait_ge(m_logits, t)
                    nc.scalar.activation(D["xT"][:, :], MISC[:, :], ACT.Copy).then_inc(xT_ready, 1)
                elif st == 3:
                    e.wait_ge(m_logits, t + 1)
                    e.wait_ge(m_affT, t)
                    if first(j):
                        e.wait_ge(m_zeroed, m.sup0 // NSUP + 1)
                    if m.kind == 0:
                        nc.scalar.activation(D["aff"][0:E0, :], MISC[0:E0, :], ACT.Sigmoid,
                                             bias=router0_b[:, :]).then_inc(m_aff, 1)
                    else:
                        nc.scalar.activation(D["aff"][0:E1, :], MISC[0:E1, :], ACT.Copy).then_inc(m_aff, 1)
                elif st == 4 and m.kind == 1:
                    e.wait_ge(m_top, j * m.steps + (m.step0 + 2))
                    nc.scalar.activation(D["w"][:, :, 0:E1], D["rep"][:, :, 0:E1], ACT.Exp).then_inc(m_exp, 1)
                elif st == 6:
                    rows = 3 * E0 + 1 if m.kind == 0 else 3 * E1
                    e.wait_ge(m_w3T, t + 1)
                    if not first(j):
                        e.wait_ge(m_up, (j - 1) * m.slots + m.slot0)
                    nc.scalar.activation(D["wT"][0:rows, par, :], MISC[:, :].bitcast(BF16)[0:rows, 0:W],
                                         ACT.Copy).then_inc(m_wT, 1)

            def round_h(b, K, mm):
                e.wait_ge(m_h, mm + (CREDIT + 1))
                e.wait_ge(m_down, mm + (CREDIT - 1))
                nc.scalar.activation(D["hh"][0:K, b, :], D["h"][0:K, b, :], ACT.Copy).then_inc(m_hh, 1)

            def front(par, j, q, mm, rr):
                b, K, routed = (par * m.slots + q) % 2, m.width(q), q < m.routed
                if m.kind == 1 and routed:
                    e.wait_ge(m_bc, rr + 1)
                    e.wait_ge(m_h, mm + (CREDIT - 1))
                    nc.scalar.activation(D["wb"][:, b, :], WB[b][:, :], ACT.Copy).then_inc(m_wbs, 1)
                e.wait_ge(m_upused, mm + (CREDIT - 1))
                if m.kind == 0:
                    e.wait_ge(m_gate, mm + 1)
                    ins = nc.scalar.activation(D["sil"][0:K, b, :], GB[b][0:K, :], ACT.Silu, bias=bg_sb[0:K, q:q + 1])
                elif routed:
                    e.wait_ge(m_gs, rr + (1 - m.spared))
                    ins = nc.scalar.activation(D["sil"][:, b, :], D["gs"][:, b, :], ACT.Silu)
                else:
                    e.wait_ge(m_gate, mm + 1)
                    ins = nc.scalar.activation(D["sil"][:, b, :], GB[b][:, :], ACT.Silu)
                ins.then_inc(m_silu, 1)
                if not (first(j) and q == 0):
                    round_h(1 - b, m.width((q - 1) % m.slots), mm - 1)

            def tail():
                round_h(1, m.width(m.slots - 1), m.slot0 + NSUP * m.slots - 1)

            def finish(j, st):
                if st == 0:
                    e.wait_ge(m_down, (j + 1) * m.slots + (m.slot0 + CREDIT))
                    e.wait_ge(m_yt, j + m.sup0)
                    nc.scalar.activation(D["yT"][:, :], YB[:, :], ACT.Copy).then_inc(m_yT, 1)

            mlp_order(m, e.Fori, prep, front, nothing, finish, tail)

        def mlp_pool(e, m, ln0):
            D = mlp

            def prep(par, j, st):
                if st == 0:
                    ln_pool(e, j + ln0)

            def front(par, j, q, mm, rr):
                b, K = (par * m.slots + q) % 2, m.width(q)
                e.wait_ge(m_hh, mm + 1)
                e.wait_ge(m_down, mm + (CREDIT - 1))
                nc.gpsimd.tensor_tensor(D["hl"][0:K, b, :], D["h"][0:K, b, :], D["hh"][0:K, b, :].bitcast(FP32),
                                        ALU.subtract).then_inc(m_hl, 1)

            mlp_order(m, e.Fori, prep, front, nothing, nothing, nothing)

        def mlp_tensor(e, m, ln0):
            D = mlp
            E = E0 if m.kind == 0 else E1

            def weights(k, q, part):
                if m.kind == 0 and q == PAIRS:
                    t = (f0s_hi, f0s_lo)[part]
                    return t[:, k, 0:I0] if k < 2 else t[0:I0, k, :]
                return ((f0_hi, f0_lo) if m.kind == 0 else (f1_hi, f1_lo))[part][:, k, q, :]

            def three(dst, k, q, hi, lo, start, stop):
                nc.tensor.matmul(dst, weights(k, q, 0), hi, start=start, stop=False)
                nc.tensor.matmul(dst, weights(k, q, 0), lo, start=False, stop=False)
                return nc.tensor.matmul(dst, weights(k, q, 1), hi, start=False, stop=stop)

            def prep(par, j, st):
                t = j + m.sup0
                if st == 1:
                    if not first(j):
                        e.wait_ge(m_wT, t)
                        e.wait_ge(m_xadd, t - 1)
                    ln_tensor(e, j + ln0, MISC)
                elif st == 3:
                    e.wait_ge(xT_ready, j + (ln0 + 1))
                    rw = router0_w if m.kind == 0 else gate1_w
                    nc.tensor.matmul(MISC[0:E, :], rw[:, :], D["xT"][:, :], start=True, stop=True).then_inc(m_logits, 1)
                elif st == 4:
                    e.wait_ge(m_aff, t + 1)
                    for k in range(SUP):
                        last = nc.tensor.transpose(MISC[:, k * P:(k + 1) * P], D["aff"][:, k * P:(k + 1) * P], ident[:, :])
                    last.then_inc(m_affT, 1)
                elif st == 6:
                    rows, w3 = (3 * E0 + 1, D["w3"]) if m.kind == 0 else (3 * E1, D["w3_1"])
                    e.wait_ge(m_w3, t + 1)
                    for k in range(SUP):
                        last = nc.tensor.transpose(MISC[:, :].bitcast(BF16)[0:rows, k * P:(k + 1) * P], w3[:, k, 0:rows],
                                                   identb[:, :])
                    last.then_inc(m_w3T, 1)

            def front(par, j, q, mm, rr):
                b, N, routed = (par * m.slots + q) % 2, m.width(q), q < m.routed
                if q == 0:
                    e.wait_ge(m_xs, (j + m.sup0) * 2 + 2)
                    e.wait_ge(m_wT, j + (m.sup0 + 1))

                def spread():
                    nc.tensor.matmul(WB[b][:, :], (sel0 if m.kind == 0 else sel1)[:, q, :], D["wT"][0:m.rows, par, :],
                                     start=True, stop=True).then_inc(m_bc, 1)

                if m.kind == 1 and routed:
                    e.wait_ge(m_wbs, rr + ((CREDIT if q == 0 else CREDIT - 1) - m.spared))
                    spread()
                if m.kind == 1:
                    e.wait_ge(m_upused, mm + (CREDIT - 1))
                e.wait_ge(m_silu, mm + (CREDIT - 1))
                three(GB[b][0:N, :], 0, q, D["xh"][:, par, :], D["xl"][:, par, :], True, True).then_inc(m_gate, 1)
                e.wait_ge(m_upused, mm + (CREDIT - 1))
                three(UB[b][0:N, :], 1, q, D["xh"][:, par, :], D["xl"][:, par, :], True, True).then_inc(m_up, 1)
                if m.kind == 0 and routed:
                    e.wait_ge(m_h, mm + (CREDIT - 1))
                    spread()

            def back(par, j, q, mm):
                b, K = (par * m.slots + q) % 2, m.width(q)
                if q == 0:
                    e.wait_ge(m_yT, j + m.sup0)
                    if m.kind == 0:
                        for r in range(3):
                            nc.tensor.matmul(YB[:, :], bd_parts[:, r, :], D["wT"][0:3 * E0 + 1, par, :], start=(r == 0),
                                             stop=False)
                e.wait_ge(m_hl, mm + (CREDIT + 1))
                three(YB[:, :], 2, q, D["hh"][0:K, b, :], D["hl"][0:K, b, :], m.kind == 1 and q == 0,
                      q == m.slots - 1).then_inc(m_down, 1)

            def finish(j, st):
                if st == 1:
                    e.wait_ge(m_yT, j + (m.sup0 + 1))
                    e.wait_ge(m_wT, min(j + 2, NSUP) + m.sup0 if isinstance(j, int) else j + (m.sup0 + 2))
                    e.wait_ge(m_xadd, j + m.sup0)
                    for k in range(SUP):
                        last = nc.tensor.transpose(MISC[:, k * P:(k + 1) * P], D["yT"][:, k * P:(k + 1) * P], ident[:, :])
                    last.then_inc(m_yt, 1)

            mlp_order(m, e.Fori, prep, front, back, finish, nothing)


        LIN_KV, LIN_TURN, LIN_OUT = banks[5], banks[6], banks[7]

        def lin_vector(e, ln0):
            D = lin

            def stage(s, i, b, par):
                if s == 0:
                    ln_vector_stats(e, i + ln0, i)
                elif s == 1:
                    ln_vector_norm(e, i + ln0, i)
                    e.wait_ge(l_qkv, i + 1)
                    for k in range(SUP):
                        last = nc.vector.tensor_tensor(D["qkv"][:, par, k, :], banks[1 + k][:, 0:3 * C], D["qkv_b"][:, :], ALU.add)
                    last.then_inc(l_biased, 1)
                else:
                    e.wait_ge(l_sq, i + 1)
                    nc.vector.reduce_sum(D["ss"][:, :, :], D["sq"][:, :, :].rearrange("p k (h d) -> p k h d", d=LIN_D),
                                         AX.X).then_inc(l_ss, 1)
                    e.wait_ge(l_ss, i * 2 + 1)
                    nc.vector.tensor_scalar(D["ss"][:, :, :], D["ss"][:, :, :], 1e-24, None, ALU.max).then_inc(l_ss, 1)
                    e.wait_ge(l_rn, i * 2 + 1)
                    nc.vector.reciprocal(D["rn"][:, :, :], D["rn"][:, :, :]).then_inc(l_rn, 1)
                    e.wait_ge(l_rn, i * 2 + 2)
                    qk = D["qkv"][:, par, :, 0:2 * C]
                    nc.vector.tensor_tensor(qk.rearrange("p k (h d) -> p k h d", d=LIN_D),
                                            qk.rearrange("p k (h d) -> p k h d", d=LIN_D),
                                            D["rn"][:, :, :, None].to_broadcast([P, SUP, 2 * LIN_H, LIN_D]), ALU.mult
                                            ).then_inc(l_unit, 1)
                    if par == 1:
                        e.wait_ge(l_kv, b + 1)
                        nc.vector.tensor_tensor(D["kvm"][:, :], LIN_KV[:, 0:C], D["blocks"][:, :], ALU.mult).then_inc(l_kvm, 1)
                        for half in range(2):
                            e.wait_ge(l_out, b * 2 + half + 1)
                            e.wait_ge(l_pb, b + 1)
                            at = bass.ds(b * SPB + half * SUP, SUP)
                            nc.vector.tensor_tensor(X[:, at, :], X[:, at, :], LIN_OUT[:, :].rearrange("p (k c) -> p k c", k=SUP),
                                                    ALU.add).then_inc(l_add, 1)
            pipeline(e.Fori, 3, stage)

        def lin_pool(e, ln0):
            D = lin

            def stage(s, i, b, par):
                if s == 0:
                    ln_pool(e, i + ln0)
                elif s == 2:
                    if par == 1:
                        e.wait_ge(xn_ready, b * 2 + (ln0 + 2))
                        at = bass.ds(b * SPB, SPB)
                        nc.gpsimd.tensor_tensor(X[:, at, :], X[:, at, :], D["proj_b"][:, None, :].to_broadcast([P, SPB, C]),
                                                ALU.add).then_inc(l_pb, 1)
            nc.gpsimd.memset(D["blocks"][:, :], 1.0).then_inc(l_const, 1)
            e.wait_ge(l_const, 1)
            v = D["blocks"][:, :].rearrange("p (h d) -> p h d", d=LIN_D)
            nc.gpsimd.affine_select(out=v, in_=v, compare_op=ALU.is_ge, fill=0.0, base=0,
                                    pattern=[[-LIN_D, LIN_H], [0, LIN_D]], channel_multiplier=1).then_inc(l_const, 1)
            e.wait_ge(l_const, 2)
            nc.gpsimd.affine_select(out=v, in_=v, compare_op=ALU.is_ge, fill=0.0, base=LIN_D - 1,
                                    pattern=[[LIN_D, LIN_H], [0, LIN_D]], channel_multiplier=-1).then_inc(l_const, 1)
            pipeline(e.Fori, 3, stage)

        def lin_scalar(e, ln0):
            D = lin

            def stage(s, i, b, par):
                if s == 1:
                    e.wait_ge(xn_turned, i + (ln0 + 1))
                    e.wait_ge(l_qkv, i)
                    nc.scalar.activation(D["xT"][:, :], banks[0][:, :], ACT.Copy).then_inc(xT_ready, 1)
                elif s == 2:
                    e.wait_ge(l_biased, i + 1)
                    e.wait_ge(l_ss, i * 2)
                    nc.scalar.activation(D["sq"][:, :, :], D["qkv"][:, par, :, 0:2 * C], ACT.Square).then_inc(l_sq, 1)
                    e.wait_ge(l_ss, i * 2 + 2)
                    nc.scalar.activation(D["rn"][:, :, :], D["ss"][:, :, :], ACT.Sqrt).then_inc(l_rn, 1)
                    e.wait_ge(l_qt, i + 1)
                    e.wait_ge(l_out, b * 2)
                    nc.scalar.activation(D["qT"][:, par, :], LIN_TURN[:, :], ACT.Copy).then_inc(l_qT, 1)
                    if par == 1:
                        e.wait_ge(l_m, b + 1)
                        nc.scalar.activation(D["m"][:, :], LIN_OUT[:, 0:C], ACT.Copy).then_inc(l_mb, 1)
            nc.scalar.preload_act_table(ACT.Sqrt)
            pipeline(e.Fori, 3, stage)

        def lin_tensor(e, ln0):
            D = lin

            def stage(s, i, b, par):
                if s == 1:
                    e.wait_ge(xT_ready, i + ln0)
                    ln_tensor(e, i + ln0, banks[0])
                    e.wait_ge(xT_ready, i + (ln0 + 1))
                    e.wait_ge(l_biased, i)
                    for k in range(SUP):
                        last = nc.tensor.matmul(banks[1 + k][:, 0:3 * C], D["xT"][:, k * P:(k + 1) * P], D["qkv_w"][:, :],
                                                start=True, stop=True)
                    last.then_inc(l_qkv, 1)
                elif s == 2:
                    e.wait_ge(l_unit, i + 1)
                    e.wait_ge(l_qT, i)
                    for k in range(SUP):
                        last = nc.tensor.transpose(LIN_TURN[:, k * P:(k + 1) * P], D["qkv"][:, par, k, 0:C], ident[:, :])
                    last.then_inc(l_qt, 1)
                    if par == 0:
                        e.wait_ge(l_kvm, b)
                    for k in range(SUP):
                        last = nc.tensor.matmul(LIN_KV[:, 0:C], D["qkv"][:, par, k, 2 * C:3 * C], D["qkv"][:, par, k, C:2 * C],
                                                start=(par == 0 and k == 0), stop=(par == 1 and k == SUP - 1))
                    if par == 1:
                        last.then_inc(l_kv, 1)
                        e.wait_ge(l_kvm, b + 1)
                        e.wait_ge(l_add, b * 2)
                        nc.tensor.matmul(LIN_OUT[:, 0:C], D["kvm"][:, :], D["proj_w"][:, :], start=True, stop=True).then_inc(l_m, 1)
                        e.wait_ge(l_mb, b + 1)
                        e.wait_ge(l_qT, i + 1)
                        for half in range(2):
                            e.wait_ge(l_add, b * 2 + half)
                            for k in range(SUP):
                                last = nc.tensor.matmul(LIN_OUT[:, k * C:(k + 1) * C], D["qT"][:, half, k * P:(k + 1) * P],
                                                        D["m"][:, :], start=True, stop=True)
                            last.then_inc(l_out, 1)
            pipeline(e.Fori, 3, stage)

        POWER_BANKS = [banks[7], banks[0], banks[1], banks[2]]
        POWERS_L = [1, 2, 4, 8, 16, 32, 64, 128, 256, 512]
        POWERS_R = [1, 2, 3, 4, 5, 6, 7, 8, 16, 32, 64, 128, 256]
        LI = {k: n for n, k in enumerate(POWERS_L)}
        RI = {k: n for n, k in enumerate(POWERS_R)}
        RECIPES = [("L", 2, 1, 1), ("R", 2, 1, 1), ("R", 3, 1, 2), ("L", 4, 2, 2), ("R", 4, 2, 2), ("R", 5, 1, 4), ("R", 6, 2, 4),
                   ("R", 7, 4, 3), ("L", 8, 4, 4), ("R", 8, 4, 4)]
        for k in (16, 32, 64, 128, 256):
            RECIPES += [("L", k, k // 2, k // 2), ("R", k, k // 2, k // 2)]
        RECIPES.append(("L", 512, 256, 256))
        RECIPES += [("G", k, k, 0) for k in range(1, SPB)]
        HALVES = 21

        def spectral_vector(e):
            D = rnn
            nc.vector.memset(D["u"][:, :], P ** -0.5).then_inc(p_vec, 1)
            nc.vector.memset(D["ones"][:, :], 1.0).then_inc(p_vec, 1)

            def half(n, dst):
                e.wait_ge(p_raw, n + 1)
                nc.vector.tensor_copy(D["raw"][:, :], banks[0][:, 0:3]).then_inc(p_vec, 1)
                e.wait_ge(p_norm, n + 1)
                for step, ins in enumerate((
                        lambda: nc.vector.tensor_scalar(D["norm1"][:, :], D["norm"][:, :], 1e-12, None, ALU.add),
                        lambda: nc.vector.reciprocal(D["inv"][:, :], D["norm1"][:, :]),
                        lambda: nc.vector.tensor_tensor(dst, D["raw"][:, :], D["inv"][:, :], ALU.mult))):
                    if step:
                        e.wait_ge(p_vec, n * 4 + (3 + step))
                    ins().then_inc(p_vec, 1)

            with e.Fori(0, HALVES // 2) as it:
                half(it * 2, D["v"][:, :])
                half(it * 2 + 1, D["u"][:, :])
            half(HALVES - 1, D["v"][:, :])
            e.wait_ge(p_raw, HALVES + 1)
            nc.vector.tensor_tensor(D["sq"][:, :], banks[0][:, 0:3], D["u"][:, :], ALU.mult).then_inc(p_sq, 1)
            e.wait_ge(p_sum, HALVES + 1)
            nc.vector.reciprocal(D["isig"][:, :], banks[1][:, 0:3]).then_inc(p_sigma, 1)
            e.wait_ge(p_sigma, 1)
            nc.vector.tensor_scalar(D["R"][:, 0, :], D["w"][:, 0, :], D["isig"][:, 0:1], None, ALU.mult)
            nc.vector.tensor_scalar(D["L"][:, 0, :], D["wT"][:, 0, :], D["isig"][:, 0:1], None, ALU.mult)
            nc.vector.tensor_scalar(D["CT"][:, :], D["wT"][:, 2, :], D["isig"][:, 2:3], None, ALU.mult).then_inc(p_scaled, 1)

        def spectral_scalar(e):
            D = rnn
            e.wait_ge(p_turned, 1)
            nc.scalar.activation(D["wT"][:, :, :], banks[2][:, 0:3 * P].rearrange("p (m c) -> p m c", m=3), ACT.Copy).then_inc(p_wT, 1)

            def half(n):
                e.wait_ge(p_vec, n * 4 + 3)
                nc.scalar.activation(D["sq"][:, :], D["raw"][:, :], ACT.Square).then_inc(p_sq, 1)
                e.wait_ge(p_sum, n + 1)
                nc.scalar.activation(D["norm"][:, :], banks[1][:, 0:3], ACT.Sqrt).then_inc(p_norm, 1)

            nc.scalar.preload_act_table(ACT.Sqrt)
            with e.Fori(0, HALVES) as n:
                half(n)

        def spectral_tensor(e):
            D = rnn
            for k in range(3):
                last = nc.tensor.transpose(banks[2][:, k * P:(k + 1) * P], D["w"][:, k, :], ident[:, :])
            last.then_inc(p_turned, 1)
            e.wait_ge(p_wT, 1)

            def half(n, w, x):
                e.wait_ge(p_vec, n * 4 + 2)
                for k in range(3):
                    last = nc.tensor.matmul(banks[0][:, k:k + 1], D[w][:, k, :], D[x][:, k:k + 1], start=True, stop=True)
                last.then_inc(p_raw, 1)
                e.wait_ge(p_sq, n + 1)
                nc.tensor.matmul(banks[1][:, 0:3], D["ones"][:, :], D["sq"][:, :], start=True, stop=True).then_inc(p_sum, 1)

            with e.Fori(0, HALVES // 2) as it:
                half(it * 2, "w", "u")
                half(it * 2 + 1, "wT", "v")
            half(HALVES - 1, "w", "u")
            half(HALVES, "wT", "v")

        def rnn_vector(e, ln0):
            D = rnn
            spectral_vector(e)

            def stage(s, i, b, par):
                if s == 0:
                    ln_vector_stats(e, i + ln0, i)
                elif s == 1:
                    ln_vector_norm(e, i + ln0, i)
            pipeline(e.Fori, 3, stage)
            e.wait_ge(r_u, NSUP)
            U = D["U"]
            nc.vector.memset(D["carry"][:, :, 0:1], 0.0)
            for s in range(1, SPB):
                e.wait_ge(r_step, s)
                nc.vector.tensor_tensor(U[:, :, s, :], U[:, :, s, :], banks[3][:, :].rearrange("p (b j) -> p b j", b=NB),
                                        ALU.add).then_inc(r_stepped, 1)
            e.wait_ge(r_stepped, SPB - 1)
            nc.vector.tensor_copy(D["carry"][:, :, 1:P + 1], U[:, :, SPB - 1, :]).then_inc(r_carried, 1)
            for n in range(7):
                d = 1 << n
                e.wait_ge(r_jump, n + 1)
                if n:
                    e.wait_ge(r_carried, n + 1)
                nc.vector.tensor_tensor(D["carry"][:, :, 1 + d:P + 1], D["carry"][:, :, 1 + d:P + 1],
                                        banks[3 + n % 2][:, 0:NB * (P - d)].rearrange("p (b j) -> p b j", b=NB),
                                        ALU.add).then_inc(r_carried, 1)
            for i in range(NSUP):
                e.wait_ge(r_out, i + 1)
                at = slice(i * SUP, (i + 1) * SUP)
                nc.vector.tensor_tensor(X[:, at, :], X[:, at, :], banks[5 + i % 2][:, :].rearrange("p (k c) -> p k c", k=SUP),
                                        ALU.add).then_inc(r_add, 1)

        def rnn_pool(e, ln0):
            def stage(s, i, b, par):
                if s == 0:
                    ln_pool(e, i + ln0)
            pipeline(e.Fori, 3, stage)

        def rnn_scalar(e, ln0):
            D = rnn
            spectral_scalar(e)
            e.wait_ge(p_scaled, 1)

            def stage(s, i, b, par):
                if s == 1:
                    e.wait_ge(xn_turned, i + (ln0 + 1))
                    e.wait_ge(r_bx, i - 1 if not isinstance(i, int) else max(i - 1, 0))
                    nc.scalar.activation(D["xT"][:, par, :], banks[0][:, :], ACT.Copy).then_inc(xT_ready, 1)
                elif s == 2:
                    e.wait_ge(r_bx, i + 1)
                    nc.scalar.activation(D["U"][:, :, :, :].rearrange("p b s j -> p (b s j)")[:, bass.ds(i * W, W)], banks[1 + par][:, :], ACT.Copy,
                                         scale=D["isig"][:, 1:2]).then_inc(r_u, 1)
            pipeline(e.Fori, 3, stage)
            for n, (kind, k, _, _) in enumerate(RECIPES):
                e.wait_ge(r_pow, n + 1)
                dst = {"L": lambda: D["L"][:, LI[k], :], "R": lambda: D["R"][:, RI[k], :], "G": lambda: D["G"][:, k, :]}[kind]()
                nc.scalar.activation(dst, POWER_BANKS[n % 4][:, 0:P], ACT.Copy).then_inc(r_power, 1)

        def rnn_tensor(e, ln0):
            D = rnn
            spectral_tensor(e)
            e.wait_ge(p_scaled, 1)

            def stage(s, i, b, par):
                if s == 1:
                    e.wait_ge(xT_ready, i + ln0)
                    ln_tensor(e, i + ln0, banks[0])
                elif s == 2:
                    e.wait_ge(xT_ready, i + (ln0 + 1))
                    e.wait_ge(r_u, i - 1 if not isinstance(i, int) else max(i - 1, 0))
                    nc.tensor.matmul(banks[1 + par][:, :], D["wT"][:, 1, :], D["xT"][:, par, :], start=True, stop=True).then_inc(r_bx, 1)
            pipeline(e.Fori, 3, stage)
            done = {("L", 1): 0, ("R", 1): 0, ("G", 0): 0}
            n = [0]

            def powers(count):
                for _ in range(count):
                    if n[0] == len(RECIPES):
                        return
                    kind, k, a, b = RECIPES[n[0]]
                    if kind == "G":
                        lhsT, rhs, need = D["R"][:, RI[k], :], D["CT"][:, :], done[("R", k)]
                    else:
                        one, two = (("R", "L") if kind == "L" else ("L", "R"))
                        index = {"L": LI, "R": RI}
                        lhsT, rhs = D[one][:, index[one][a], :], D[two][:, index[two][b], :]
                        need = max(done[(one, a)], done[(two, b)])
                    e.wait_ge(r_power, max(need, n[0] - 3))
                    nc.tensor.matmul(POWER_BANKS[n[0] % 4][:, 0:P], lhsT, rhs, start=True, stop=True).then_inc(r_pow, 1)
                    n[0] += 1
                    done[(kind, k)] = n[0]

            U, carry = D["U"], D["carry"]
            e.wait_ge(r_u, NSUP)
            for s in range(1, SPB):
                e.wait_ge(r_stepped, s - 1)
                nc.tensor.matmul(banks[3][:, :].rearrange("p (b j) -> p b j", b=NB), D["L"][:, 0, :], U[:, :, s - 1, :], start=True, stop=True).then_inc(r_step, 1)
                powers(4)
            for m_ in range(7):
                d = 1 << m_
                while ("L", SPB * d) not in done:
                    powers(1)
                e.wait_ge(r_power, done[("L", SPB * d)])
                e.wait_ge(r_carried, m_ + 1)
                nc.tensor.matmul(banks[3 + m_ % 2][:, 0:NB * (P - d)].rearrange("p (b j) -> p b j", b=NB), D["L"][:, LI[SPB * d], :],
                                 carry[:, :, 1:P + 1 - d], start=True, stop=True).then_inc(r_jump, 1)
                powers(2)
            powers(len(RECIPES))
            e.wait_ge(r_power, len(RECIPES))
            e.wait_ge(r_carried, 8)
            for i in range(NSUP):
                b, half = divmod(i, 2)
                if i >= 2:
                    e.wait_ge(r_add, i - 1)
                for k in range(SUP):
                    s = half * SUP + k
                    dst = banks[5 + i % 2][:, k * P:(k + 1) * P]
                    if s == SPB - 1:
                        last = nc.tensor.matmul(dst, carry[:, b, 1:P + 1], D["CT"][:, :], start=True, stop=True)
                    else:
                        nc.tensor.matmul(dst, U[:, b, s, :], D["CT"][:, :], start=True, stop=False)
                        last = nc.tensor.matmul(dst, carry[:, b, 0:P], D["G"][:, s + 1, :], start=False, stop=True)
                last.then_inc(r_out, 1)


        YBANK, BBANK, CBANK, PROD = banks[0:2], banks[2:4], banks[4:6], banks[6:8]
        UNITS, RING = 2 * SSM_N, 4
        HALF1 = [("h0", 1), ("h1", 2), ("g0", 3), ("g1", 4), ("c0", 5), ("c1", 7), ("ts", 9), ("bc", 10), ("split", 11),
                 ("dt0", 11), ("dt1", 12), ("soft", 13), ("delta", 14)]
        HALF0 = [("stats0", 0), ("rms0", 1), ("norm0", 2), ("stats1", 2), ("rms1", 3), ("norm1", 4), ("h0", 5), ("h1", 6),
                 ("g0", 7), ("g1", 7), ("c0", 8), ("c1", 9), ("ts", 10), ("bc", 11), ("split", 12), ("dt0", 12),
                 ("dt1", 13), ("soft", 13), ("delta", 14)]
        PRODUCTS = {"norm0": -2, "norm1": -1, "h0": 0, "h1": 1, "g0": 2, "g1": 3, "c0": 4, "c1": 5, "ts": 6, "bc": 7,
                    "dt0": 8, "dt1": 9}

        def ssm_order(fori, prep, front, back, finish, result):
            def prepare(half, b, at, what):
                prep(what, b, half, at + PRODUCTS.get(what, 0))

            for what, _ in HALF0:
                prepare(0, 0, 2, what)
            front(0, 0, 0)

            def body(b, last):
                for q in range(2 * SSM_N):
                    if not (last and q == 2 * SSM_N - 1):
                        nxt = q + 1
                        front(b + nxt // (2 * SSM_N), nxt // SSM_N % 2, nxt % SSM_N)
                    back(b, q // SSM_N, q % SSM_N)
                    for what, at in HALF1:
                        if at == q:
                            prepare(1, b, b * 22 + 12, what)
                    if not last:
                        for what, at in HALF0:
                            if at + SSM_N == q:
                                prepare(0, b + 1, b * 22 + 24, what)
                    if q == SSM_N - 1:
                        finish(b, 0)
                finish(b, 1)
                result(b, last)

            with fori(0, NB - 1) as b:
                body(b, False)
            body(NB - 1, True)

        def started(b, half):
            return isinstance(b, int) and b == 0 and half == 0

        def ssm_vector(e, ln0):
            D = ssm

            def prep(what, b, half, at):
                c = b * 2 + half
                if what[:-1] == "stats":
                    i = b * 2 + int(what[-1])
                    ln_vector_stats(e, i + ln0, i)
                elif what[:-1] == "rms":
                    i = b * 2 + int(what[-1])
                    e.wait_ge(ln_rstd_done, i + (ln0 + 1))
                    nc.vector.tensor_tensor(D["ms"][:, :], ln_rstd[:, :], ln_rstd[:, :], ALU.mult).then_inc(s_rms, 1)
                    e.wait_ge(s_rms, i * 4 + 1)
                    nc.vector.tensor_tensor(D["ms"][:, :], D["ms"][:, :], ln_mv[:, :, 1], ALU.mult).then_inc(s_rms, 1)
                    e.wait_ge(s_rms, i * 4 + 2)
                    nc.vector.tensor_scalar(D["ms"][:, :], D["ms"][:, :], 1e-6, None, ALU.add).then_inc(s_rms, 1)
                elif what[:-1] == "norm":
                    i = b * 2 + int(what[-1])
                    e.wait_ge(s_rpow, i + 1)
                    nc.vector.tensor_tensor(ln_rstd[:, :], ln_rstd[:, :], D["ms2"][:, :], ALU.mult).then_inc(s_rms, 1)
                    e.wait_ge(s_rms, i * 4 + 4)
                    ln_vector_norm(e, i + ln0, i)
                elif what == "split":
                    if not started(b, half):
                        e.wait_ge(s_bc, (c - 1) * SSM_N)
                    e.wait_ge(s_evac, evac_number(b, half, 7) + 1)
                    bc, v0, r = D["bc"][:, half, :], D["v0"], D["r"]
                    steps = (lambda: nc.vector.tensor_copy(bc[0:96], v0[0:96, :]),
                             lambda: nc.vector.tensor_tensor(r[:, :], v0[:, :], bc[0:96], ALU.subtract),
                             lambda: [nc.vector.tensor_copy(bc[32 * j:32 * (j + 1)], r[32 * j:32 * (j + 1), :]) for j in (1, 2)][-1],
                             lambda: nc.vector.tensor_tensor(bc[64:96], r[64:96, :], bc[64:96], ALU.subtract))
                    for k, ins in enumerate(steps):
                        if k:
                            e.wait_ge(s_split, c * 4 + k)
                        ins().then_inc(s_split, 1)
                elif what == "delta":
                    if not started(b, half):
                        e.wait_ge(s_da, (c - 1) * UNITS + RING)
                        e.wait_ge(s_dbu, (c - 1) * UNITS + RING)
                    delta = D["delta"][:, half, :, :]
                    e.wait_ge(s_soft, c * 8 + 6)
                    nc.vector.scalar_tensor_tensor(D["ez"][:, :, :], D["uz"][:, :, :], 1.0, D["ez"][:, :, :],
                                                   ALU.subtract, ALU.subtract).then_inc(s_delta, 1)
                    e.wait_ge(s_soft, c * 8 + 8)
                    nc.vector.scalar_tensor_tensor(delta, D["zb"][:, :, :], 0.0, D["lz"][:, :, :], ALU.max,
                                                   ALU.add).then_inc(s_delta, 1)
                    e.wait_ge(s_delta, c * 3 + 2)
                    nc.vector.tensor_tensor(delta, delta, D["ez"][:, :, :], ALU.subtract).then_inc(s_delta, 1)
                    e.wait_ge(s_delta, c * 3 + 3)
                    nc.vector.tensor_tensor(D["du"][:, half, :, :], D["delta"][:, half, :, :], D["cv"][:, half, :, :],
                                            ALU.mult).then_inc(s_du, 1)

            def back(b, half, n):
                c = b * 2 + half
                for blk in range(2):
                    u = c * UNITS + (2 * n + blk)
                    ring = (2 * n + blk) % RING
                    e.wait_ge(s_da, u + (RING + 1))
                    e.wait_ge(s_dbu, u + (RING + 1))
                    last = D["last"][:, 2 * n + blk:2 * n + blk + 1]
                    nc.vector.tensor_tensor_scan(D["st"][:, ring, :], D["da"][:, ring, :], D["dbu"][:, ring, :],
                                                 last if half else 0.0, ALU.mult, ALU.add).then_inc(s_scan, 1)
                for blk in range(2):
                    u = c * UNITS + (2 * n + blk)
                    ring = (2 * n + blk) % RING
                    e.wait_ge(s_scan, u + (RING + 1))
                    if half == 0:
                        nc.vector.tensor_copy(D["last"][:, 2 * n + blk:2 * n + blk + 1], D["st"][:, ring, W - 1:W])
                    if blk == 0:
                        e.wait_ge(s_bc, c * SSM_N + (n + 1))
                    e.wait_ge(s_acc, u + 1)
                    nc.vector.tensor_tensor(D["sc"][:, ring, :], D["st"][:, ring, :], CBANK[n % 2][:, :], ALU.mult).then_inc(s_mult, 1)

            def finish(b, half):
                c = b * 2 + half
                e.wait_ge(s_acc, (c + 1) * UNITS + RING)
                for blk in range(2):
                    nc.vector.scalar_tensor_tensor(D["y2"][:, blk, :], D["cv"][:, half, blk, :], ssm_D[:, blk:blk + 1],
                                                   YBANK[blk][:, :], ALU.mult, ALU.add).then_inc(s_y, 1)
                e.wait_ge(s_y, c * 2 + 2)
                nc.vector.tensor_tensor(D["yb"][:, :, half * W:(half + 1) * W], D["y2"][:, :, :], D["gs"][:, half, :, :],
                                        ALU.mult).then_inc(s_y3, 1)

            def result(b, last):
                e.wait_ge(s_pb, b + 1)
                for k in range(2):
                    e.wait_ge(s_out, b * 2 + k + 1)
                    at = bass.ds(b * SPB + k * SUP, SUP)
                    nc.vector.tensor_tensor(X[:, at, :], X[:, at, :], PROD[k][:, :].rearrange("p (k c) -> p k c", k=SUP),
                                            ALU.add).then_inc(s_oadd, 1)

            nc.vector.memset(D["hp"][:, 0, :, 0:SSM_K - 1], 0.0).then_inc(s_const, 1)
            e.wait_ge(s_const, 6)
            nc.vector.tensor_scalar(D["negA"][:, :, :], D["negA"][:, :, :], -1.0, None, ALU.mult).then_inc(s_const, 1)
            e.wait_ge(s_const, 7)
            ssm_order(e.Fori, prep, nothing, back, finish, result)

        def evac_number(b, half, k):
            return 2 + k if started(b, half) else (b * 22 + (12 + k) if half else (b - 1) * 22 + (24 + k))

        def ssm_pool(e, ln0):
            D = ssm

            def prep(what, b, half, at):
                i = b * 2 + int(what[-1]) if what[-1] in "01" else None
                if what[:-1] == "stats":
                    ln_pool(e, i + ln0)
                elif what[:-1] == "rms":
                    e.wait_ge(s_rms, i * 4 + 3)
                    nc.gpsimd.tensor_tensor(D["ms2"][:, :], D["ms"][:, :], minus_half[:, 0:SUP], ALU.pow).then_inc(s_rpow, 1)
                elif what == "h0" and half == 1:
                    e.wait_ge(xn_ready, b * 2 + (ln0 + 2))
                    at = bass.ds(b * SPB, SPB)
                    nc.gpsimd.tensor_tensor(X[:, at, :], X[:, at, :], ssm_out_b[:, None, :].to_broadcast([P, SPB, C]),
                                            ALU.add).then_inc(s_pb, 1)

            def front(b, half, n):
                c = b * 2 + half
                if n == 0:
                    e.wait_ge(s_du, c + 1)
                e.wait_ge(s_bs, c * SSM_N + (n + 1))
                for blk in range(2):
                    u = c * UNITS + (2 * n + blk)
                    e.wait_ge(s_scan, u + 1)
                    nc.gpsimd.tensor_tensor(D["dbu"][:, (2 * n + blk) % RING, :], D["du"][:, half, blk, :], D["bs"][:, n % 2, :],
                                            ALU.mult).then_inc(s_dbu, 1)

            nc.gpsimd.memset(D["sel"][:, :, :], 0.0)
            nc.gpsimd.memset(D["diag"][:, :, :, :], 0.0).then_inc(s_diag, 1)
            e.wait_ge(s_diag, 1)
            for j in range(3):
                nc.gpsimd.affine_select(out=D["sel"][:, :, :], in_=D["sel"][:, :, :], compare_op=ALU.not_equal, fill=1.0,
                                        base=-32 * j, pattern=[[-1, 32], [0, P]], channel_multiplier=1).then_inc(s_diag, 1)
                e.wait_ge(s_diag, j + 2)
            for blk in range(2):
                for k in range(SSM_K):
                    last = nc.gpsimd.tensor_scalar(D["diag"][:, blk, k, :], ident[:, :], ssm_conv_w[:, blk, k:k + 1], None, ALU.mult)
            last.then_inc(s_const, 4)
            ssm_order(e.Fori, prep, front, nothing, nothing, nothing)

        def ssm_scalar(e, ln0):
            D = ssm
            ready = lambda at: e.wait_ge(s_prod, at + 1)

            def prep(what, b, half, at):
                c = b * 2 + half
                if what[:-1] == "norm":
                    u = int(what[-1])
                    i = b * 2 + u
                    e.wait_ge(xn_turned, i + (ln0 + 1))
                    nc.scalar.activation(D["xT"][:, :].rearrange("p (j s) -> p s j", s=SPB)[:, u * SUP:(u + 1) * SUP, :],
                                         PROD[u][:, :].rearrange("p (s j) -> p s j", s=SUP), ACT.Copy,
                                         scale=ssm_norm[:, :]).then_inc(s_evac, 1)
                elif what[0] == "h":
                    k = int(what[1])
                    if k == 0 and half == 1:
                        e.wait_ge(s_evac, at - 9)
                        nc.scalar.activation(D["hp"][:, 1, :, 0:SSM_K - 1], D["hp"][:, 0, :, W:W + SSM_K - 1], ACT.Copy)
                    ready(at)
                    nc.scalar.activation(D["hp"][:, half, k, SSM_K - 1:], PROD[k][:, :], ACT.Identity,
                                         bias=ssm_in_b[:, k:k + 1]).then_inc(s_evac, 1)
                elif what[0] == "g":
                    k = int(what[1])
                    ready(at)
                    if not started(b, half):
                        e.wait_ge(s_y3, c - 1)
                    nc.scalar.activation(D["gs"][:, half, k, :], PROD[k][:, :], ACT.Silu, bias=ssm_in_b[:, 2 + k:3 + k]).then_inc(s_evac, 1)
                elif what[0] == "c":
                    k = int(what[1])
                    ready(at)
                    nc.scalar.activation(D["cv"][:, half, k, :], PROD[k][:, :], ACT.Silu, bias=ssm_conv_b[:, k:k + 1]).then_inc(s_evac, 1)
                elif what == "ts":
                    ready(at)
                    nc.scalar.activation(D["ts"][:, :], PROD[0][0:SSM_R, :], ACT.Copy).then_inc(s_evac, 1)
                elif what == "bc":
                    ready(at)
                    e.wait_ge(s_split, c * 4)
                    nc.scalar.activation(D["v0"][:, :], PROD[1][0:96, :], ACT.Copy).then_inc(s_evac, 1)
                elif what[:2] == "dt":
                    k = int(what[2])
                    ready(at)
                    e.wait_ge(s_delta, c * 3)
                    nc.scalar.activation(D["zb"][:, k, :], PROD[k][:, :], ACT.Identity, bias=ssm_dt_b[:, k:k + 1]).then_inc(s_evac, 1)
                elif what == "soft":
                    e.wait_ge(s_evac, evac_number(b, half, 9) + 1)
                    for step, (dst, src, fn, scale, bias) in enumerate((
                            ("ez", "zb", ACT.Abs, 1.0, 0.0), ("ez", "ez", ACT.Exp, -1.0, 0.0),
                            ("uz", "ez", ACT.Identity, 1.0, 1.0), ("lz", "uz", ACT.Ln, 1.0, 0.0))):
                        for k in range(2):
                            if step:
                                e.wait_ge(s_soft, c * 8 + (2 * step - 1 + k))
                            nc.scalar.activation(D[dst][:, k, :], D[src][:, k, :], fn, scale=scale, bias=bias).then_inc(s_soft, 1)

            def front(b, half, n):
                c = b * 2 + half
                e.wait_ge(s_bb, c * SSM_N + (n + 1))
                e.wait_ge(s_dbu, c * UNITS + (2 * n + RING - 2))
                nc.scalar.activation(D["bs"][:, n % 2, :], BBANK[n % 2][:, :], ACT.Copy).then_inc(s_bs, 1)
                if n == 0:
                    e.wait_ge(s_delta, c * 3 + 3)
                for blk in range(2):
                    u = c * UNITS + (2 * n + blk)
                    e.wait_ge(s_scan, u + 1)
                    nc.scalar.activation(D["da"][:, (2 * n + blk) % RING, :], D["delta"][:, half, blk, :], ACT.Exp,
                                         scale=D["negA"][:, blk, n:n + 1]).then_inc(s_da, 1)

            nc.scalar.activation(D["negA"][:, :, :], ssm_A_log[:, :, :], ACT.Exp).then_inc(s_const, 1)
            e.wait_ge(s_const, 7)
            ssm_order(e.Fori, prep, front, nothing, nothing, nothing)
            e.sem_inc(xT_ready, NSUP)

        def ssm_tensor(e, ln0):
            D = ssm

            def free(b, half, k):
                if k >= 2:
                    e.wait_ge(s_evac, evac_number(b, half, k) - 1)
                elif half == 0:
                    e.wait_ge(s_evac, evac_number(b, half, k) - 1)
                else:
                    e.wait_ge(s_evac, evac_number(b, half, k) - 1)
                    e.wait_ge(s_oadd, b * 2)

            def prep(what, b, half, at):
                c = b * 2 + half
                k = PRODUCTS.get(what)
                if k is None:
                    return
                if k < 0:
                    u = int(what[-1])
                    if not started(b, half):
                        e.wait_ge(s_evac, (b - 1) * 22 + (22 + u) - 1)
                    ln_tensor_to(e, b * 2 + u + ln0, PROD[u])
                    return
                free(b, half, k)
                xT = D["xT"][:, half * W:(half + 1) * W]
                if what[0] in "hg":
                    blk = int(what[1])
                    at_w = blk + (2 if what[0] == "g" else 0)
                    if what == "h0":
                        e.wait_ge(s_evac, evac_number(b, half, 0))
                    last = nc.tensor.matmul(PROD[blk][:, :], ssm_in_w[:, at_w * P:(at_w + 1) * P], xT, start=True, stop=True)
                elif what[0] == "c":
                    blk = int(what[1])
                    e.wait_ge(s_evac, evac_number(b, half, 1) + 1)
                    for tap in range(SSM_K):
                        last = nc.tensor.matmul(PROD[blk][:, :], D["diag"][:, blk, tap, :], D["hp"][:, half, blk, tap:tap + W],
                                                start=(tap == 0), stop=(tap == SSM_K - 1))
                elif what == "ts":
                    e.wait_ge(s_evac, evac_number(b, half, 5) + 1)
                    for blk in range(2):
                        last = nc.tensor.matmul(PROD[0][0:SSM_R, :], ssm_xproj[:, blk, 0:SSM_R], D["cv"][:, half, blk, :],
                                                start=(blk == 0), stop=(blk == 1))
                elif what == "bc":
                    for blk in range(2):
                        last = nc.tensor.matmul(PROD[1][0:96, :], ssm_xbc[:, blk, :], D["cv"][:, half, blk, :],
                                                start=(blk == 0), stop=(blk == 1))
                else:
                    blk = int(what[2])
                    e.wait_ge(s_evac, evac_number(b, half, 6) + 1)
                    last = nc.tensor.matmul(PROD[blk][:, :], ssm_dt_w[:, blk * P:(blk + 1) * P], D["ts"][:, :], start=True, stop=True)
                last.then_inc(s_prod, 1)

            def ln_tensor_to(e, n, bank):
                e.wait_ge(xn_ready, n + 1)
                for k in range(SUP):
                    last = nc.tensor.transpose(bank[:, k * P:(k + 1) * P], xn[:, k, :], ident[:, :])
                last.then_inc(xn_turned, 1)
                e.sem_inc(s_prod, 1)

            def front(b, half, n):
                c = b * 2 + half
                if n == 0:
                    e.wait_ge(s_split, c * 4 + 4)
                e.wait_ge(s_bs, c * SSM_N + n - 1 if not (started(b, half) and n < 1) else 0)
                nc.tensor.matmul(BBANK[n % 2][:, :], D["sel"][:, n, :], D["bc"][:, half, :], start=True, stop=True).then_inc(s_bb, 1)
                e.wait_ge(s_mult, c * UNITS + 2 * n - 2 if not (started(b, half) and n < 1) else 0)
                nc.tensor.matmul(CBANK[n % 2][:, :], D["sel"][:, SSM_N + n, :], D["bc"][:, half, :], start=True, stop=True).then_inc(s_bc, 1)

            def back(b, half, n):
                c = b * 2 + half
                if n == 0:
                    e.wait_ge(s_y, c * 2)
                for blk in range(2):
                    u = c * UNITS + (2 * n + blk)
                    e.wait_ge(s_mult, u + 1)
                    nc.tensor.matmul(YBANK[blk][:, :], ident[:, :], D["sc"][:, (2 * n + blk) % RING, :], start=(n == 0),
                                     stop=(n == SSM_N - 1)).then_inc(s_acc, 1)

            def result(b, last):
                e.wait_ge(s_y3, b * 2 + 2)
                e.wait_ge(s_evac, b * 22 + (22 if last else 34))
                for k in range(2):
                    for t in range(SUP):
                        s = k * SUP + t
                        for blk in range(2):
                            ins = nc.tensor.matmul(PROD[k][:, t * C:(t + 1) * C],
                                                   D["yb"][:, blk, :].rearrange("p (j s) -> p s j", s=SPB)[:, s, :],
                                                   ssm_out_w[:, blk, :], start=(blk == 0), stop=(blk == 1))
                    ins.then_inc(s_out, 1)

            e.wait_ge(s_const, 7)
            ssm_order(e.Fori, prep, front, back, nothing, result)

        TB, EB, SB, OB = banks[0], banks[1:3], banks[3:7], banks[7]
        MAX_EXP = 87.0
        POSTS = 9
        SCALE = float(MQK) ** -0.5

        def ml_order(fori, pre, front, back, post):
            for k in range(4):
                pre(0, 0, k)
            front(0, 0, 0)

            def body(c, par, is_first, is_last):
                for b in range(NB):
                    if b + 1 < NB:
                        front(c, par, b + 1)
                    elif not is_last:
                        front(c + 1, 1 - par, 0)
                    if not is_last and b < NB - 1:
                        for k in ((0, 1), (2,), (3,))[b]:
                            pre(c + 1, 1 - par, k)
                    back(c, par, b)
                    if not is_first:
                        post(c - 1, 1 - par, b)

            body(0, 0, True, False)
            with fori(0, CHUNKS // 2 - 1) as it:
                body(it * 2 + 1, 1, False, False)
                body(it * 2 + 2, 0, False, False)
            body(CHUNKS - 1, 1, False, True)
            for k in range(4):
                post(CHUNKS - 1, 1, k)

        def ml_vector(e, ln0):
            D = ml
            for n, v in (("if_pad", 0.0), ("qk_pad", 0.0), ("kw", 0.0), ("S", 0.0), ("brows", 0.0), ("ones", 1.0), ("v1", 1.0),
                         ("restart", 1.0), ("mprev", FAR)):
                ap = D[n][tuple([slice(None)] * len(D[n].shape))]
                last = nc.vector.memset(ap, v)
            last.then_inc(g_const, 1)
            e.wait_ge(g_const, 1)
            nc.vector.memset(D["restart"][:, :].rearrange("p (c t) -> p c t", t=P)[:, :, 0:1], 0.0)
            for k in range(2):
                nc.vector.tensor_copy(D["qk_pad"][:, k, :, :].rearrange("p g (h d) -> p (g h) d", d=32)[:, :, 0:MQK],
                                      ml_qk_w[:, k, :].rearrange("p (h d) -> p h d", d=MQK))
                nc.vector.tensor_copy(D["if_pad"][:, k, 0:3 * MH].rearrange("p (r h) -> p r h", h=MH),
                                      ml_if_w[:, k, None, :].to_broadcast([P, 3, MH]))
            nc.vector.tensor_copy(
                D["brows"][:, :].rearrange("p (b r h) -> p b r h", b=NB, h=MH)[:, :, 0:3, :],
                ml_if_b[:, None, None, :].to_broadcast([2, NB, 3, MH])).then_inc(g_const, 1)
            q4 = ident[:, :].rearrange("p (b r h) -> p h b r", b=NB, h=MH)
            nc.vector.reduce_sum(D["later"][:, 0:1], ident[:, :].rearrange("p (b x) -> p b x", b=NB)[:, :, MH:32], AX.XY)
            nc.vector.reduce_sum(D["later"][:, 1:2], ident[:, :].rearrange("p (b x) -> p b x", b=NB)[:, :, 2 * MH:32], AX.XY)
            nc.vector.reduce_sum(D["indf"][:, :], q4[:, :, :, 0:3], AX.XY)
            nc.vector.reduce_sum(D["head"][:, :], q4[:, :, :, 0], AX.X)
            nc.vector.reduce_sum(D["blocks"][:, :], ident[:, :].rearrange("p (h d) -> p h d", d=32), AX.X).then_inc(g_const, 1)
            e.wait_ge(g_const, 3)
            nc.vector.tensor_scalar(D["later"][:, :], D["later"][:, :], -1.0, None, ALU.mult)
            nc.vector.tensor_copy(D["ind"][:, :].rearrange("p (h g) -> p g h", g=2), D["indf"][:, :].rearrange("p (g h) -> p g h", g=2))
            nc.vector.tensor_copy(D["heads"][:, :, :].rearrange("p g (h d) -> p (g h) d", d=32),
                                  D["head"][:, :, None].to_broadcast([P, MH, 32])).then_inc(g_ind, 1)
            e.wait_ge(g_bias, 1)
            nc.vector.tensor_scalar(D["bcols"][:, :], banks[7][:, 0:2], 1.0 / GATE_CAP, None, ALU.mult).then_inc(g_bias, 1)

            def stage(s, i, b, par):
                if s == 0:
                    ln_vector_stats(e, i + ln0, i)
                elif s == 1:
                    ln_vector_norm(e, i + ln0, i)
            pipeline(e.Fori, 3, stage)

            r = {n: D[n][:, :] for n in ("i", "f", "e", "u", "l", "m", "a", "b", "part", "a3", "b3")}
            chunks = lambda ap: ap.rearrange("p (c t) -> p c t", t=P)
            V = nc.vector

            e.wait_ge(g_rows, 4)
            V.tensor_scalar(r["f"], r["f"], GATE_CAP, None, ALU.mult).then_inc(g_rows, 1)
            e.wait_ge(g_rows, 5)
            V.tensor_scalar(r["i"], r["i"], GATE_CAP, None, ALU.mult).then_inc(g_rows, 1)
            e.wait_ge(g_rows, 10)
            V.scalar_tensor_tensor(r["e"], r["u"], 1.0, r["e"], ALU.subtract, ALU.subtract).then_inc(g_rows, 1)
            e.wait_ge(g_rows, 11)
            V.scalar_tensor_tensor(r["l"], r["f"], 0.0, r["l"], ALU.min, ALU.subtract).then_inc(g_rows, 1)
            e.wait_ge(g_rows, 12)
            V.tensor_tensor(r["l"], r["l"], r["e"], ALU.add).then_inc(g_rows, 1)
            e.wait_ge(g_rows, 13)
            V.tensor_tensor_scan(r["u"], D["restart"][:, :], r["l"], 0.0, ALU.mult, ALU.add).then_inc(g_rows, 1)
            e.wait_ge(g_rows, 14)
            V.tensor_tensor_scan(r["m"], r["l"], r["i"], FAR, ALU.add, ALU.max).then_inc(g_rows, 1)
            e.wait_ge(g_rows, 15)
            V.tensor_copy(D["mprev"][:, 1:], chunks(r["m"])[:, 0:CHUNKS - 1, P - 1])
            V.tensor_tensor(r["a"], r["i"], r["u"], ALU.subtract)
            V.tensor_tensor(r["b"], r["u"], r["m"], ALU.subtract).then_inc(g_rows, 1)
            e.wait_ge(g_rows, 16)
            V.tensor_tensor(chunks(r["i"]), chunks(r["a"]), chunks(r["b"])[:, :, P - 1:P].to_broadcast([P, CHUNKS, P]), ALU.add)
            V.tensor_tensor(chunks(r["f"]), chunks(r["b"]), D["mprev"][:, :, None].to_broadcast([P, CHUNKS, P]),
                            ALU.add).then_inc(g_rows, 1)
            e.wait_ge(g_rows, 20)
            at = 20
            for x, parts in (("a", "a3"), ("b", "b3")):
                for k in range(2):
                    V.tensor_copy(r["part"], r[x]).then_inc(g_rows, 1)
                    at += 1
                    e.wait_ge(g_rows, at)
                    V.scalar_tensor_tensor(r[parts] if k else r[x], r["part"], D["later"][:, k:k + 1], r[x], ALU.mult,
                                           ALU.add).then_inc(g_rows, 1)
                    at += 1
                    e.wait_ge(g_rows, at)
            for n, dst in enumerate(("WT", "RT", "eT")):
                for half in range(2):
                    e.wait_ge(g_turn, 2 * n + half + 1)
                    last = V.tensor_scalar(D[dst][:, half * 4 * NB * MH:(half + 1) * 4 * NB * MH].rearrange("p (c b h) -> p c b h", c=4, b=NB),
                                         banks[2 * n + half][:, :].rearrange("p (c b x) -> p c b x", c=4, b=NB)[:, :, :, 0:MH],
                                         1e-6 if dst == "eT" else 0.0, None, ALU.add)
            e.wait_ge(g_turn, 6 + 2 * NB)
            V.tensor_copy(D["decay"][:, :].rearrange("p (c x) -> p x c", c=CHUNKS),
                          banks[6][:, 0:2 * NB * CHUNKS].rearrange("p (x c) -> p x c", c=CHUNKS)).then_inc(g_const, 1)
            e.wait_ge(g_const, 4)

            def pre(c, par, k):
                if k == 0:
                    if not first(c):
                        e.wait_ge(g_e, c * NB - NB)
                        e.wait_ge(g_ovk, c * NB - NB)
                    V.tensor_copy(D["ac"][:, par, :], D["a3"][:, bass.ds(c * P, P)])
                    V.tensor_copy(D["xc"][:, par, :].rearrange("p (b t) -> p b t", b=NB),
                                  D["xT"][:, :].rearrange("p (b t) -> p b t", b=NB)[:, :, bass.ds(c * P, P)]).then_inc(g_xc, 1)

            def front(c, par, b):
                u, k = c * NB + b, b % 2
                e.wait_ge(g_D, u + 1)
                e.wait_ge(g_s, u + 1)
                e.wait_ge(g_o, u + 1)
                for r in range(4):
                    C_ = D["D"][:, k, r * 2 * P:(r + 1) * 2 * P]
                    last = V.tensor_tensor(C_, C_, SB[r][:, 0:2 * P], ALU.mult)
                last.then_inc(g_c, 1)

            def back(c, par, b):
                u, k, n = c * NB + b, b % 2, MH * MV1
                bank = OB
                e.wait_ge(g_o, u + (CREDIT + 1))
                V.tensor_tensor(D["t1"][:, k, :].rearrange("p (h d) -> p h d", h=MH),
                                bank[:, n:2 * n].rearrange("p (h d) -> p h d", h=MH),
                                D["RT"][:, bass.ds(c * (NB * MH) + b * MH, MH), None].to_broadcast([P, MH, MV1]),
                                ALU.mult).then_inc(g_t, 1)
                V.tensor_tensor(D["um"][:, k, :].rearrange("p (g h d) -> p g h d", g=2, h=4),
                                bank[:, 2 * n:3 * n].rearrange("p (g h d) -> p g h d", g=2, h=4),
                                D["blocks"][:, None, :, None].to_broadcast([P, 2, 4, MV1]), ALU.mult).then_inc(g_t, 1)
                e.wait_ge(g_t, u * 2 + 1)
                V.tensor_tensor(D["T"][:, par, b, :, :].rearrange("p h d -> p (h d)"), D["t1"][:, k, :], bank[:, 0:n],
                                ALU.add).then_inc(g_T, 1)
                e.wait_ge(g_t, u * 2 + 2)
                e.wait_ge(g_state, u + 1)
                for g in range(2):
                    last = V.scalar_tensor_tensor(D["S"][:, b, g, :], D["S"][:, b, g, :],
                                                  D["decay"][:, bass.ds(c * (2 * NB) + (g * NB + b), 1)],
                                                  D["um"][:, k, g * 4 * MV1:(g + 1) * 4 * MV1], ALU.mult, ALU.add)
                last.then_inc(g_state, 1)

            def post(c, par, piece):
                T = D["T"][:, par, :, :, :]
                of_h = [P, NB, MH, MV]
                n, h, mu, hc = D["n"][:, :, :], D["h"][:, :, :, :], D["mu"][:, :, :], D["hc"][:, :, :, :]

                def steps(at, *todo):
                    for k, ins in enumerate(todo):
                        if k:
                            e.wait_ge(g_post, c * POSTS + (at + k + POSTS))
                        ins().then_inc(g_post, 1)

                if piece == 0:
                    e.wait_ge(g_T, c * NB + (NB + CREDIT))
                    e.wait_ge(g_y, c)
                    V.tensor_scalar(D["eo1"][:, :, :], D["eo"][:, par, :, :], MAX_EXP, None, ALU.min)
                    steps(0, lambda: V.scalar_tensor_tensor(n, T[:, :, :, MV], -1.0, T[:, :, :, MV], ALU.mult, ALU.max),
                          lambda: V.scalar_tensor_tensor(n, n, 1e-6,
                                                         D["eT"][:, bass.ds(c * (NB * MH), NB * MH)].rearrange("p (b h) -> p b h", h=MH),
                                                         ALU.add, ALU.max),
                          lambda: V.reciprocal(n, n),
                          lambda: V.tensor_tensor(h, T[:, :, :, 0:MV], D["n"][:, :, :, None].to_broadcast(of_h), ALU.mult),
                          lambda: V.reduce_sum(mu, h, AX.X),
                          lambda: V.scalar_tensor_tensor(hc, D["mu"][:, :, :, None].to_broadcast(of_h), -1.0 / MV, h, ALU.mult,
                                                         ALU.add))
                elif piece == 1:
                    e.wait_ge(g_sq, c + 1)
                    V.tensor_scalar(D["eo1"][:, :, :], D["eo1"][:, :, :], 1.0, None, ALU.add)
                    steps(6, lambda: V.reduce_sum(mu, D["sq"][:, :, :, :], AX.X),
                          lambda: V.tensor_scalar(D["var"][:, :, :], mu, 1.0 / MV, 1e-6, ALU.mult, ALU.add))
                elif piece == 2:
                    e.wait_ge(g_post, c * POSTS + (8 + POSTS))
                    V.reciprocal(D["eo1"][:, :, :], D["eo1"][:, :, :])
                    e.wait_ge(g_pow, c + 1)
                    V.tensor_tensor(h, D["hw"][:, :, :, :], D["rstd"][:, :, :, None].to_broadcast(of_h), ALU.mult).then_inc(g_post, 1)
                    e.wait_ge(g_post, c * POSTS + (9 + POSTS))
                    if not first(c):
                        e.wait_ge(g_b0, y_fill(c - 1) + 1)
                    V.tensor_tensor(D["y"][:, :, :], D["h"][:, :, :, :].rearrange("p b h d -> p b (h d)"), D["eo1"][:, :, :],
                                    ALU.mult).then_inc(g_y, 1)

            ml_order(e.Fori, pre, front, back, post)
            for i in range(NSUP):
                e.wait_ge(g_down, i + 1)
                at = slice(i * SUP, (i + 1) * SUP)
                V.tensor_tensor(X[:, at, :], X[:, at, :], banks[2 + i % 2][:, :].rearrange("p (k c) -> p k c", k=SUP),
                                ALU.add).then_inc(g_add, 1)

        def pre_fill(c, k):
            return c * 4 + k if isinstance(c, int) and c < 2 else c * 5 + (k - 2)

        def y_fill(c):
            return 38 + c - 6 if isinstance(c, int) and c > 5 else c * 5 + 12

        def fills_before(c, b):
            if isinstance(c, int) and c < 2:
                return [4, 4, 6, 7][b] if c == 0 else 8
            if isinstance(c, int):
                return pre_fill(c + 1, 0)
            return c * 5 + 2 if b == 0 else c * 5 + 3 + [0, 2, 3][b - 1]

        def ml_pool(e, ln0):
            D = ml
            nc.gpsimd.memset(D["causal"][:, :], 0.0).then_inc(g_pconst, 1)
            e.wait_ge(g_pconst, 1)
            nc.gpsimd.affine_select(out=D["causal"][:, :], in_=D["causal"][:, :], compare_op=ALU.is_ge, fill=FAR,
                                    base=0, pattern=[[1, P]], channel_multiplier=-1).then_inc(g_pconst, 1)

            def stage(s, i, b, par):
                if s == 0:
                    ln_pool(e, i + ln0)
            pipeline(e.Fori, 3, stage)
            e.wait_ge(g_rows, 28)
            e.wait_ge(g_const, 4)

            def pre(c, par, k):
                if k == 0:
                    if not first(c):
                        e.wait_ge(g_e, c * NB - NB)
                    nc.gpsimd.tensor_tensor(D["bm"][:, par, :, :],
                                            D["b3"][:, None, bass.ds(c * P, P)].to_broadcast([P, MH, P]),
                                            D["ind"][:, :, None].to_broadcast([P, MH, P]), ALU.mult).then_inc(g_bm, 1)

            def front(c, par, b):
                u, k = c * NB + b, b % 2
                e.wait_ge(g_ovkused, u + 1)
                e.wait_ge(g_o, u + 1)
                nc.gpsimd.tensor_tensor(D["kw"][:, k, :, 0:MQK], D["k"][:, k, :].rearrange("p (h d) -> p h d", d=MQK),
                                        D["WT"][:, bass.ds(c * (NB * MH) + b * MH, MH), None].to_broadcast([P, MH, MQK]),
                                        ALU.mult).then_inc(g_kw, 1)

            def post(c, par, piece):
                if piece == 1:
                    e.wait_ge(g_y, c)
                    e.wait_ge(g_post, c * POSTS + (6 + POSTS))
                    nc.gpsimd.tensor_tensor(D["hw"][:, :, :, :], D["hc"][:, :, :, :],
                                            ml_norm_w[:, None, :].to_broadcast([P, NB, C]).rearrange("p b (h d) -> p b h d", d=MV),
                                            ALU.mult)
                    e.wait_ge(g_post, c * POSTS + (8 + POSTS))
                    nc.gpsimd.tensor_tensor(D["rstd"][:, :, :], D["var"][:, :, :],
                                            minus_half[:, 0:NB * MH].rearrange("p (b h) -> p b h", h=MH), ALU.pow).then_inc(g_pow, 1)

            ml_order(e.Fori, pre, front, nothing, post)

        def ml_scalar(e, ln0):
            D = ml

            def stage(s, i, b, par):
                if s == 1:
                    e.wait_ge(xn_turned, i + (ln0 + 1))
                    xT = D["xT"][:, bass.ds(b * NT, NT)].rearrange("p (j s) -> p s j", s=SPB)[:, par * SUP:(par + 1) * SUP, :]
                    nc.scalar.activation(xT, banks[4][:, :].rearrange("p (s j) -> p s j", s=SUP), ACT.Copy).then_inc(xT_ready, 1)
            pipeline(e.Fori, 3, stage)
            e.wait_ge(g_bias, 2)
            n = 0
            for k, name in ((1, "f"), (0, "i")):
                for half in range(2):
                    n += 1
                    e.wait_ge(g_gate, n)
                    nc.scalar.activation(D[name][:, half * W:(half + 1) * W], banks[n - 1][:, :], ACT.Tanh, scale=1.0 / GATE_CAP,
                                         bias=D["bcols"][:, k:k + 1]).then_inc(g_rows, 1)
            for at, dst, src, fn, scale, bias in ((6, "e", "f", ACT.Abs, 1.0, 0.0), (7, "e", "e", ACT.Exp, -1.0, 0.0),
                                                  (8, "u", "e", ACT.Identity, 1.0, 1.0), (9, "l", "u", ACT.Ln, 1.0, 0.0),
                                                  (17, "i", "i", ACT.Exp, 1.0, 0.0), (17, "f", "f", ACT.Exp, 1.0, 0.0),
                                                  (17, "e", "m", ACT.Exp, -1.0, 0.0)):
                e.wait_ge(g_rows, at)
                nc.scalar.activation(D[dst][:, :], D[src][:, :], fn, scale=scale, bias=bias).then_inc(g_rows, 1)

            def pre(c, par, k):
                e.wait_ge(g_b0, pre_fill(c, k) + 1)
                if not first(c):
                    e.wait_ge(g_o, c * NB + (CREDIT - NB))
                dst = D["qT" if k % 2 == 0 else "kT"][:, par, k // 2, :]
                nc.scalar.activation(dst, TB[:, :], ACT.Copy, scale=1.0 if k % 2 == 0 else SCALE).then_inc(g_b0used, 1)

            def front(c, par, b):
                u, k = c * NB + b, b % 2
                e.wait_ge(g_e, u + 1)
                e.wait_ge(g_o, u + 1)
                for g in range(2):
                    last = nc.scalar.activation(D["D"][:, k, g * W:(g + 1) * W], EB[g][:, :], ACT.Exp)
                last.then_inc(g_D, 1)
                e.wait_ge(g_ovk, u + 1)
                if b == 0 and not first(c):
                    e.wait_ge(g_post, c * POSTS + (1 - POSTS))
                nc.scalar.activation(D["eo"][:, par, b, :], TB[:, 0:C], ACT.Copy, scale=-1.0)
                nc.scalar.activation(D["v1"][:, k, :, 0:MV], TB[:, C:2 * C].rearrange("p (h d) -> p h d", d=MV), ACT.Copy)
                nc.scalar.activation(D["k"][:, k, :], TB[:, 2 * C:2 * C + MH * MQK], ACT.Copy,
                                     scale=SCALE).then_inc(g_ovkused, 1)

            def post(c, par, piece):
                if piece == 0:
                    e.wait_ge(g_post, c * POSTS + (6 + POSTS))
                    nc.scalar.activation(D["eo1"][:, :, :], D["eo1"][:, :, :], ACT.Exp)
                    nc.scalar.activation(D["sq"][:, :, :, :], D["hc"][:, :, :, :], ACT.Square).then_inc(g_sq, 1)
                elif piece == 3:
                    e.wait_ge(g_b0, y_fill(c) + 1)
                    nc.scalar.activation(D["xT"][:, :].rearrange("p (b t) -> p b t", b=NB)[:, :, bass.ds(c * P, P)], TB[:, :].rearrange("p (b t) -> p b t", b=NB),
                                         ACT.Copy).then_inc(g_b0used, 1)

            e.wait_ge(g_const, 4)
            ml_order(e.Fori, pre, front, nothing, post)

        def ml_tensor(e, ln0):
            D = ml
            e.wait_ge(g_const, 2)
            nc.tensor.transpose(banks[7][:, 0:2], D["brows"][:, :], ident[0:2, 0:2]).then_inc(g_bias, 1)

            def stage(s, i, b, par):
                if s == 1:
                    e.wait_ge(xT_ready, i + ln0)
                    ln_tensor(e, i + ln0, banks[4])
            pipeline(e.Fori, 3, stage)
            e.wait_ge(xT_ready, ln0 + NSUP)
            n = 0
            for k in (1, 0):
                for half in range(2):
                    for b in range(NB):
                        last = nc.tensor.matmul(banks[n][32 * b:32 * (b + 1), :], D["if_pad"][:, k, :],
                                                D["xT"][:, b * NT + half * W:b * NT + (half + 1) * W], start=True, stop=True)
                    last.then_inc(g_gate, 1)
                    n += 1
            e.wait_ge(g_rows, 20)
            for n, src in enumerate("ife"):
                for half in range(2):
                    for k in range(4):
                        last = nc.tensor.transpose(banks[2 * n + half][:, k * P:(k + 1) * P],
                                                   D[src][:, (half * 4 + k) * P:(half * 4 + k + 1) * P], ident[:, :])
                    last.then_inc(g_turn, 1)
            for g in range(2):
                for b in range(NB):
                    at = (g * NB + b) * CHUNKS
                    last = nc.tensor.matmul(banks[6][:, at:at + CHUNKS], D["heads"][32 * b:32 * (b + 1), g, :],
                                            D["f"][32 * b:32 * (b + 1), :].rearrange("p (c t) -> p c t", t=P)[:, :, P - 1],
                                            start=True, stop=True)
                    last.then_inc(g_turn, 1)
                    e.wait_ge(g_turn, 6 + g * NB + b + 1)
            e.wait_ge(g_const, 4)
            e.wait_ge(g_pconst, 2)

            def pre(c, par, k):
                e.wait_ge(g_xc, c + 1)
                if not first(c):
                    e.wait_ge(g_ovkused, c * NB + ((0, 0, 1, 2)[k] + 2 - NB))
                if not (first(c) and k == 0):
                    e.wait_ge(g_b0used, pre_fill(c, k))
                nc.tensor.matmul(TB[:, :], D["qk_pad"][:, k % 2, k // 2, :], D["xc"][:, par, :], start=True,
                                 stop=True).then_inc(g_b0, 1)

            def front(c, par, b):
                u = c * NB + b
                rows, cols = slice(32 * b, 32 * (b + 1)), slice(b * P, (b + 1) * P)
                e.wait_ge(g_bm, c + 1)
                e.wait_ge(g_D, u)
                for g in range(2):
                    dst = EB[g][:, :].rearrange("p (h s) -> p h s", h=4)
                    nc.tensor.matmul(dst, D["ac"][rows, par, :], D["ind"][rows, g * 4:(g + 1) * 4, None].to_broadcast([32, 4, P]),
                                     start=True, stop=False)
                    nc.tensor.matmul(dst, D["ones"][rows, :], D["bm"][rows, par, g * 4:(g + 1) * 4, :], start=False, stop=False)
                    last = nc.tensor.matmul(dst, identb[:, :], D["causal"][:, None, :].to_broadcast([P, 4, P]), start=False, stop=True)
                last.then_inc(g_e, 1)
                e.wait_ge(g_ovkused, u)
                e.wait_ge(g_b0used, fills_before(c, b))
                nc.tensor.matmul(TB[:, 0:2 * C + MH * MQK], D["xc"][:, par, cols], ml_ovk_w[:, :], start=True,
                                 stop=True).then_inc(g_ovk, 1)
                e.wait_ge(g_c, u + CREDIT)
                if b == 0:
                    e.wait_ge(g_b0used, pre_fill(c, 3) + 1)
                for h in range(MH):
                    at = slice(32 * (h % 4), 32 * (h % 4) + MQK)
                    last = nc.tensor.matmul(SB[h % 4][:, (h // 4) * P:(h // 4 + 1) * P], D["kT"][at, par, h // 4, cols],
                                            D["qT"][at, par, h // 4, cols], start=True, stop=True)
                last.then_inc(g_s, 1)

            def back(c, par, b):
                u, k, n = c * NB + b, b % 2, MH * MV1
                cols = slice(b * P, (b + 1) * P)
                e.wait_ge(g_T, u + CREDIT)
                e.wait_ge(g_c, u + (CREDIT + 1))
                e.wait_ge(g_ovkused, u + 1)
                for h in range(MH):
                    nc.tensor.matmul(OB[:, h * MV1:(h + 1) * MV1], D["D"][:, k, (h % 4 * 2 + h // 4) * P:(h % 4 * 2 + h // 4 + 1) * P],
                                     D["v1"][:, k, h, :], start=True, stop=True)
                e.wait_ge(g_state, u + 1)
                for g in range(2):
                    nc.tensor.matmul(OB[:, n + g * 4 * MV1:n + (g + 1) * 4 * MV1], D["qT"][:, par, g, cols], D["S"][:, b, g, :],
                                     start=True, stop=True)
                e.wait_ge(g_kw, u + 1)
                for g in range(2):
                    last = nc.tensor.matmul(OB[:, 2 * n + g * 4 * MV1:2 * n + (g + 1) * 4 * MV1],
                                            D["kw"][:, k, g * 4:(g + 1) * 4, :].rearrange("p h d -> p (h d)"),
                                            D["v1"][:, k, g * 4:(g + 1) * 4, :].rearrange("p h d -> p (h d)"), start=True, stop=True)
                last.then_inc(g_o, 1)

            def post(c, par, piece):
                if piece == 3:
                    e.wait_ge(g_y, c + 1)
                    e.wait_ge(g_b0used, y_fill(c))
                    e.wait_ge(g_ovkused, CHUNKS * NB if isinstance(c, int) and c > 5 else c * NB + (2 * NB + 1))
                    for b in range(NB):
                        last = nc.tensor.transpose(TB[:, b * P:(b + 1) * P], D["y"][:, b, :], ident[:, :])
                    last.then_inc(g_b0, 1)

            ml_order(e.Fori, pre, front, back, post)
            e.wait_ge(g_b0used, y_fill(CHUNKS - 1) + 1)
            for i in range(NSUP):
                b, half = divmod(i, 2)
                if i >= 2:
                    e.wait_ge(g_add, i - 1)
                for k in range(SUP):
                    last = nc.tensor.matmul(banks[2 + i % 2][:, k * C:(k + 1) * C],
                                            D["xT"][:, b * NT:(b + 1) * NT].rearrange("p (j s) -> p s j", s=SPB)[:, half * SUP + k, :],
                                            ml_down_w[:, :], start=True, stop=True)
                last.then_inc(g_down, 1)


        def run(e, name):
            mlps = []
            ln = 0
            for k, phase in enumerate(order):
                if k:
                    e.wait_ge(phase_done, 4 * k)
                if phase in ("ffn0", "ffn1"):
                    kind = int(phase[-1])
                    {"vector": mlp_vector, "scalar": mlp_scalar, "gpsimd": mlp_pool, "tensor": mlp_tensor}[name](
                        e, Mlp(kind, mlps), ln)
                    mlps.append(kind)
                else:
                    PARTS[phase][name](e, ln)
                if phase != "setup":
                    ln += NSUP
                e.drain().then_inc(phase_done, 1)

        PARTS = {"setup": {"vector": lambda e, n: setup_vector(e), "scalar": lambda e, n: setup_scalar(e),
                           "gpsimd": lambda e, n: setup_pool(e), "tensor": lambda e, n: setup_tensor(e)}}
        PARTS["lin"] = {"vector": lin_vector, "scalar": lin_scalar, "gpsimd": lin_pool, "tensor": lin_tensor}
        PARTS["rnn"] = {"vector": rnn_vector, "scalar": rnn_scalar, "gpsimd": rnn_pool, "tensor": rnn_tensor}
        PARTS["ssm"] = {"vector": ssm_vector, "scalar": ssm_scalar, "gpsimd": ssm_pool, "tensor": ssm_tensor}
        PARTS["mlstm"] = {"vector": ml_vector, "scalar": ml_scalar, "gpsimd": ml_pool, "tensor": ml_tensor}

        block = ctx.enter_context(nc.Block())

        @block.sync
        def _(e):
            setup_sync(e)
            e.wait_ge(x_loaded, 16 * NB)
            e.wait_ge(phase_done, 4 * len(order))
            for b in range(NB):
                e.dma_start(out[b].rearrange("(j s) c -> j s c", s=SPB), X[:, b * SPB:(b + 1) * SPB, :]).then_inc(stored, 16)
            e.wait_ge(stored, 16 * NB)

        @block.vector
        def _(e):
            for s in (m_upused, m_h, g_c, g_T):
                e.sem_inc(s, CREDIT)
            e.sem_inc(g_state, NB)
            e.sem_inc(g_post, POSTS)
            e.sem_inc(s_scan, RING)
            e.wait_ge(x_loaded, 16 * NB)
            run(e, "vector")

        @block.scalar
        def _(e):
            for s in (m_silu, m_wbs):
                e.sem_inc(s, CREDIT)
            e.sem_inc(s_da, RING)
            run(e, "scalar")

        @block.gpsimd
        def _(e):
            e.sem_inc(m_hl, CREDIT)
            e.sem_inc(s_dbu, RING)
            run(e, "gpsimd")

        @block.tensor
        def _(e):
            e.sem_inc(m_down, CREDIT)
            e.sem_inc(g_o, CREDIT)
            e.sem_inc(s_acc, RING)
            run(e, "tensor")


_INS = ['L0_attn_a_x', 'L0_attn_a_qkv_w', 'L0_attn_a_qkv_b', 'L0_attn_a_proj_w', 'L0_attn_a_proj_b', 'L0_attn_b_W_A', 'L0_attn_b_W_B', 'L0_attn_b_W_C', 'L0_ffn_Wr', 'L0_ffn_br', 'L0_ffn_Wg_s', 'L0_ffn_bg_s', 'L0_ffn_Wu_s', 'L0_ffn_bu_s', 'L0_ffn_Wd_s', 'L0_ffn_bd_s', 'L0_ffn_Wg', 'L0_ffn_bg', 'L0_ffn_Wu', 'L0_ffn_bu', 'L0_ffn_Wd', 'L0_ffn_bd', 'L1_attn_a_norm_scale', 'L1_attn_a_in_w', 'L1_attn_a_in_b', 'L1_attn_a_conv_w', 'L1_attn_a_conv_b', 'L1_attn_a_xproj_w', 'L1_attn_a_dt_w', 'L1_attn_a_dt_b', 'L1_attn_a_A_log', 'L1_attn_a_D', 'L1_attn_a_out_w', 'L1_attn_a_out_b', 'L1_attn_b_Wq', 'L1_attn_b_Wk', 'L1_attn_b_Wv', 'L1_attn_b_Wo', 'L1_attn_b_Wi', 'L1_attn_b_bi', 'L1_attn_b_Wf', 'L1_attn_b_bf', 'L1_attn_b_outnorm_w', 'L1_attn_b_Wdown', 'L1_ffn_gate_w', 'L1_ffn_w1', 'L1_ffn_w2', 'L1_ffn_w3', 'L1_ffn_w1s', 'L1_ffn_w2s', 'L1_ffn_w3s']


def kernel(**inputs):
    import numpy as _np
    import concourse.bacc as _bacc
    from concourse import mybir as _mybir
    from concourse.bass_utils import run_bass_kernel_spmd as _run

    nc = _bacc.Bacc("TRN2", target_bir_lowering=False, num_devices=1)
    arrays, aps = {}, {}
    for name in _INS:
        a = _np.ascontiguousarray(inputs[name])
        arrays[f"in_{name}"] = a
        aps[name] = nc.dram_tensor(f"in_{name}", a.shape, _mybir.dt.from_np(a.dtype), kind="ExternalInput").ap()
    out = nc.dram_tensor("out", (NB, NT, C), _mybir.dt.float32, kind="ExternalOutput").ap()
    build(nc, aps, out)
    r = _run(nc, [arrays], core_ids=[0])
    return r.results[0]["out"]
```

```python
import concourse.bass as bass
from concourse import mybir
from contextlib import ExitStack

FP32 = mybir.dt.float32
FP32R = mybir.dt.float32r
BF16 = mybir.dt.bfloat16
ALU = mybir.AluOpType
ACT = mybir.ActivationFunctionType
AX = mybir.AxisListType

P = 128
NB, NT, C = 4, 1024, 128
SPB = NT // P
TILES = NB * SPB
SUP = 4
NSUP = TILES // SUP
W = SUP * P
LN_EPS = 1e-5

E0, I0, TOP0 = 32, 64, 8
PAIRS = E0 // 2
SLOTS0 = PAIRS + 1
E1, I1, TOP1 = 8, 128, 2
SLOTS1 = E1 + 1
SSM_N, SSM_R, SSM_K = 16, 64, 4
LIN_H, LIN_D = 16, 8
MH, MQK, MV = 8, 8, 16
MV1 = MV + 1
GATE_CAP = 15.0
CHUNKS = NT // P
FAR = -1e30
AHEAD = 3

ORDER = ["setup", "lin", "ffn0", "rnn", "ffn0", "ssm", "ffn1", "mlstm", "ffn1"]


def build(nc, A, out, order=ORDER):
    ctx = ExitStack()
    with ctx:
        def sem(name):
            return ctx.enter_context(nc.semaphore(name))

        def sb(name, shape, dt=FP32, where=ctx):
            return where.enter_context(nc.sbuf_tensor(name, shape, dt))

        X = sb("X", [P, TILES, C])
        ident = sb("ident", [P, P])
        identb = sb("identb", [P, P], BF16)
        settle_cell = sb("settle_cell", [P, 1])
        ln_stats = sb("ln_stats", [P, SUP, 6])
        ln_mv = sb("ln_mv", [P, SUP, 2])
        ln_var = sb("ln_var", [P, SUP])
        ln_rstd = sb("ln_rstd", [P, SUP])
        minus_half = sb("minus_half", [P, P])
        xn = sb("xn", [P, SUP, C])
        f1_hi = sb("f1_hi", [P, 3, SLOTS1, P], FP32R)
        f1_lo = sb("f1_lo", [P, 3, SLOTS1, P], FP32R)
        sel1 = sb("sel1", [3 * E1, E1, P], BF16)
        gate1_w = sb("gate1_w", [P, E1])
        sel0 = sb("sel0", [3 * E0, PAIRS, P], BF16)
        router0_w = sb("router0_w", [P, E0])
        router0_b = sb("router0_b", [E0, 1])
        bg_sb = sb("bg_sb", [P, SLOTS0])
        bu_sb = sb("bu_sb", [P, SLOTS0])
        bd_raw = sb("bd_raw", [3 * E0 + 1, P])
        bd_rest = sb("bd_rest", [3 * E0 + 1, P])
        bd_parts = sb("bd_parts", [3 * E0 + 1, 3, P], BF16)
        lin_qkv_w = sb("lin_qkv_w", [P, 3 * C])
        lin_qkv_b = sb("lin_qkv_b", [P, 3 * C])
        lin_proj_w = sb("lin_proj_w", [P, C])
        lin_proj_b = sb("lin_proj_b", [P, C])
        rnn_w = sb("rnn_w", [P, 3, P])
        ssm_in_w = sb("ssm_in_w", [P, 4 * P])
        ssm_xproj = sb("ssm_xproj", [P, 2, SSM_R])
        ssm_xbc = sb("ssm_xbc", [P, 2, 96])
        ssm_dt_w = sb("ssm_dt_w", [SSM_R, 2 * P])
        ssm_out_w = sb("ssm_out_w", [P, 2, C])
        ssm_out_b = sb("ssm_out_b", [P, C])
        ssm_A_log = sb("ssm_A_log", [P, 2, SSM_N])
        ssm_norm = sb("ssm_norm", [P, 1])
        ssm_in_b = sb("ssm_in_b", [P, 4])
        ssm_conv_w = sb("ssm_conv_w", [P, 2, SSM_K])
        ssm_conv_b = sb("ssm_conv_b", [P, 2])
        ssm_dt_b = sb("ssm_dt_b", [P, 2])
        ssm_D = sb("ssm_D", [P, 2])
        ml_qk_w = sb("ml_qk_w", [P, 2, MH * MQK])
        ml_o_w = sb("ml_o_w", [P, C])
        ml_vk_w = sb("ml_vk_w", [P, C + MH * MQK])
        ml_if_w = sb("ml_if_w", [P, 2, MH])
        ml_if_b = sb("ml_if_b", [2, MH])
        ml_norm_w = sb("ml_norm_w", [P, C])
        ml_down_w = sb("ml_down_w", [P, C])
        turns = []

        def turn(name, rows, width, src, dst):
            turns.append((sb(name, [rows, width])[:, :], dst, src))

        def row(ap):
            return ap.rearrange("(a n) -> a n", a=1)

        for n, dst in (("bg", bg_sb), ("bu", bu_sb)):
            turn(f"{n}_rows", PAIRS, P, A["L0_ffn_" + n].rearrange("(a e) i -> a (e i)", e=2), dst[:, 0:PAIRS])
            turn(f"{n}s_row", 1, I0, row(A[f"L0_ffn_{n}_s"]), dst[0:I0, PAIRS:SLOTS0])
        turn("br_row", 1, E0, row(A["L0_ffn_br"]), router0_b[:, :])
        a = "L1_attn_a_"
        turn("norm_row", 1, P, row(A[a + "norm_scale"]), ssm_norm[:, :])
        turn("in_b_rows", 4, P, A[a + "in_b"].rearrange("(k p) -> k p", p=P), ssm_in_b[:, :])
        for blk in range(2):
            turn(f"conv_w_rows{blk}", SSM_K, P, A[a + "conv_w"][:, blk * P:(blk + 1) * P], ssm_conv_w[:, blk, :])
        turn("conv_b_rows", 2, P, A[a + "conv_b"].rearrange("(k p) -> k p", p=P), ssm_conv_b[:, :])
        turn("dt_b_rows", 2, P, A[a + "dt_b"].rearrange("(k p) -> k p", p=P), ssm_dt_b[:, :])
        turn("D_rows", 2, P, A[a + "D"].rearrange("(k p) -> k p", p=P), ssm_D[:, :])
        turn("gate1_rows", E1, P, A["L1_ffn_gate_w"], gate1_w[:, :])

        banks = [ctx.enter_context(nc.psum_tensor(f"bank{i}", [P, 512], FP32)) for i in range(8)]

        region = ExitStack()
        f0_hi = sb("f0_hi", [P, 3, PAIRS, P], FP32R, region)
        f0_lo = sb("f0_lo", [P, 3, PAIRS, P], FP32R, region)
        f0s_hi = sb("f0s_hi", [P, 3, P], FP32R, region)
        f0s_lo = sb("f0s_lo", [P, 3, P], FP32R, region)
        inner = ExitStack()
        st0 = sb("st0", [P, 3, PAIRS, P], where=inner)
        st0s = sb("st0s", [P, 3, P], where=inner)
        st1 = sb("st1", [P, 3, SLOTS1, P], where=inner)
        inner.close()
        inner = ExitStack()
        mlp = {}
        for n, shape, dt in (("xT", [P, W], FP32), ("xh", [P, 2, W], FP32R), ("xl", [P, 2, W], FP32R),
                             ("aff", [P, W], FP32), ("top", [P, SUP, 8], FP32), ("rep", [P, SUP, E0], FP32), ("rep1", [P, SUP, E1 + 8 - TOP1], FP32),
                             ("sum", [P, SUP], FP32), ("rsum", [P, SUP], FP32),
                             ("w", [P, SUP, E0], FP32), ("s", [P, SUP, E1 + 8 - TOP1], FP32), ("rest", [P, SUP, E0], FP32),
                             ("w3", [P, SUP, 3 * E0 + 1], BF16), ("w3_1", [P, SUP, 3 * E1], BF16),
                             ("wT", [P, 2, W], BF16), ("sil", [P, 2, W], FP32), ("gs", [P, 2, W], FP32), ("wb", [P, 2, W], FP32),
                             ("t1", [P, 2, W], FP32), ("h", [P, 2, W], FP32), ("hh", [P, 2, W], FP32R),
                             ("hl", [P, 2, W], FP32R), ("yT", [P, W], FP32)):
            mlp[n] = sb("mlp_" + n, shape, dt, inner)
        inner.close()
        inner = ExitStack()
        lin = {n: sb("lin_" + n, shape, dt, inner) for n, shape, dt in (
            ("xT", [P, W], FP32), ("qkv", [P, 2, SUP, 3 * C], FP32), ("sq", [P, SUP, 2 * C], FP32),
            ("ss", [P, SUP, 2 * LIN_H], FP32), ("rn", [P, SUP, 2 * LIN_H], FP32), ("qT", [P, 2, W], FP32),
            ("kvm", [P, C], FP32), ("m", [P, C], FP32), ("blocks", [P, C], FP32))}
        inner.close()
        inner = ExitStack()
        rnn = {n: sb("rnn_" + n, shape, FP32, inner) for n, shape in (
            ("u", [P, 3]), ("v", [P, 3]), ("raw", [P, 3]), ("sq", [P, 3]), ("norm", [P, 3]), ("norm1", [P, 3]), ("inv", [P, 3]),
            ("isig", [P, 3]), ("ones", [P, P]), ("wT", [P, 3, P]), ("CT", [P, P]), ("xT", [P, 2, W]), ("U", [P, NB, SPB, P]),
            ("carry", [P, NB, P + 1]), ("L", [P, 10, P]), ("R", [P, 13, P]), ("G", [P, SPB, P]))}
        inner.close()
        region.close()
        region = ExitStack()
        ssm = {n: sb("ssm_" + n, shape, dt, region) for n, shape, dt in (
            ("ms", [P, SUP], FP32), ("ms2", [P, SUP], FP32), ("xT", [P, NT], FP32), ("hp", [P, 2, 2, W + SSM_K - 1], FP32),
            ("gs", [P, 2, 2, W], FP32), ("cv", [P, 2, 2, W], FP32), ("ts", [SSM_R, W], FP32), ("v0", [96, W], FP32),
            ("r", [96, W], FP32), ("bc", [96, 2, W], BF16), ("zb", [P, 2, W], FP32), ("ez", [P, 2, W], FP32), ("uz", [P, 2, W], FP32),
            ("lz", [P, 2, W], FP32),
            ("delta", [P, 2, 2, W], FP32), ("du", [P, 2, 2, W], FP32), ("negA", [P, 2, SSM_N], FP32),
            ("last", [P, 2 * SSM_N], FP32), ("bs", [P, 2, W], FP32), ("da", [P, 4, W], FP32), ("dbu", [P, 4, W], FP32),
            ("st", [P, 4, W], FP32), ("sc", [P, 4, W], FP32), ("y2", [P, 2, W], FP32), ("yb", [P, 2, NT], FP32),
            ("sel1", [96, 32], FP32), ("sel", [96, 32, P], BF16), ("diag", [P, 2, SSM_K, P], FP32))}
        region.close()
        region = ExitStack()
        ml = {n: sb("ml_" + n, shape, dt, region) for n, shape, dt in (
            ("brows", [2, P], FP32), ("bcols", [P, 2], FP32), ("if_pad", [P, 2, 32], FP32), ("qk_pad", [P, 2, 2, P], FP32),
            ("ones", [P, P], BF16), ("indf", [P, MH], FP32), ("ind", [P, MH], BF16),
            ("head", [P, MH], FP32), ("heads", [P, 2, P], FP32), ("blocks", [P, 4], FP32),
            ("causal", [P, P], BF16), ("later", [P, 2], FP32), ("restart", [P, NT], FP32),
            ("xT", [P, NB * NT], FP32), ("gate", [P, NB * NT], FP32),
            ("i", [P, NT], FP32), ("f", [P, NT], FP32), ("e", [P, NT], FP32), ("u", [P, NT], FP32), ("l", [P, NT], FP32),
            ("m", [P, NT], FP32),
            ("part", [P, NT], BF16), ("a3", [P, NT], BF16), ("b3", [P, NT], BF16), ("mprev", [P, CHUNKS], FP32),
            ("WT", [P, CHUNKS * NB * MH], FP32), ("RT", [P, CHUNKS * NB * MH], FP32), ("eT", [P, CHUNKS * NB * MH], FP32),
            ("decay", [P, CHUNKS * 2 * NB], FP32), ("S", [P, NB, 2, 4 * MV1], FP32),
            ("xc", [P, 2, W], FP32), ("ac", [P, 2, P], BF16), ("bm", [P, 2, MH, P], BF16),
            ("qT", [P, 2, 2, W], FP32), ("kT", [P, 2, 2, W], FP32), ("v1", [P, 2, MH, 32], FP32), ("oT", [P, 2, 2 * P], FP32),
            ("k", [P, 2, MH * MQK], FP32), ("kw", [P, 2, MH, 32], FP32), ("D", [P, 2, MH * P], FP32),
            ("t1", [P, 2, MH * MV1], FP32), ("um", [P, 2, MH * MV1], FP32), ("T", [P, 2, NB, MH, MV1], FP32),
            ("n", [P, NB, MH], FP32), ("h", [P, NB, MH, MV], FP32), ("mu", [P, NB, MH], FP32), ("hc", [P, NB, MH, MV], FP32),
            ("sq", [P, NB, MH, MV], FP32), ("var", [P, NB, MH], FP32), ("rstd", [P, NB, MH], FP32),
            ("hw", [P, NB, MH, MV], FP32), ("y", [P, NB, C], FP32))}
        region.close()
        rnn["w"] = rnn_w
        lin["qkv_w"], lin["qkv_b"], lin["proj_w"], lin["proj_b"] = lin_qkv_w, lin_qkv_b, lin_proj_w, lin_proj_b

        st_loaded = sem("st_loaded")
        loaded = sem("loaded")
        x_loaded = sem("x_loaded")
        consts_ready = sem("consts_ready")
        consts_step = sem("consts_step")
        hi_split = sem("hi_split")
        lo_split = sem("lo_split")
        bd_step = sem("bd_step")
        rows_turned = sem("rows_turned")
        stored = sem("stored")
        phase_done = sem("phase_done")

        ln_stats_done = sem("ln_stats_done")
        ln_mv_done = sem("ln_mv_done")
        ln_var_done = sem("ln_var_done")
        ln_rstd_done = sem("ln_rstd_done")
        xn_ready = sem("xn_ready")
        xn_turned = sem("xn_turned")
        xT_ready = sem("xT_ready")

        l_const, l_qkv, l_biased, l_sq, l_ss, l_rn, l_unit, l_qt, l_qT, l_kv, l_kvm, l_m, l_mb, l_out, l_add, l_pb = (
            sem("l_" + n) for n in (
                "const",
                "qkv",
                "biased",
                "sq",
                "ss",
                "rn",
                "unit",
                "qt", "qT",
                "kv", "kvm",
                "m", "mb",
                "out", "add",
                "pb"))
        p_turned, p_wT, p_vec, p_raw, p_sq, p_sum, p_norm, p_sigma, p_scaled = (
            sem("p_" + n) for n in (
                "turned", "wT",
                "vec",
                "raw",
                "sq", "sum",
                "norm",
                "sigma",
                "scaled"))
        r_bx, r_u, r_step, r_stepped, r_pow, r_power, r_jump, r_carried, r_out, r_add = (
            sem("r_" + n) for n in (
                "bx", "u",
                "step", "stepped",
                "pow", "power",
                "jump", "carried",
                "out", "add"))

        (s_const, s_diag, s_rms, s_rpow, s_prod, s_evac, s_silu, s_split, s_soft, s_delta, s_du, s_bb, s_bc, s_bs, s_da, s_dbu, s_scan,
         s_mult, s_acc, s_y, s_y3, s_out, s_oadd, s_pb) = (sem("s_" + n) for n in (
             "const",
             "diag",
             "rms", "rpow",
             "prod", "evac",
             "silu",
             "split",
             "soft",
             "delta", "du",
             "bb", "bc",
             "bs",
             "da",
             "dbu",
             "scan",
             "mult",
             "acc",
             "y", "y3",
             "out", "oadd",
             "pb"))

        (g_const, g_ind, g_pconst, g_bias, g_open, g_opened, g_gate, g_rows, g_turn, g_xc, g_bm, g_b0, g_b0used, g_vk, g_vkused, g_kw, g_e, g_D, g_s,
         g_c, g_oT, g_oTused, g_o, g_um, g_t, g_T, g_state, g_post, g_sq, g_pow, g_y, g_down, g_add) = (sem("g_" + n) for n in (
             "const",
             "ind",
             "pconst",
             "bias",
             "open", "opened",
             "gate",
             "rows",
             "turn",
             "xc", "bm",
             "b0", "b0used",
             "vk", "vkused",
             "kw",
             "e", "D",
             "s", "c",
             "oT", "oTused",
             "o",
             "um",
             "t", "T",
             "state",
             "post",
             "sq", "pow",
             "y",
             "down", "add"))

        n_loads = [0]

        def load(eng, dst, src, s=loaded):
            eng.dma_start(dst, src).then_inc(s, 16)
            if s is loaded:
                n_loads[0] += 1

        def setup_sync(e):
            for k, n in enumerate(("Wg", "Wu")):
                load(e, st0[:, k, :, :].rearrange("p a (e i) -> p (a e) i", e=2), A["L0_ffn_" + n].rearrange("e h i -> h e i"), st_loaded)
                load(e, st0s[:, k, 0:I0], A[f"L0_ffn_{n}_s"], st_loaded)
            load(e, st0[:, 2, :, :], A["L0_ffn_Wd"].rearrange("(a e) i h -> (e i) a h", e=2), st_loaded)
            load(e, st0s[0:I0, 2, :], A["L0_ffn_Wd_s"], st_loaded)
            for k, n in enumerate(("w1", "w3", "w2")):
                load(e, st1[:, k, 0:E1, :], A["L1_ffn_" + n].rearrange("e d h -> d e h"), st_loaded)
                load(e, st1[:, k, E1, :], A[f"L1_ffn_{n}s"][0], st_loaded)
            for b in range(NB):
                load(e, X[:, b * SPB:(b + 1) * SPB, :], A["L0_attn_a_x"][b].rearrange("(j s) c -> j s c", s=SPB), x_loaded)
            load(e, router0_w[:, :], A["L0_ffn_Wr"])
            for raw, _, src in turns:
                load(e, raw, src)
            for j in range(3):
                load(e, bd_raw[j * E0:(j + 1) * E0, :], A["L0_ffn_bd"])
            load(e, bd_raw[3 * E0:3 * E0 + 1, :], A["L0_ffn_bd_s"].rearrange("(a h) -> a h", a=1))
            load_more(e)

        def setup_pool(e):
            n = [0]

            def step(i):
                n[0] += 1
                i.then_inc(consts_step, 1)
                e.wait_ge(consts_step, n[0])

            step(nc.gpsimd.memset(ident[:, :], 0.0))
            step(nc.gpsimd.affine_select(out=ident[:, :], in_=ident[:, :], compare_op=ALU.not_equal, fill=1.0,
                                         base=0, pattern=[[-1, P]], channel_multiplier=1))
            step(nc.gpsimd.tensor_copy(identb[:, :], ident[:, :]))
            step(nc.gpsimd.memset(minus_half[:, :], -0.5))
            step(nc.gpsimd.memset(sel0[:, :, :], 0.0))
            for j in range(3):
                step(nc.gpsimd.affine_select(out=sel0[:, :, :], in_=sel0[:, :, :], compare_op=ALU.not_equal, fill=1.0,
                                             base=-E0 * j, pattern=[[-2, PAIRS], [-1, 2], [0, I0]], channel_multiplier=1))
            step(nc.gpsimd.memset(sel1[:, :, :], 0.0))
            for j in range(3):
                step(nc.gpsimd.affine_select(out=sel1[:, :, :], in_=sel1[:, :, :], compare_op=ALU.not_equal, fill=1.0,
                                             base=-E1 * j, pattern=[[-1, E1], [0, P]], channel_multiplier=1))
            e.sem_inc(consts_ready, 1)

        def setup_scalar(e):
            e.wait_ge(st_loaded, 16 * 12)
            for k in range(3):
                nc.scalar.activation(f0_hi[:, k, :, :], st0[:, k, :, :], ACT.Copy).then_inc(hi_split, 1)
                kk = I0 if k == 2 else P
                nn = P if k == 2 else I0
                nc.scalar.activation(f0s_hi[0:kk, k, 0:nn], st0s[0:kk, k, 0:nn], ACT.Copy).then_inc(hi_split, 1)
            for k in range(3):
                nc.scalar.activation(f1_hi[:, k, :, :], st1[:, k, :, :], ACT.Copy).then_inc(hi_split, 1)
            e.wait_ge(loaded, 16 * n_loads[0])
            nc.scalar.activation(bd_parts[:, 0, :], bd_raw[:, :], ACT.Copy).then_inc(bd_step, 1)

        def setup_vector(e):
            for k in range(3):
                e.wait_ge(hi_split, 2 * k + 1)
                nc.vector.tensor_tensor(f0_lo[:, k, :, :], st0[:, k, :, :], f0_hi[:, k, :, :].bitcast(FP32),
                                        ALU.subtract).then_inc(lo_split, 1)
                kk = I0 if k == 2 else P
                nn = P if k == 2 else I0
                e.wait_ge(hi_split, 2 * k + 2)
                nc.vector.tensor_tensor(f0s_lo[0:kk, k, 0:nn], st0s[0:kk, k, 0:nn], f0s_hi[0:kk, k, 0:nn].bitcast(FP32),
                                        ALU.subtract).then_inc(lo_split, 1)
            for k in range(3):
                e.wait_ge(hi_split, 7 + k)
                nc.vector.tensor_tensor(f1_lo[:, k, :, :], st1[:, k, :, :], f1_hi[:, k, :, :].bitcast(FP32),
                                        ALU.subtract).then_inc(lo_split, 1)
            e.wait_ge(bd_step, 1)
            nc.vector.tensor_tensor(bd_rest[:, :], bd_raw[:, :], bd_parts[:, 0, :], ALU.subtract).then_inc(bd_step, 1)
            e.wait_ge(bd_step, 2)
            nc.vector.tensor_copy(bd_parts[:, 1, :], bd_rest[:, :]).then_inc(bd_step, 1)
            e.wait_ge(bd_step, 3)
            nc.vector.tensor_tensor(bd_parts[:, 2, :], bd_rest[:, :], bd_parts[:, 1, :], ALU.subtract).then_inc(bd_step, 1)
            e.wait_ge(x_loaded, 16 * NB)
            e.wait_ge(rows_turned, 1)
            at = 0
            for raw, dst, _ in turns:
                r, n = raw.shape
                nc.vector.tensor_copy(dst, banks[0][0:n, at:at + r])
                at += r

        def setup_tensor(e):
            e.wait_ge(loaded, 16 * n_loads[0])
            e.wait_ge(consts_ready, 1)
            at = 0
            for raw, _, _ in turns:
                r, n = raw.shape
                last = nc.tensor.transpose(banks[0][0:n, at:at + r], raw, ident[0:r, 0:r])
                at += r
            last.then_inc(rows_turned, 1)

        def load_more(e):
            load(e, lin_qkv_w[:, :], A["L0_attn_a_qkv_w"])
            load(e, lin_qkv_b[:, :], row(A["L0_attn_a_qkv_b"]).to_broadcast([P, 3 * C]))
            load(e, lin_proj_w[:, :], A["L0_attn_a_proj_w"])
            load(e, lin_proj_b[:, :], row(A["L0_attn_a_proj_b"]).to_broadcast([P, C]))
            for k, n in enumerate("ABC"):
                load(e, rnn_w[:, k, :], A["L0_attn_b_W_" + n])
            a = "L1_attn_a_"
            load(e, ssm_in_w[:, :], A[a + "in_w"])
            xw = A[a + "xproj_w"].rearrange("(k p) n -> p k n", p=P)
            load(e, ssm_xproj[:, :, :], xw[:, :, 0:SSM_R])
            for j in range(3):
                load(e, ssm_xbc[:, :, 32 * j:32 * (j + 1)], xw[:, :, SSM_R:SSM_R + 32])
            load(e, ssm_dt_w[:, :], A[a + "dt_w"])
            load(e, ssm_out_w[:, :, :], A[a + "out_w"].rearrange("(k p) n -> p k n", p=P))
            load(e, ssm_out_b[:, :], row(A[a + "out_b"]).to_broadcast([P, C]))
            a2 = "L1_attn_b_"
            for k, n in enumerate(("Wq", "Wk")):
                load(e, ml_qk_w[:, k, :], A[a2 + n])
            load(e, ml_o_w[:, :], A[a2 + "Wo"])
            for n, at, width in (("Wv", 0, C), ("Wk", C, MH * MQK)):
                load(e, ml_vk_w[:, at:at + width], A[a2 + n])
            for k, n in enumerate("if"):
                load(e, ml_if_w[:, k, :], A[a2 + "W" + n])
                load(e, ml_if_b[k:k + 1, :], row(A[a2 + "b" + n]))
            load(e, ml_norm_w[:, :], A[a2 + "outnorm_w"].rearrange("(a h) d -> a (h d)", a=1).to_broadcast([P, C]))
            load(e, ml_down_w[:, :], A[a2 + "Wdown"])
            load(e, ssm_A_log[:, :, :], A[a + "A_log"].rearrange("(k p) n -> p k n", p=P))

        def settle(e):
            nc.vector.memset(settle_cell[:, :], 0.0)

        def ln_vector_stats(e, n, i):
            for k in range(SUP):
                last = nc.vector.bn_stats(ln_stats[:, k, :], X[:, bass.ds(i * SUP + k, 1), :])
            last.then_inc(ln_stats_done, 1)
            e.wait_ge(ln_stats_done, n + 1)
            settle(e)
            for k in range(SUP):
                last = nc.vector.bn_aggr(ln_mv[:, k, :], ln_stats[:, k, :])
            last.then_inc(ln_mv_done, 1)
            e.wait_ge(ln_mv_done, n + 1)
            nc.vector.tensor_scalar(ln_var[:, :], ln_mv[:, :, 1], LN_EPS, None, ALU.add).then_inc(ln_var_done, 1)

        def ln_pool(e, n):
            e.wait_ge(ln_var_done, n + 1)
            nc.gpsimd.tensor_tensor(ln_rstd[:, :], ln_var[:, :], minus_half[:, 0:SUP], ALU.pow).then_inc(ln_rstd_done, 1)

        def ln_vector_norm(e, n, i):
            e.wait_ge(ln_rstd_done, n + 1)
            e.wait_ge(xn_turned, n)
            for k in range(SUP):
                last = nc.vector.tensor_scalar(xn[:, k, :], X[:, bass.ds(i * SUP + k, 1), :], ln_mv[:, k, 0:1],
                                               ln_rstd[:, k:k + 1], ALU.subtract, ALU.mult)
            last.then_inc(xn_ready, 1)

        def ln_tensor(e, n, bank):
            e.wait_ge(xn_ready, n + 1)
            for k in range(SUP):
                last = nc.tensor.transpose(bank[:, k * P:(k + 1) * P], xn[:, k, :], ident[:, :])
            last.then_inc(xn_turned, 1)

        def pipeline(fori, depth, stage, beside=None):
            def turn_of(tau, b0, first, last):
                for s in reversed(range(depth)):
                    if first <= tau - s <= last:
                        i = tau - s
                        stage(s, b0 * 2 + i, b0 + i // 2, i % 2)
                if beside:
                    beside(b0 * 2 + tau)

            loops = (NSUP - depth) // 2
            for tau in range(depth):
                turn_of(tau, 0, 0, NSUP)
            with fori(0, loops) as it:
                for tau in range(depth, depth + 2):
                    turn_of(tau, it, 0, NSUP)
            for tau in range(depth + 2 * loops, NSUP + depth):
                turn_of(tau, 0, 0, NSUP - 1)

        m_logits = sem("m_logits")
        m_zeroed = sem("m_zeroed")
        m_aff = sem("m_aff")
        m_affT = sem("m_affT")
        m_top = sem("m_top")
        m_exp = sem("m_exp")
        m_w3 = sem("m_w3")
        m_w3T = sem("m_w3T")
        m_wT = sem("m_wT")
        m_xs = sem("m_xs")
        m_gate = sem("m_gate")
        m_up = sem("m_up")
        m_bc = sem("m_bc")
        m_down = sem("m_down")
        m_silu = sem("m_silu")
        m_gs = sem("m_gs")
        m_wbs = sem("m_wbs")
        m_upused = sem("m_upused")
        m_h = sem("m_h")
        m_hh = sem("m_hh")
        m_hl = sem("m_hl")
        m_yT = sem("m_yT")
        m_yt = sem("m_yt")
        m_xadd = sem("m_xadd")
        GB, UB, WB, YB, MISC = banks[0:2], banks[2:4], banks[4:6], banks[6], banks[7]
        CREDIT = 2

        class Mlp:
            def __init__(self, kind, calls):
                self.kind = kind
                self.slots = SLOTS0 if kind == 0 else SLOTS1
                self.routed = PAIRS if kind == 0 else E1
                self.rows = 3 * (E0 if kind == 0 else E1)
                self.steps = 9 if kind == 0 else 12
                self.slot0 = sum(NSUP * (SLOTS0 if c == 0 else SLOTS1) for c in calls)
                self.routed0 = sum(NSUP * (PAIRS if c == 0 else E1) for c in calls)
                self.spared = NSUP * PAIRS * sum(c == 0 for c in calls)
                self.sup0 = NSUP * len(calls)
                self.exp0 = NSUP * sum(c == 1 for c in calls)
                self.step0 = sum(NSUP * (9 if c == 0 else 12) for c in calls)
                spread = [[0, 2, 4, 6, 8, 9, 12], [17, 19, 21, 23, 25, 27, 29]]
                self.stages = ([spread] * 3 if kind == 0 else
                               [[[-4, -2, 1, 1, 2, 3, 4], [3, 5, 7, 7, 10, 12, 12]],
                                [[0, 0, 0, 1, 2, 3, 4], [6, 6, 6, 7, 9, 9, 13]],
                                [[0, 0, 0, 1, 2, 3, 4], [6, 6, 6, 8, 11, 11, 13]]])
                self.finish_at = SLOTS0 + 1 if kind == 0 else 14

            def width(self, q):
                return I0 if self.kind == 0 and q == PAIRS else P

        def mlp_order(m, lane, fori, prep, early, front, back, finish, tail):
            L = m.slots
            stages = m.stages[lane]
            for st in range(7):
                prep(0, 0, st)
            for st, at in enumerate(stages[0]):
                if at < 0:
                    prep(1, 1, st)
            early(0, 0, 0, m.slot0, m.routed0)
            for f in range(AHEAD):
                early(0, 0, f + 1, m.slot0 + f + 1, m.routed0 + f + 1)
                front(0, 0, f, m.slot0 + f, m.routed0 + f)

            def body(it, last):
                for q in range(2 * L):
                    f = q + AHEAD
                    if q == L:
                        finish(it * 2, 0)
                    for slot, part in ((f + 1, early), (f, front)):
                        if not last or slot < 2 * L:
                            ahead, fq = divmod(slot, L)
                            part(ahead % 2, it * 2 + ahead, fq, it * (2 * L) + (m.slot0 + slot),
                                 it * (2 * m.routed) + (m.routed0 + ahead * m.routed + fq))
                    if last and f == 2 * L:
                        tail()
                    back(q // L, it * 2 + q // L, q % L, it * (2 * L) + (m.slot0 + q))
                    if q == m.finish_at:
                        finish(it * 2, 1)
                    for half in range(1 if last else 2):
                        for st, at in enumerate(stages[half]):
                            if at == q:
                                prep(1 - half, it * 2 + 1 + half, st)
                            elif at + 2 * L == q and not last:
                                prep(1, it * 2 + 3, st)
                finish(it * 2 + 1, 0)
                finish(it * 2 + 1, 2)

            with fori(0, NSUP // 2 - 1) as it:
                body(it, False)
            body(NSUP // 2 - 1, True)

        def nothing(*_):
            pass

        def first(j):
            return isinstance(j, int) and j == 0

        def mlp_vector(e, m, ln0):
            D = mlp

            def prep(par, j, st):
                t = j + m.sup0
                if st == 0:
                    ln_vector_stats(e, j + ln0, j)
                elif st == 1:
                    ln_vector_norm(e, j + ln0, j)
                elif st == 2:
                    e.wait_ge(xT_ready, j + (ln0 + 1))
                    if not first(j):
                        e.wait_ge(m_up, (j - 1) * m.slots + m.slot0)
                    nc.vector.tensor_copy(D["xh"][:, par, :], D["xT"][:, :]).then_inc(m_xs, 1)
                    e.wait_ge(m_xs, t * 2 + 1)
                    nc.vector.tensor_tensor(D["xl"][:, par, :], D["xT"][:, :], D["xh"][:, par, :].bitcast(FP32),
                                            ALU.subtract).then_inc(m_xs, 1)
                elif st in (4, 5):
                    count = [0 if st == 4 else 9 if m.kind == 0 else 2]

                    def step(ins):
                        count[0] += 1
                        ins.then_inc(m_top, 1)
                        e.wait_ge(m_top, j * m.steps + (m.step0 + count[0]))

                    def split(w, rest, w3, E):
                        e.wait_ge(m_w3T, t)
                        step(nc.vector.tensor_copy(w3[:, :, 0:E], w))
                        step(nc.vector.tensor_tensor(rest, w, w3[:, :, 0:E], ALU.subtract))
                        step(nc.vector.tensor_copy(w3[:, :, E:2 * E], rest))
                        nc.vector.tensor_tensor(w3[:, :, 2 * E:3 * E], rest, w3[:, :, E:2 * E], ALU.subtract).then_inc(m_w3, 1)

                    if m.kind == 0 and st == 4:
                        e.wait_ge(m_affT, t + 1)
                        aff = MISC[:, :].rearrange("p (k e) -> p k e", k=SUP)[:, :, 0:E0]
                        settle(e)
                        for k in range(SUP):
                            last = nc.vector.max(D["top"][:, k, :], aff[:, k, :])
                        step(last)
                        settle(e)
                        for k in range(SUP):
                            nc.vector.match_replace(D["rep"][:, k, :], D["top"][:, k, :], aff[:, k, :], 0.0)
                        step(nc.vector.reduce_sum(D["sum"][:, :], D["top"][:, :, :], AX.X))
                        step(nc.vector.tensor_scalar(D["rsum"][:, :], D["sum"][:, :], 1e-9, None, ALU.add))
                        step(nc.vector.reciprocal(D["sum"][:, :], D["rsum"][:, :]))
                        step(nc.vector.tensor_tensor(D["w"][:, :, :], aff, D["rep"][:, :, :], ALU.subtract))
                        step(nc.vector.tensor_tensor(D["rest"][:, :, :], D["w"][:, :, :],
                                                     D["sum"][:, :, None].to_broadcast([P, SUP, E0]), ALU.mult))
                        split(D["rest"][:, :, :], D["w"][:, :, :], D["w3"], E0)
                    elif m.kind == 1 and st == 4:
                        e.wait_ge(m_affT, t + 1)
                        lg = MISC[:, :].rearrange("p (k e) -> p k e", k=SUP)[:, :, 0:E1]
                        settle(e)
                        for k in range(SUP):
                            last = nc.vector.max(D["top"][:, k, :], lg[:, k, :])
                        step(last)
                        step(nc.vector.tensor_tensor(D["rep"][:, :, 0:E1], lg, D["top"][:, :, 0:1].to_broadcast([P, SUP, E1]),
                                                     ALU.subtract))
                    elif m.kind == 1 and st == 5:
                        s, real, rest = D["s"], D["s"][:, :, 0:E1], D["rest"][:, :, 0:E1]
                        e.wait_ge(m_exp, j + (m.exp0 + 1))
                        step(nc.vector.reduce_sum(D["sum"][:, :], D["w"][:, :, 0:E1], AX.X))
                        step(nc.vector.reciprocal(D["rsum"][:, :], D["sum"][:, :]))
                        step(nc.vector.tensor_tensor(real, D["w"][:, :, 0:E1],
                                                     D["rsum"][:, :, None].to_broadcast([P, SUP, E1]), ALU.mult))
                        settle(e)
                        for k in range(SUP):
                            last = nc.vector.max(D["top"][:, k, :], s[:, k, 0:E1])
                        step(last)
                        step(nc.vector.tensor_copy(D["top"][:, :, TOP1:8], s[:, :, E1:E1 + 8 - TOP1]))
                        settle(e)
                        for k in range(SUP):
                            last = nc.vector.match_replace(D["rep1"][:, k, :], D["top"][:, k, :], s[:, k, :], 0.0)
                        step(last)
                        step(nc.vector.tensor_tensor(D["w"][:, :, 0:E1], real, D["rep1"][:, :, 0:E1], ALU.subtract))
                        split(D["w"][:, :, 0:E1], rest, D["w3_1"], E1)

            def early(par, j, q, mm, rr):
                b = (par * m.slots + q) % 2
                if m.kind == 1 and q < m.routed:
                    e.wait_ge(m_wbs, rr + (CREDIT + 1 - m.spared))
                    e.wait_ge(m_gate, mm + 1)
                    nc.vector.tensor_tensor(D["gs"][:, b, :], GB[b][:, :], D["wb"][:, b, :], ALU.mult).then_inc(m_gs, 1)

            def front(par, j, q, mm, rr):
                b, K, routed = (par * m.slots + q) % 2, m.width(q), q < m.routed
                e.wait_ge(m_silu, mm + (CREDIT + 1))
                e.wait_ge(m_up, mm + 1)
                if not routed:
                    e.wait_ge(m_hl, mm + (CREDIT - 1))
                dst = (D["t1"] if routed else D["h"])[0:K, b, :]
                if m.kind == 0:
                    ins = nc.vector.scalar_tensor_tensor(dst, UB[b][0:K, :], bu_sb[0:K, q:q + 1], D["sil"][0:K, b, :],
                                                         ALU.add, ALU.mult)
                else:
                    ins = nc.vector.tensor_tensor(dst, UB[b][:, :], D["sil"][:, b, :], ALU.mult)
                ins.then_inc(m_upused, 1)
                e.wait_ge(m_upused, mm + (CREDIT + 1))
                if routed:
                    if m.kind == 0:
                        e.wait_ge(m_bc, rr + 1)
                    e.wait_ge(m_hl, mm + (CREDIT - 1))
                    by = WB[b][:, :] if m.kind == 0 else D["wb"][:, b, :]
                    nc.vector.tensor_tensor(D["h"][:, b, :], D["t1"][:, b, :], by, ALU.mult).then_inc(m_h, 1)
                else:
                    e.sem_inc(m_h, 1)

            def finish(j, st):
                if st:
                    e.wait_ge(m_yt, j + (m.sup0 + 1))
                    at = bass.ds(j * SUP, SUP)
                    nc.vector.tensor_tensor(X[:, at, :], X[:, at, :], MISC[:, :].rearrange("p (k c) -> p k c", k=SUP),
                                            ALU.add).then_inc(m_xadd, 1)

            if m.kind == 0:
                nc.vector.memset(D["w3"][:, :, 3 * E0:3 * E0 + 1], 1.0)
            else:
                nc.vector.memset(D["s"][:, :, E1:E1 + 8 - TOP1], -1.0)
            nc.vector.memset(D["aff"][:, :], 0.0).then_inc(m_zeroed, 1)
            mlp_order(m, 0, e.Fori, prep, early, front, nothing, finish, nothing)

        def mlp_scalar(e, m, ln0):
            D = mlp

            def prep(par, j, st):
                t = j + m.sup0
                if st == 2:
                    e.wait_ge(xn_turned, j + (ln0 + 1))
                    e.wait_ge(m_xs, t * 2)
                    e.wait_ge(m_logits, t)
                    nc.scalar.activation(D["xT"][:, :], MISC[:, :], ACT.Copy).then_inc(xT_ready, 1)
                elif st == 3:
                    e.wait_ge(m_logits, t + 1)
                    e.wait_ge(m_affT, t)
                    if first(j):
                        e.wait_ge(m_zeroed, m.sup0 // NSUP + 1)
                    if m.kind == 0:
                        nc.scalar.activation(D["aff"][0:E0, :], MISC[0:E0, :], ACT.Sigmoid,
                                             bias=router0_b[:, :]).then_inc(m_aff, 1)
                    else:
                        nc.scalar.activation(D["aff"][0:E1, :], MISC[0:E1, :], ACT.Copy).then_inc(m_aff, 1)
                elif st == 4 and m.kind == 1:
                    e.wait_ge(m_top, j * m.steps + (m.step0 + 2))
                    nc.scalar.activation(D["w"][:, :, 0:E1], D["rep"][:, :, 0:E1], ACT.Exp).then_inc(m_exp, 1)
                elif st == 6:
                    rows = 3 * E0 + 1 if m.kind == 0 else 3 * E1
                    e.wait_ge(m_w3T, t + 1)
                    if not first(j):
                        e.wait_ge(m_up, (j - 1) * m.slots + m.slot0)
                    nc.scalar.activation(D["wT"][0:rows, par, :], MISC[:, :].bitcast(BF16)[0:rows, 0:W],
                                         ACT.Copy).then_inc(m_wT, 1)

            def round_h(b, K, mm):
                e.wait_ge(m_h, mm + (CREDIT + 1))
                e.wait_ge(m_down, mm + (CREDIT - 1))
                nc.scalar.activation(D["hh"][0:K, b, :], D["h"][0:K, b, :], ACT.Copy).then_inc(m_hh, 1)

            def early(par, j, q, mm, rr):
                b = (par * m.slots + q) % 2
                if m.kind == 1 and q < m.routed:
                    e.wait_ge(m_bc, rr + 1)
                    e.wait_ge(m_h, mm + (CREDIT - 1))
                    nc.scalar.activation(D["wb"][:, b, :], WB[b][:, :], ACT.Copy).then_inc(m_wbs, 1)

            def front(par, j, q, mm, rr):
                b, K, routed = (par * m.slots + q) % 2, m.width(q), q < m.routed
                if m.kind == 0:
                    e.wait_ge(m_gate, mm + 1)
                    ins = nc.scalar.activation(D["sil"][0:K, b, :], GB[b][0:K, :], ACT.Silu, bias=bg_sb[0:K, q:q + 1])
                elif routed:
                    e.wait_ge(m_gs, rr + (1 - m.spared))
                    ins = nc.scalar.activation(D["sil"][:, b, :], D["gs"][:, b, :], ACT.Silu)
                else:
                    e.wait_ge(m_gate, mm + 1)
                    ins = nc.scalar.activation(D["sil"][:, b, :], GB[b][:, :], ACT.Silu)
                ins.then_inc(m_silu, 1)
                if not (first(j) and q == 0):
                    round_h(1 - b, m.width((q - 1) % m.slots), mm - 1)

            def tail():
                round_h(1, m.width(m.slots - 1), m.slot0 + NSUP * m.slots - 1)

            def finish(j, st):
                if st == 0:
                    e.wait_ge(m_down, (j + 1) * m.slots + (m.slot0 + CREDIT))
                    e.wait_ge(m_yt, j + m.sup0)
                    nc.scalar.activation(D["yT"][:, :], YB[:, :], ACT.Copy).then_inc(m_yT, 1)

            mlp_order(m, 2, e.Fori, prep, early, front, nothing, finish, tail)

        def mlp_pool(e, m, ln0):
            D = mlp

            def prep(par, j, st):
                if st == 0:
                    ln_pool(e, j + ln0)

            def front(par, j, q, mm, rr):
                b, K = (par * m.slots + q) % 2, m.width(q)
                e.wait_ge(m_hh, mm + 1)
                e.wait_ge(m_down, mm + (CREDIT - 1))
                nc.gpsimd.tensor_tensor(D["hl"][0:K, b, :], D["h"][0:K, b, :], D["hh"][0:K, b, :].bitcast(FP32),
                                        ALU.subtract).then_inc(m_hl, 1)

            mlp_order(m, 0, e.Fori, prep, nothing, front, nothing, nothing, nothing)

        def mlp_tensor(e, m, ln0):
            D = mlp
            E = E0 if m.kind == 0 else E1

            def weights(k, q, part):
                if m.kind == 0 and q == PAIRS:
                    t = (f0s_hi, f0s_lo)[part]
                    return t[:, k, 0:I0] if k < 2 else t[0:I0, k, :]
                return ((f0_hi, f0_lo) if m.kind == 0 else (f1_hi, f1_lo))[part][:, k, q, :]

            def three(dst, k, q, hi, lo, start, stop):
                nc.tensor.matmul(dst, weights(k, q, 0), hi, start=start, stop=False)
                nc.tensor.matmul(dst, weights(k, q, 0), lo, start=False, stop=False)
                return nc.tensor.matmul(dst, weights(k, q, 1), hi, start=False, stop=stop)

            def prep(par, j, st):
                t = j + m.sup0
                if st == 1:
                    if not first(j):
                        e.wait_ge(m_wT, t)
                        e.wait_ge(m_xadd, t - (2 if m.kind == 1 and par == 0 else 1))
                    ln_tensor(e, j + ln0, MISC)
                elif st == 3:
                    e.wait_ge(xT_ready, j + (ln0 + 1))
                    rw = router0_w if m.kind == 0 else gate1_w
                    nc.tensor.matmul(MISC[0:E, :], rw[:, :], D["xT"][:, :], start=True, stop=True).then_inc(m_logits, 1)
                elif st == 4:
                    e.wait_ge(m_aff, t + 1)
                    for k in range(SUP):
                        last = nc.tensor.transpose(MISC[:, k * P:(k + 1) * P], D["aff"][:, k * P:(k + 1) * P], ident[:, :])
                    last.then_inc(m_affT, 1)
                elif st == 6:
                    rows, w3 = (3 * E0 + 1, D["w3"]) if m.kind == 0 else (3 * E1, D["w3_1"])
                    e.wait_ge(m_w3, t + 1)
                    for k in range(SUP):
                        last = nc.tensor.transpose(MISC[:, :].bitcast(BF16)[0:rows, k * P:(k + 1) * P], w3[:, k, 0:rows],
                                                   identb[:, :])
                    last.then_inc(m_w3T, 1)

            def front(par, j, q, mm, rr):
                b, N, routed = (par * m.slots + q) % 2, m.width(q), q < m.routed
                if q == 0:
                    e.wait_ge(m_xs, (j + m.sup0) * 2 + 2)
                    e.wait_ge(m_wT, j + (m.sup0 + 1))

                def spread():
                    nc.tensor.matmul(WB[b][:, :], (sel0 if m.kind == 0 else sel1)[:, q, :], D["wT"][0:m.rows, par, :],
                                     start=True, stop=True).then_inc(m_bc, 1)

                if m.kind == 1:
                    e.wait_ge(m_upused, mm + (CREDIT - 1))
                    if routed:
                        spread()
                else:
                    e.wait_ge(m_silu, mm + (CREDIT - 1))
                three(GB[b][0:N, :], 0, q, D["xh"][:, par, :], D["xl"][:, par, :], True, True).then_inc(m_gate, 1)
                if m.kind == 0:
                    e.wait_ge(m_upused, mm + (CREDIT - 1))
                three(UB[b][0:N, :], 1, q, D["xh"][:, par, :], D["xl"][:, par, :], True, True).then_inc(m_up, 1)
                if m.kind == 0 and routed:
                    e.wait_ge(m_h, mm + (CREDIT - 1))
                    spread()

            def back(par, j, q, mm):
                b, K = (par * m.slots + q) % 2, m.width(q)
                if q == 0:
                    e.wait_ge(m_yT, j + m.sup0)
                    if m.kind == 0:
                        for r in range(3):
                            nc.tensor.matmul(YB[:, :], bd_parts[:, r, :], D["wT"][0:3 * E0 + 1, par, :], start=(r == 0),
                                             stop=False)
                e.wait_ge(m_hl, mm + (CREDIT + 1))
                three(YB[:, :], 2, q, D["hh"][0:K, b, :], D["hl"][0:K, b, :], m.kind == 1 and q == 0,
                      q == m.slots - 1).then_inc(m_down, 1)

            def finish(j, st):
                if st:
                    e.wait_ge(m_yT, j + (m.sup0 + 1))
                    ready = 3 if m.kind == 1 and st == 1 else 2
                    e.wait_ge(m_wT, min(j + ready, NSUP) + m.sup0 if isinstance(j, int) else j + (m.sup0 + ready))
                    e.wait_ge(m_xadd, j + m.sup0)
                    for k in range(SUP):
                        last = nc.tensor.transpose(MISC[:, k * P:(k + 1) * P], D["yT"][:, k * P:(k + 1) * P], ident[:, :])
                    last.then_inc(m_yt, 1)

            upper = (nothing, front) if m.kind == 0 else (front, nothing)
            mlp_order(m, 1, e.Fori, prep, *upper, back, finish, nothing)


        LIN_DEPTH = 6
        LIN_KV, LIN_TURN, LIN_OUT = banks[5], banks[6], banks[7]

        def lin_vector(e, ln0):
            D = lin

            def stage(s, i, b, par):
                if s == 0:
                    ln_vector_stats(e, i + ln0, i)
                elif s == 1:
                    ln_vector_norm(e, i + ln0, i)
                elif s == 2:
                    e.wait_ge(l_qkv, i + 1)
                    for k in range(SUP):
                        last = nc.vector.tensor_tensor(D["qkv"][:, par, k, :], banks[1 + k][:, 0:3 * C], D["qkv_b"][:, :], ALU.add)
                    last.then_inc(l_biased, 1)
                elif s == 3:
                    e.wait_ge(l_sq, i + 1)
                    nc.vector.reduce_sum(D["ss"][:, :, :], D["sq"][:, :, :].rearrange("p k (h d) -> p k h d", d=LIN_D),
                                         AX.X).then_inc(l_ss, 1)
                    e.wait_ge(l_ss, i * 2 + 1)
                    nc.vector.tensor_scalar(D["ss"][:, :, :], D["ss"][:, :, :], 1e-24, None, ALU.max).then_inc(l_ss, 1)
                    e.wait_ge(l_rn, i * 2 + 1)
                    nc.vector.reciprocal(D["rn"][:, :, :], D["rn"][:, :, :]).then_inc(l_rn, 1)
                    e.wait_ge(l_rn, i * 2 + 2)
                    qk = D["qkv"][:, par, :, 0:2 * C]
                    nc.vector.tensor_tensor(qk.rearrange("p k (h d) -> p k h d", d=LIN_D),
                                            qk.rearrange("p k (h d) -> p k h d", d=LIN_D),
                                            D["rn"][:, :, :, None].to_broadcast([P, SUP, 2 * LIN_H, LIN_D]), ALU.mult
                                            ).then_inc(l_unit, 1)
                elif s == 4 and par == 1:
                    e.wait_ge(l_kv, b + 1)
                    nc.vector.tensor_tensor(D["kvm"][:, :], LIN_KV[:, 0:C], D["blocks"][:, :], ALU.mult).then_inc(l_kvm, 1)
                elif s == 5 and par == 1:
                    for half in range(2):
                        e.wait_ge(l_out, b * 2 + half + 1)
                        e.wait_ge(l_pb, b + 1)
                        at = bass.ds(b * SPB + half * SUP, SUP)
                        nc.vector.tensor_tensor(X[:, at, :], X[:, at, :], LIN_OUT[:, :].rearrange("p (k c) -> p k c", k=SUP),
                                                ALU.add).then_inc(l_add, 1)
            pipeline(e.Fori, LIN_DEPTH, stage)

        def lin_pool(e, ln0):
            D = lin

            def stage(s, i, b, par):
                if s == 0:
                    ln_pool(e, i + ln0)
                elif s == 2:
                    if par == 1:
                        e.wait_ge(xn_ready, b * 2 + (ln0 + 2))
                        at = bass.ds(b * SPB, SPB)
                        nc.gpsimd.tensor_tensor(X[:, at, :], X[:, at, :], D["proj_b"][:, None, :].to_broadcast([P, SPB, C]),
                                                ALU.add).then_inc(l_pb, 1)
            nc.gpsimd.memset(D["blocks"][:, :], 1.0).then_inc(l_const, 1)
            e.wait_ge(l_const, 1)
            v = D["blocks"][:, :].rearrange("p (h d) -> p h d", d=LIN_D)
            nc.gpsimd.affine_select(out=v, in_=v, compare_op=ALU.is_ge, fill=0.0, base=0,
                                    pattern=[[-LIN_D, LIN_H], [0, LIN_D]], channel_multiplier=1).then_inc(l_const, 1)
            e.wait_ge(l_const, 2)
            nc.gpsimd.affine_select(out=v, in_=v, compare_op=ALU.is_ge, fill=0.0, base=LIN_D - 1,
                                    pattern=[[LIN_D, LIN_H], [0, LIN_D]], channel_multiplier=-1).then_inc(l_const, 1)
            pipeline(e.Fori, LIN_DEPTH, stage)

        def lin_scalar(e, ln0):
            D = lin

            def stage(s, i, b, par):
                if s == 1:
                    e.wait_ge(xn_turned, i + (ln0 + 1))
                    e.wait_ge(l_qkv, i)
                    nc.scalar.activation(D["xT"][:, :], banks[0][:, :], ACT.Copy).then_inc(xT_ready, 1)
                elif s == 2:
                    e.wait_ge(l_biased, i + 1)
                    e.wait_ge(l_ss, i * 2)
                    nc.scalar.activation(D["sq"][:, :, :], D["qkv"][:, par, :, 0:2 * C], ACT.Square).then_inc(l_sq, 1)
                elif s == 3:
                    e.wait_ge(l_ss, i * 2 + 2)
                    nc.scalar.activation(D["rn"][:, :, :], D["ss"][:, :, :], ACT.Sqrt).then_inc(l_rn, 1)
                elif s == 4:
                    e.wait_ge(l_qt, i + 1)
                    e.wait_ge(l_out, b * 2)
                    nc.scalar.activation(D["qT"][:, par, :], LIN_TURN[:, :], ACT.Copy).then_inc(l_qT, 1)
                    if par == 1:
                        e.wait_ge(l_m, b + 1)
                        nc.scalar.activation(D["m"][:, :], LIN_KV[:, C:2 * C], ACT.Copy).then_inc(l_mb, 1)
            nc.scalar.preload_act_table(ACT.Sqrt)
            pipeline(e.Fori, LIN_DEPTH, stage)

        def lin_tensor(e, ln0):
            D = lin

            def stage(s, i, b, par):
                if s == 1:
                    e.wait_ge(xT_ready, i + ln0)
                    ln_tensor(e, i + ln0, banks[0])
                    e.wait_ge(xT_ready, i + (ln0 + 1))
                    e.wait_ge(l_biased, i)
                    for k in range(SUP):
                        last = nc.tensor.matmul(banks[1 + k][:, 0:3 * C], D["xT"][:, k * P:(k + 1) * P], D["qkv_w"][:, :],
                                                start=True, stop=True)
                    last.then_inc(l_qkv, 1)
                elif s == 3:
                    e.wait_ge(l_unit, i + 1)
                    e.wait_ge(l_qT, i)
                    for k in range(SUP):
                        last = nc.tensor.transpose(LIN_TURN[:, k * P:(k + 1) * P], D["qkv"][:, par, k, 0:C], ident[:, :])
                    last.then_inc(l_qt, 1)
                    if par == 0:
                        e.wait_ge(l_mb, b)
                    for k in range(SUP):
                        last = nc.tensor.matmul(LIN_KV[:, 0:C], D["qkv"][:, par, k, 2 * C:3 * C], D["qkv"][:, par, k, C:2 * C],
                                                start=(par == 0 and k == 0), stop=(par == 1 and k == SUP - 1))
                    if par == 1:
                        last.then_inc(l_kv, 1)
                elif s == 4 and par == 1:
                    e.wait_ge(l_kvm, b + 1)
                    nc.tensor.matmul(LIN_KV[:, C:2 * C], D["kvm"][:, :], D["proj_w"][:, :], start=True, stop=True).then_inc(l_m, 1)
                elif s == 5 and par == 1:
                    e.wait_ge(l_mb, b + 1)
                    e.wait_ge(l_qT, i + 1)
                    for half in range(2):
                        e.wait_ge(l_add, b * 2 + half)
                        for k in range(SUP):
                            last = nc.tensor.matmul(LIN_OUT[:, k * C:(k + 1) * C], D["qT"][:, half, k * P:(k + 1) * P],
                                                    D["m"][:, :], start=True, stop=True)
                        last.then_inc(l_out, 1)
            pipeline(e.Fori, LIN_DEPTH, stage)

        POWER_BANKS = [banks[7], banks[0], banks[1], banks[2]]
        POWERS_L = [1, 2, 4, 8, 16, 32, 64, 128, 256, 512]
        POWERS_R = [1, 2, 3, 4, 5, 6, 7, 8, 16, 32, 64, 128, 256]
        LI = {k: n for n, k in enumerate(POWERS_L)}
        RI = {k: n for n, k in enumerate(POWERS_R)}
        RECIPES = [("L", 2, 1, 1), ("R", 2, 1, 1), ("R", 3, 1, 2), ("L", 4, 2, 2), ("R", 4, 2, 2), ("R", 5, 1, 4), ("R", 6, 2, 4),
                   ("R", 7, 4, 3), ("L", 8, 4, 4), ("R", 8, 4, 4)]
        for k in (16, 32, 64, 128, 256):
            RECIPES += [("L", k, k // 2, k // 2), ("R", k, k // 2, k // 2)]
        RECIPES.append(("L", 512, 256, 256))
        RECIPES += [("G", k, k, 0) for k in range(1, SPB)]
        PW = banks[5:7]
        RNN_DEPTH = 3
        TURNS = NSUP + RNN_DEPTH
        HALVES = 21

        def spectral_vector(e, stage):
            D = rnn
            nc.vector.memset(D["u"][:, :], P ** -0.5).then_inc(p_vec, 1)
            nc.vector.memset(D["ones"][:, :], 1.0).then_inc(p_vec, 1)

            def half(n, dst):
                e.wait_ge(p_raw, n + 1)
                nc.vector.tensor_copy(D["raw"][:, :], PW[0][:, 0:3]).then_inc(p_vec, 1)
                e.wait_ge(p_norm, n + 1)
                for step, ins in enumerate((
                        lambda: nc.vector.tensor_scalar(D["norm1"][:, :], D["norm"][:, :], 1e-12, None, ALU.add),
                        lambda: nc.vector.reciprocal(D["inv"][:, :], D["norm1"][:, :]),
                        lambda: nc.vector.tensor_tensor(dst, D["raw"][:, :], D["inv"][:, :], ALU.mult))):
                    if step:
                        e.wait_ge(p_vec, n * 4 + (3 + step))
                    ins().then_inc(p_vec, 1)

            def beside(n):
                half(n * 2, D["v"][:, :])
                if not (isinstance(n, int) and n == TURNS - 1):
                    half(n * 2 + 1, D["u"][:, :])

            pipeline(e.Fori, RNN_DEPTH, stage, beside)
            e.wait_ge(p_raw, HALVES + 1)
            nc.vector.tensor_tensor(D["sq"][:, :], PW[0][:, 0:3], D["u"][:, :], ALU.mult).then_inc(p_sq, 1)
            e.wait_ge(p_sum, HALVES + 1)
            nc.vector.reciprocal(D["isig"][:, :], PW[1][:, 0:3]).then_inc(p_sigma, 1)
            e.wait_ge(p_sigma, 1)
            nc.vector.tensor_tensor(D["isig"][:, 2:3], D["isig"][:, 2:3], D["isig"][:, 1:2], ALU.mult).then_inc(p_sigma, 1)
            e.wait_ge(p_sigma, 2)
            nc.vector.tensor_scalar(D["R"][:, 0, :], D["w"][:, 0, :], D["isig"][:, 0:1], None, ALU.mult)
            nc.vector.tensor_scalar(D["L"][:, 0, :], D["wT"][:, 0, :], D["isig"][:, 0:1], None, ALU.mult)
            nc.vector.tensor_scalar(D["CT"][:, :], D["wT"][:, 2, :], D["isig"][:, 2:3], None, ALU.mult).then_inc(p_scaled, 1)

        def spectral_scalar(e, stage):
            D = rnn
            e.wait_ge(p_turned, 1)
            nc.scalar.activation(D["wT"][:, :, :], banks[2][:, 0:3 * P].rearrange("p (m c) -> p m c", m=3), ACT.Copy).then_inc(p_wT, 1)

            def half(n):
                e.wait_ge(p_vec, n * 4 + 3)
                nc.scalar.activation(D["sq"][:, :], D["raw"][:, :], ACT.Square).then_inc(p_sq, 1)
                e.wait_ge(p_sum, n + 1)
                nc.scalar.activation(D["norm"][:, :], PW[1][:, 0:3], ACT.Sqrt).then_inc(p_norm, 1)

            def beside(n):
                half(n * 2)
                if not (isinstance(n, int) and n == TURNS - 1):
                    half(n * 2 + 1)

            nc.scalar.preload_act_table(ACT.Sqrt)
            pipeline(e.Fori, RNN_DEPTH, stage, beside)

        def spectral_tensor(e, stage):
            D = rnn
            for k in range(3):
                last = nc.tensor.transpose(banks[2][:, k * P:(k + 1) * P], D["w"][:, k, :], ident[:, :])
            last.then_inc(p_turned, 1)
            e.wait_ge(p_wT, 1)

            def half(n, w, x):
                e.wait_ge(p_vec, n * 4 + 2)
                for k in range(3):
                    last = nc.tensor.matmul(PW[0][:, k:k + 1], D[w][:, k, :], D[x][:, k:k + 1], start=True, stop=True)
                last.then_inc(p_raw, 1)
                e.wait_ge(p_sq, n + 1)
                nc.tensor.matmul(PW[1][:, 0:3], D["ones"][:, :], D["sq"][:, :], start=True, stop=True).then_inc(p_sum, 1)

            def beside(n):
                half(n * 2, "w", "u")
                half(n * 2 + 1, "wT", "v")

            pipeline(e.Fori, RNN_DEPTH, stage, beside)

        def rnn_vector(e, ln0):
            D = rnn

            def stage(s, i, b, par):
                if s == 0:
                    ln_vector_stats(e, i + ln0, i)
                elif s == 1:
                    ln_vector_norm(e, i + ln0, i)
            spectral_vector(e, stage)
            e.wait_ge(r_u, NSUP)
            U = D["U"]
            nc.vector.memset(D["carry"][:, :, 0:1], 0.0)
            for s in range(1, SPB):
                e.wait_ge(r_step, s)
                nc.vector.tensor_tensor(U[:, :, s, :], U[:, :, s, :], banks[3][:, :].rearrange("p (b j) -> p b j", b=NB),
                                        ALU.add).then_inc(r_stepped, 1)
            e.wait_ge(r_stepped, SPB - 1)
            nc.vector.tensor_copy(D["carry"][:, :, 1:P + 1], U[:, :, SPB - 1, :]).then_inc(r_carried, 1)
            for n in range(7):
                d = 1 << n
                e.wait_ge(r_jump, n + 1)
                if n:
                    e.wait_ge(r_carried, n + 1)
                nc.vector.tensor_tensor(D["carry"][:, :, 1 + d:P + 1], D["carry"][:, :, 1 + d:P + 1],
                                        banks[3 + n % 2][:, 0:NB * (P - d)].rearrange("p (b j) -> p b j", b=NB),
                                        ALU.add).then_inc(r_carried, 1)
            for i in range(NSUP):
                e.wait_ge(r_out, i + 1)
                at = slice(i * SUP, (i + 1) * SUP)
                nc.vector.tensor_tensor(X[:, at, :], X[:, at, :], banks[5 + i % 2][:, :].rearrange("p (k c) -> p k c", k=SUP),
                                        ALU.add).then_inc(r_add, 1)

        def rnn_pool(e, ln0):
            def stage(s, i, b, par):
                if s == 0:
                    ln_pool(e, i + ln0)
            pipeline(e.Fori, 3, stage)

        def rnn_scalar(e, ln0):
            D = rnn

            def stage(s, i, b, par):
                if s == 1:
                    e.wait_ge(xn_turned, i + (ln0 + 1))
                    e.wait_ge(r_bx, i - 1 if not isinstance(i, int) else max(i - 1, 0))
                    nc.scalar.activation(D["xT"][:, par, :], banks[0][:, :], ACT.Copy).then_inc(xT_ready, 1)
                elif s == 2:
                    e.wait_ge(r_bx, i + 1)
                    nc.scalar.activation(D["U"][:, :, :, :].rearrange("p b s j -> p (b s j)")[:, bass.ds(i * W, W)], banks[1 + par][:, :],
                                         ACT.Copy).then_inc(r_u, 1)
            spectral_scalar(e, stage)
            for n, (kind, k, _, _) in enumerate(RECIPES):
                e.wait_ge(r_pow, n + 1)
                dst = {"L": lambda: D["L"][:, LI[k], :], "R": lambda: D["R"][:, RI[k], :], "G": lambda: D["G"][:, k, :]}[kind]()
                nc.scalar.activation(dst, POWER_BANKS[n % 4][:, 0:P], ACT.Copy).then_inc(r_power, 1)

        def rnn_tensor(e, ln0):
            D = rnn

            def stage(s, i, b, par):
                if s == 1:
                    e.wait_ge(xT_ready, i + ln0)
                    ln_tensor(e, i + ln0, banks[0])
                elif s == 2:
                    e.wait_ge(xT_ready, i + (ln0 + 1))
                    e.wait_ge(r_u, i - 1 if not isinstance(i, int) else max(i - 1, 0))
                    nc.tensor.matmul(banks[1 + par][:, :], D["wT"][:, 1, :], D["xT"][:, par, :], start=True, stop=True).then_inc(r_bx, 1)
            spectral_tensor(e, stage)
            e.wait_ge(p_scaled, 1)
            done = {("L", 1): 0, ("R", 1): 0, ("G", 0): 0}
            n = [0]

            def powers(count):
                for _ in range(count):
                    if n[0] == len(RECIPES):
                        return
                    kind, k, a, b = RECIPES[n[0]]
                    if kind == "G":
                        lhsT, rhs, need = D["R"][:, RI[k], :], D["CT"][:, :], done[("R", k)]
                    else:
                        one, two = (("R", "L") if kind == "L" else ("L", "R"))
                        index = {"L": LI, "R": RI}
                        lhsT, rhs = D[one][:, index[one][a], :], D[two][:, index[two][b], :]
                        need = max(done[(one, a)], done[(two, b)])
                    e.wait_ge(r_power, max(need, n[0] - 3))
                    nc.tensor.matmul(POWER_BANKS[n[0] % 4][:, 0:P], lhsT, rhs, start=True, stop=True).then_inc(r_pow, 1)
                    n[0] += 1
                    done[(kind, k)] = n[0]

            U, carry = D["U"], D["carry"]
            e.wait_ge(r_u, NSUP)
            for s in range(1, SPB):
                e.wait_ge(r_stepped, s - 1)
                nc.tensor.matmul(banks[3][:, :].rearrange("p (b j) -> p b j", b=NB), D["L"][:, 0, :], U[:, :, s - 1, :],
                                 start=True, stop=True).then_inc(r_step, 1)
                powers(4)
            for m_ in range(7):
                d = 1 << m_
                while ("L", SPB * d) not in done:
                    powers(1)
                e.wait_ge(r_power, done[("L", SPB * d)])
                e.wait_ge(r_carried, m_ + 1)
                nc.tensor.matmul(banks[3 + m_ % 2][:, 0:NB * (P - d)].rearrange("p (b j) -> p b j", b=NB), D["L"][:, LI[SPB * d], :],
                                 carry[:, :, 1:P + 1 - d], start=True, stop=True).then_inc(r_jump, 1)
                powers(2)
            powers(len(RECIPES))
            e.wait_ge(r_power, len(RECIPES))
            e.wait_ge(r_carried, 8)
            for i in range(NSUP):
                b, half = divmod(i, 2)
                if i >= 2:
                    e.wait_ge(r_add, i - 1)
                for k in range(SUP):
                    s = half * SUP + k
                    dst = banks[5 + i % 2][:, k * P:(k + 1) * P]
                    if s == SPB - 1:
                        last = nc.tensor.matmul(dst, carry[:, b, 1:P + 1], D["CT"][:, :], start=True, stop=True)
                    else:
                        nc.tensor.matmul(dst, U[:, b, s, :], D["CT"][:, :], start=True, stop=False)
                        last = nc.tensor.matmul(dst, carry[:, b, 0:P], D["G"][:, s + 1, :], start=False, stop=True)
                last.then_inc(r_out, 1)


        YBANK, BBANK, CBANK, PROD = banks[0:2], banks[2:4], banks[4:6], banks[6:8]
        UNITS, RING = 2 * SSM_N, 4
        HALF1 = [("bias", 0, 0, 0), ("h0", 0, 0, 1), ("h1", 0, 0, 1), ("g0", 0, 3, 4), ("g1", 0, 3, 4), ("c0", 0, 5, 6), ("c1", 0, 6, 7),
                 ("silu", 0, 0, 8), ("ts", 0, 9, 10), ("bc", 0, 10, 11), ("split", 12, 0, 0), ("dt0", 0, 11, 12),
                 ("dt1", 0, 12, 13), ("soft", 0, 0, 13), ("delta", 14, 0, 0)]
        HALF0 = [("stats0", -6, 0, 0), ("rms0", -5, 0, 0), ("norm0", -4, -3, -2), ("stats1", -3, 0, 0), ("rms1", -2, 0, 0),
                 ("norm1", -1, 0, 1), ("h0", 0, 2, 3), ("h1", 0, 2, 3), ("g0", 0, 4, 5), ("g1", 0, 4, 5), ("c0", 0, 6, 7),
                 ("c1", 0, 7, 8), ("silu", 0, 0, 9), ("ts", 0, 10, 11), ("bc", 0, 11, 12), ("split", 13, 0, 0),
                 ("dt0", 0, 12, 13), ("dt1", 0, 13, 13), ("soft", 0, 0, 13), ("delta", 14, 0, 0)]
        RESULT_AT = 2
        PRODUCTS = {"norm0": -2, "norm1": -1, "h0": 0, "h1": 1, "g0": 2, "g1": 3, "c0": 4, "c1": 5, "ts": 6, "bc": 7,
                    "dt0": 8, "dt1": 9}

        def ssm_order(fori, lane, prep, far, front, back, finish, result):
            def prepare(half, b, at, what):
                prep(what, b, half, at + PRODUCTS.get(what, 0))

            for piece in HALF0:
                prepare(0, 0, 2, piece[0])
            far(0, 0, 0)
            far(0, 0, 1)
            front(0, 0, 0)

            def body(b, is_first, last):
                for q in range(2 * SSM_N):
                    for ahead, piece in ((2, far), (1, front)) if lane == 2 else ((1, front), (2, far)):
                        if not (last and q + ahead >= 2 * SSM_N):
                            piece(b + (q + ahead) // (2 * SSM_N), (q + ahead) // SSM_N % 2, (q + ahead) % SSM_N)
                    if lane != 2:
                        back(b, q // SSM_N, q % SSM_N)
                    if q == RESULT_AT and not is_first:
                        result(b - 1, False)
                    for piece in HALF1:
                        if piece[lane] == q:
                            prepare(1, b, b * 22 + 12, piece[0])
                    if not last:
                        for piece in HALF0:
                            if piece[lane] + SSM_N == q:
                                prepare(0, b + 1, b * 22 + 24, piece[0])
                    if lane == 2:
                        back(b, q // SSM_N, q % SSM_N)
                    if q == SSM_N - 1:
                        finish(b, 0)
                finish(b, 1)

            body(0, True, False)
            with fori(0, NB - 2) as it:
                body(it + 1, False, False)
            body(NB - 1, False, True)
            result(NB - 1, True)

        def started(b, half):
            return isinstance(b, int) and b == 0 and half == 0

        def ssm_vector(e, ln0):
            D = ssm

            def prep(what, b, half, at):
                c = b * 2 + half
                if what[:-1] == "stats":
                    i = b * 2 + int(what[-1])
                    ln_vector_stats(e, i + ln0, i)
                elif what[:-1] == "rms":
                    i = b * 2 + int(what[-1])
                    e.wait_ge(ln_rstd_done, i + (ln0 + 1))
                    nc.vector.tensor_tensor(D["ms"][:, :], ln_rstd[:, :], ln_rstd[:, :], ALU.mult).then_inc(s_rms, 1)
                    e.wait_ge(s_rms, i * 4 + 1)
                    nc.vector.tensor_tensor(D["ms"][:, :], D["ms"][:, :], ln_mv[:, :, 1], ALU.mult).then_inc(s_rms, 1)
                    e.wait_ge(s_rms, i * 4 + 2)
                    nc.vector.tensor_scalar(D["ms"][:, :], D["ms"][:, :], 1e-6, None, ALU.add).then_inc(s_rms, 1)
                elif what[:-1] == "norm":
                    i = b * 2 + int(what[-1])
                    e.wait_ge(s_rpow, i + 1)
                    nc.vector.tensor_tensor(ln_rstd[:, :], ln_rstd[:, :], D["ms2"][:, :], ALU.mult).then_inc(s_rms, 1)
                    e.wait_ge(s_rms, i * 4 + 4)
                    ln_vector_norm(e, i + ln0, i)
                elif what == "split":
                    if not started(b, half):
                        e.wait_ge(s_bc, (c - 1) * SSM_N)
                    e.wait_ge(s_evac, evac_number(b, half, 7) + 1)
                    bc, v0, r = D["bc"][:, half, :], D["v0"], D["r"]
                    steps = (lambda: nc.vector.tensor_copy(bc[0:96], v0[0:96, :]),
                             lambda: nc.vector.tensor_tensor(r[:, :], v0[:, :], bc[0:96], ALU.subtract),
                             lambda: [nc.vector.tensor_copy(bc[32 * j:32 * (j + 1)], r[32 * j:32 * (j + 1), :]) for j in (1, 2)][-1],
                             lambda: nc.vector.tensor_tensor(bc[64:96], r[64:96, :], bc[64:96], ALU.subtract))
                    for k, ins in enumerate(steps):
                        if k:
                            e.wait_ge(s_split, c * 4 + k)
                        ins().then_inc(s_split, 1)
                elif what == "delta":
                    if not started(b, half):
                        e.wait_ge(s_da, (c - 1) * UNITS + RING)
                        e.wait_ge(s_dbu, (c - 1) * UNITS + RING)
                    delta = D["delta"][:, half, :, :]
                    e.wait_ge(s_soft, c * 8 + 6)
                    nc.vector.scalar_tensor_tensor(D["ez"][:, :, :], D["uz"][:, :, :], 1.0, D["ez"][:, :, :],
                                                   ALU.subtract, ALU.subtract).then_inc(s_delta, 1)
                    e.wait_ge(s_soft, c * 8 + 8)
                    nc.vector.scalar_tensor_tensor(delta, D["zb"][:, :, :], 0.0, D["lz"][:, :, :], ALU.max,
                                                   ALU.add).then_inc(s_delta, 1)
                    e.wait_ge(s_delta, c * 3 + 2)
                    nc.vector.tensor_tensor(delta, delta, D["ez"][:, :, :], ALU.subtract).then_inc(s_delta, 1)
                    e.wait_ge(s_delta, c * 3 + 3)
                    nc.vector.tensor_tensor(D["du"][:, half, :, :], D["delta"][:, half, :, :], D["cv"][:, half, :, :],
                                            ALU.mult).then_inc(s_du, 1)

            def back(b, half, n):
                c = b * 2 + half
                for blk in range(2):
                    u = c * UNITS + (2 * n + blk)
                    ring = (2 * n + blk) % RING
                    e.wait_ge(s_da, u + (RING + 1))
                    e.wait_ge(s_dbu, u + (RING + 1))
                    last = D["last"][:, 2 * n + blk:2 * n + blk + 1]
                    nc.vector.tensor_tensor_scan(D["st"][:, ring, :], D["da"][:, ring, :], D["dbu"][:, ring, :],
                                                 last if half else 0.0, ALU.mult, ALU.add).then_inc(s_scan, 1)
                for blk in range(2):
                    u = c * UNITS + (2 * n + blk)
                    ring = (2 * n + blk) % RING
                    e.wait_ge(s_scan, u + (RING + 1))
                    if half == 0:
                        nc.vector.tensor_copy(D["last"][:, 2 * n + blk:2 * n + blk + 1], D["st"][:, ring, W - 1:W])
                    if blk == 0:
                        e.wait_ge(s_bc, c * SSM_N + (n + 1))
                    e.wait_ge(s_acc, u + 1)
                    nc.vector.tensor_tensor(D["sc"][:, ring, :], D["st"][:, ring, :], CBANK[n % 2][:, :], ALU.mult).then_inc(s_mult, 1)

            def finish(b, half):
                c = b * 2 + half
                e.wait_ge(s_acc, (c + 1) * UNITS + RING)
                if not first(b):
                    e.wait_ge(s_out, b * 2)
                for blk in range(2):
                    nc.vector.scalar_tensor_tensor(D["y2"][:, blk, :], D["cv"][:, half, blk, :], ssm_D[:, blk:blk + 1],
                                                   YBANK[blk][:, :], ALU.mult, ALU.add).then_inc(s_y, 1)
                e.wait_ge(s_y, c * 2 + 2)
                nc.vector.tensor_tensor(D["yb"][:, :, half * W:(half + 1) * W], D["y2"][:, :, :], D["gs"][:, half, :, :],
                                        ALU.mult).then_inc(s_y3, 1)

            def result(b, last):
                e.wait_ge(s_pb, b + 1)
                for k in range(2):
                    e.wait_ge(s_out, b * 2 + k + 1)
                    at = bass.ds(b * SPB + k * SUP, SUP)
                    nc.vector.tensor_tensor(X[:, at, :], X[:, at, :], PROD[k][:, :].rearrange("p (k c) -> p k c", k=SUP),
                                            ALU.add).then_inc(s_oadd, 1)

            nc.vector.memset(D["hp"][:, 0, :, 0:SSM_K - 1], 0.0)
            nc.vector.reduce_sum(D["sel1"][:, :], ident[0:96, 0:96].rearrange("p (j m) -> p m j", j=3), AX.X).then_inc(s_diag, 1)
            e.wait_ge(s_diag, 1)
            nc.vector.tensor_copy(D["sel"][:, :, :], D["sel1"][:, :, None].to_broadcast([96, 32, P])).then_inc(s_const, 1)
            e.wait_ge(s_const, 6)
            nc.vector.tensor_scalar(D["negA"][:, :, :], D["negA"][:, :, :], -1.0, None, ALU.mult).then_inc(s_const, 1)
            e.wait_ge(s_const, 7)
            ssm_order(e.Fori, 1, prep, nothing, nothing, back, finish, result)

        def evac_number(b, half, k):
            return 2 + k if started(b, half) else (b * 22 + (12 + k) if half else (b - 1) * 22 + (24 + k))

        def ssm_pool(e, ln0):
            D = ssm

            def prep(what, b, half, at):
                i = b * 2 + int(what[-1]) if what[-1] in "01" else None
                if what[:-1] == "stats":
                    ln_pool(e, i + ln0)
                elif what[:-1] == "rms":
                    e.wait_ge(s_rms, i * 4 + 3)
                    nc.gpsimd.tensor_tensor(D["ms2"][:, :], D["ms"][:, :], minus_half[:, 0:SUP], ALU.pow).then_inc(s_rpow, 1)
                elif what == "bias":
                    e.wait_ge(xn_ready, b * 2 + (ln0 + 2))
                    at = bass.ds(b * SPB, SPB)
                    nc.gpsimd.tensor_tensor(X[:, at, :], X[:, at, :], ssm_out_b[:, None, :].to_broadcast([P, SPB, C]),
                                            ALU.add).then_inc(s_pb, 1)

            def front(b, half, n):
                c = b * 2 + half
                if n == 0:
                    e.wait_ge(s_du, c + 1)
                e.wait_ge(s_bs, c * SSM_N + (n + 1))
                for blk in range(2):
                    u = c * UNITS + (2 * n + blk)
                    e.wait_ge(s_scan, u + 1)
                    nc.gpsimd.tensor_tensor(D["dbu"][:, (2 * n + blk) % RING, :], D["du"][:, half, blk, :], D["bs"][:, n % 2, :],
                                            ALU.mult).then_inc(s_dbu, 1)

            for blk in range(2):
                for k in range(SSM_K):
                    last = nc.gpsimd.tensor_scalar(D["diag"][:, blk, k, :], ident[:, :], ssm_conv_w[:, blk, k:k + 1], None, ALU.mult)
            last.then_inc(s_const, 4)
            ssm_order(e.Fori, 1, prep, nothing, front, nothing, nothing, nothing)

        def ssm_scalar(e, ln0):
            D = ssm
            ready = lambda at: e.wait_ge(s_prod, at + 1)

            def prep(what, b, half, at):
                c = b * 2 + half
                if what[:-1] == "norm":
                    u = int(what[-1])
                    i = b * 2 + u
                    e.wait_ge(xn_turned, i + (ln0 + 1))
                    nc.scalar.activation(D["xT"][:, :].rearrange("p (j s) -> p s j", s=SPB)[:, u * SUP:(u + 1) * SUP, :],
                                         PROD[u][:, :].rearrange("p (s j) -> p s j", s=SUP), ACT.Copy,
                                         scale=ssm_norm[:, :]).then_inc(s_evac, 1)
                elif what[0] == "h":
                    k = int(what[1])
                    if k == 0 and half == 1:
                        e.wait_ge(s_evac, at - 9)
                        nc.scalar.activation(D["hp"][:, 1, :, 0:SSM_K - 1], D["hp"][:, 0, :, W:W + SSM_K - 1], ACT.Copy)
                    ready(at)
                    nc.scalar.activation(D["hp"][:, half, k, SSM_K - 1:], PROD[k][:, :], ACT.Identity,
                                         bias=ssm_in_b[:, k:k + 1]).then_inc(s_evac, 1)
                elif what[0] == "g":
                    k = int(what[1])
                    ready(at)
                    if not started(b, half):
                        e.wait_ge(s_y3, c - 1)
                    nc.scalar.activation(D["gs"][:, half, k, :], PROD[k][:, :], ACT.Identity, bias=ssm_in_b[:, 2 + k:3 + k]).then_inc(s_evac, 1)
                elif what[0] == "c":
                    k = int(what[1])
                    ready(at)
                    nc.scalar.activation(D["cv"][:, half, k, :], PROD[k][:, :], ACT.Identity, bias=ssm_conv_b[:, k:k + 1]).then_inc(s_evac, 1)
                elif what == "silu":
                    e.wait_ge(s_evac, evac_number(b, half, 5) + 1)
                    nc.scalar.activation(D["cv"][:, half, :, :], D["cv"][:, half, :, :], ACT.Silu).then_inc(s_silu, 1)
                    nc.scalar.activation(D["gs"][:, half, :, :], D["gs"][:, half, :, :], ACT.Silu).then_inc(s_silu, 1)
                elif what == "ts":
                    ready(at)
                    nc.scalar.activation(D["ts"][:, :], PROD[0][0:SSM_R, :], ACT.Copy).then_inc(s_evac, 1)
                elif what == "bc":
                    ready(at)
                    e.wait_ge(s_split, c * 4)
                    nc.scalar.activation(D["v0"][:, :], PROD[1][0:96, :], ACT.Copy).then_inc(s_evac, 1)
                elif what[:2] == "dt":
                    k = int(what[2])
                    ready(at)
                    e.wait_ge(s_delta, c * 3)
                    nc.scalar.activation(D["zb"][:, k, :], PROD[k][:, :], ACT.Identity, bias=ssm_dt_b[:, k:k + 1]).then_inc(s_evac, 1)
                elif what == "soft":
                    e.wait_ge(s_evac, evac_number(b, half, 9) + 1)
                    for step, (dst, src, fn, scale, bias) in enumerate((
                            ("ez", "zb", ACT.Abs, 1.0, 0.0), ("ez", "ez", ACT.Exp, -1.0, 0.0),
                            ("uz", "ez", ACT.Identity, 1.0, 1.0), ("lz", "uz", ACT.Ln, 1.0, 0.0))):
                        for k in range(2):
                            if step:
                                e.wait_ge(s_soft, c * 8 + (2 * step - 1 + k))
                            nc.scalar.activation(D[dst][:, k, :], D[src][:, k, :], fn, scale=scale, bias=bias).then_inc(s_soft, 1)

            def far(b, half, n):
                c = b * 2 + half
                e.wait_ge(s_bb, c * SSM_N + (n + 1))
                e.wait_ge(s_dbu, c * UNITS + (2 * n + RING - 2))
                nc.scalar.activation(D["bs"][:, n % 2, :], BBANK[n % 2][:, :], ACT.Copy).then_inc(s_bs, 1)

            def front(b, half, n):
                c = b * 2 + half
                if n == 0:
                    e.wait_ge(s_delta, c * 3 + 3)
                for blk in range(2):
                    u = c * UNITS + (2 * n + blk)
                    e.wait_ge(s_scan, u + 1)
                    nc.scalar.activation(D["da"][:, (2 * n + blk) % RING, :], D["delta"][:, half, blk, :], ACT.Exp,
                                         scale=D["negA"][:, blk, n:n + 1]).then_inc(s_da, 1)

            nc.scalar.preload_act_table(ACT.Ln)
            nc.scalar.activation(D["negA"][:, :, :], ssm_A_log[:, :, :], ACT.Exp).then_inc(s_const, 1)
            e.wait_ge(s_const, 7)
            ssm_order(e.Fori, 3, prep, far, front, nothing, nothing, nothing)
            e.sem_inc(xT_ready, NSUP)

        def ssm_tensor(e, ln0):
            D = ssm

            def free(b, half, k):
                e.wait_ge(s_evac, evac_number(b, half, k) - 1)
                if half == 1 and k in (2, 3) and not first(b):
                    e.wait_ge(s_oadd, b * 2)

            def prep(what, b, half, at):
                c = b * 2 + half
                k = PRODUCTS.get(what)
                if k is None:
                    return
                if k < 0:
                    u = int(what[-1])
                    if not started(b, half):
                        e.wait_ge(s_evac, (b - 1) * 22 + (22 + u) - 1)
                    ln_tensor_to(e, b * 2 + u + ln0, PROD[u])
                    return
                free(b, half, k)
                xT = D["xT"][:, half * W:(half + 1) * W]
                if what[0] in "hg":
                    blk = int(what[1])
                    at_w = blk + (2 if what[0] == "g" else 0)
                    if what == "h0":
                        e.wait_ge(s_evac, evac_number(b, half, 0))
                    last = nc.tensor.matmul(PROD[blk][:, :], ssm_in_w[:, at_w * P:(at_w + 1) * P], xT, start=True, stop=True)
                elif what[0] == "c":
                    blk = int(what[1])
                    e.wait_ge(s_evac, evac_number(b, half, 1) + 1)
                    for tap in range(SSM_K):
                        last = nc.tensor.matmul(PROD[blk][:, :], D["diag"][:, blk, tap, :], D["hp"][:, half, blk, tap:tap + W],
                                                start=(tap == 0), stop=(tap == SSM_K - 1))
                elif what == "ts":
                    e.wait_ge(s_silu, c * 2 + 1)
                    for blk in range(2):
                        last = nc.tensor.matmul(PROD[0][0:SSM_R, :], ssm_xproj[:, blk, 0:SSM_R], D["cv"][:, half, blk, :],
                                                start=(blk == 0), stop=(blk == 1))
                elif what == "bc":
                    for blk in range(2):
                        last = nc.tensor.matmul(PROD[1][0:96, :], ssm_xbc[:, blk, :], D["cv"][:, half, blk, :],
                                                start=(blk == 0), stop=(blk == 1))
                else:
                    blk = int(what[2])
                    e.wait_ge(s_evac, evac_number(b, half, 6) + 1)
                    last = nc.tensor.matmul(PROD[blk][:, :], ssm_dt_w[:, blk * P:(blk + 1) * P], D["ts"][:, :], start=True, stop=True)
                last.then_inc(s_prod, 1)

            def ln_tensor_to(e, n, bank):
                e.wait_ge(xn_ready, n + 1)
                for k in range(SUP):
                    last = nc.tensor.transpose(bank[:, k * P:(k + 1) * P], xn[:, k, :], ident[:, :])
                last.then_inc(xn_turned, 1)
                e.sem_inc(s_prod, 1)

            def far(b, half, n):
                c = b * 2 + half
                if n == 0:
                    e.wait_ge(s_split, c * 4 + 4)
                e.wait_ge(s_bs, c * SSM_N + n - 1 if not (started(b, half) and n < 1) else 0)
                nc.tensor.matmul(BBANK[n % 2][:, :], D["sel"][:, n, :], D["bc"][:, half, :], start=True, stop=True).then_inc(s_bb, 1)

            def front(b, half, n):
                c = b * 2 + half
                e.wait_ge(s_mult, c * UNITS + 2 * n - 2 if not (started(b, half) and n < 1) else 0)
                nc.tensor.matmul(CBANK[n % 2][:, :], D["sel"][:, SSM_N + n, :], D["bc"][:, half, :], start=True, stop=True).then_inc(s_bc, 1)

            def back(b, half, n):
                c = b * 2 + half
                if n == 0:
                    e.wait_ge(s_y, c * 2)
                for blk in range(2):
                    u = c * UNITS + (2 * n + blk)
                    e.wait_ge(s_mult, u + 1)
                    nc.tensor.matmul(YBANK[blk][:, :], ident[:, :], D["sc"][:, (2 * n + blk) % RING, :], start=(n == 0),
                                     stop=(n == SSM_N - 1)).then_inc(s_acc, 1)

            def result(b, last):
                e.wait_ge(s_y3, b * 2 + 2)
                e.wait_ge(s_evac, b * 22 + (22 if last else 36))
                for k in range(2):
                    for t in range(SUP):
                        s = k * SUP + t
                        for blk in range(2):
                            ins = nc.tensor.matmul(PROD[k][:, t * C:(t + 1) * C],
                                                   D["yb"][:, blk, :].rearrange("p (j s) -> p s j", s=SPB)[:, s, :],
                                                   ssm_out_w[:, blk, :], start=(blk == 0), stop=(blk == 1))
                    ins.then_inc(s_out, 1)

            e.wait_ge(s_const, 7)
            ssm_order(e.Fori, 2, prep, far, front, back, nothing, result)

        TB, EB, SB, OB = banks[0], banks[1:3], banks[3:7], banks[7]
        POSTS = 8
        SCALE = float(MQK) ** -0.5

        def ml_order(fori, pre, weights, mid, scores, back, post):
            for k in range(4):
                pre(0, 0, k)
            weights(0, 0, 0)
            scores(0, 0, 0)

            def body(c, par, is_first, is_last):
                for b in range(NB):
                    ahead = (c, par, b + 1) if b + 1 < NB else (c + 1, 1 - par, 0)
                    any_ahead = b + 1 < NB or not is_last
                    if any_ahead:
                        weights(*ahead)
                    mid(c, par, b)
                    if any_ahead:
                        scores(*ahead)
                    if not is_last and b < NB - 1:
                        pre(c + 1, 1 - par, (0, 2, 3)[b])
                    back(c, par, b)
                    if not is_last and b == 0:
                        pre(c + 1, 1 - par, 1)
                    if not is_first:
                        post(c - 1, 1 - par, b)

            body(0, 0, True, False)
            with fori(0, CHUNKS // 2 - 1) as it:
                body(it * 2 + 1, 1, False, False)
                body(it * 2 + 2, 0, False, False)
            body(CHUNKS - 1, 1, False, True)
            for k in range(4):
                post(CHUNKS - 1, 1, k)

        def ml_vector(e, ln0):
            D = ml
            for n, v in (("if_pad", 0.0), ("qk_pad", 0.0), ("kw", 0.0), ("S", 0.0), ("brows", 0.0), ("ones", 1.0), ("v1", 0.0),
                         ("restart", 1.0), ("mprev", FAR)):
                ap = D[n][tuple([slice(None)] * len(D[n].shape))]
                last = nc.vector.memset(ap, v)
            last.then_inc(g_const, 1)
            e.wait_ge(g_const, 1)
            nc.vector.memset(D["restart"][:, :].rearrange("p (c t) -> p c t", t=P)[:, :, 0:1], 0.0)
            nc.vector.memset(D["v1"][:, :, :, MV:MV1], 1.0)
            for k in range(2):
                nc.vector.tensor_copy(D["qk_pad"][:, k, :, :].rearrange("p g (h d) -> p (g h) d", d=32)[:, :, 0:MQK],
                                      ml_qk_w[:, k, :].rearrange("p (h d) -> p h d", d=MQK))
                nc.vector.tensor_copy(D["if_pad"][:, k, 0:3 * MH].rearrange("p (r h) -> p r h", h=MH),
                                      ml_if_w[:, k, None, :].to_broadcast([P, 3, MH]))
            nc.vector.tensor_copy(
                D["brows"][:, :].rearrange("p (b r h) -> p b r h", b=NB, h=MH)[:, :, 0:3, :],
                ml_if_b[:, None, None, :].to_broadcast([2, NB, 3, MH])).then_inc(g_const, 1)
            q4 = ident[:, :].rearrange("p (b r h) -> p h b r", b=NB, h=MH)
            nc.vector.reduce_sum(D["later"][:, 0:1], ident[:, :].rearrange("p (b x) -> p b x", b=NB)[:, :, MH:32], AX.XY)
            nc.vector.reduce_sum(D["later"][:, 1:2], ident[:, :].rearrange("p (b x) -> p b x", b=NB)[:, :, 2 * MH:32], AX.XY)
            nc.vector.reduce_sum(D["indf"][:, :], q4[:, :, :, 0:3], AX.XY)
            nc.vector.reduce_sum(D["head"][:, :], q4[:, :, :, 0], AX.X)
            nc.vector.reduce_sum(D["blocks"][:, :], ident[:, :].rearrange("p (h d) -> p h d", d=32), AX.X).then_inc(g_const, 1)
            e.wait_ge(g_const, 3)
            nc.vector.tensor_scalar(D["later"][:, :], D["later"][:, :], -1.0, None, ALU.mult)
            nc.vector.tensor_copy(D["ind"][:, :].rearrange("p (h g) -> p g h", g=2), D["indf"][:, :].rearrange("p (g h) -> p g h", g=2))
            nc.vector.tensor_copy(D["heads"][:, :, :].rearrange("p g (h d) -> p (g h) d", d=32),
                                  D["head"][:, :, None].to_broadcast([P, MH, 32])).then_inc(g_ind, 1)
            e.wait_ge(g_bias, 1)
            nc.vector.tensor_scalar(D["bcols"][:, :], banks[7][:, 0:2], 1.0 / GATE_CAP, None, ALU.mult).then_inc(g_bias, 1)

            def stage(s, i, b, par):
                if s == 0:
                    ln_vector_stats(e, i + ln0, i)
                elif s == 1:
                    ln_vector_norm(e, i + ln0, i)
            pipeline(e.Fori, 3, stage)

            r = {n: D[n][:, :] for n in ("i", "f", "e", "u", "l", "m", "part", "a3", "b3")}
            r["a"], r["b"], r["L"] = r["l"], r["u"], r["u"]
            chunks = lambda ap: ap.rearrange("p (c t) -> p c t", t=P)
            V = nc.vector

            e.wait_ge(g_rows, 4)
            V.tensor_scalar(r["f"], r["f"], GATE_CAP, None, ALU.mult).then_inc(g_rows, 1)
            e.wait_ge(g_rows, 5)
            V.tensor_scalar(r["i"], r["i"], GATE_CAP, None, ALU.mult).then_inc(g_rows, 1)
            e.wait_ge(g_rows, 10)
            V.scalar_tensor_tensor(r["e"], r["u"], 1.0, r["e"], ALU.subtract, ALU.subtract).then_inc(g_rows, 1)
            e.wait_ge(g_rows, 11)
            V.scalar_tensor_tensor(r["l"], r["f"], 0.0, r["l"], ALU.min, ALU.subtract).then_inc(g_rows, 1)
            e.wait_ge(g_rows, 12)
            V.tensor_tensor(r["l"], r["l"], r["e"], ALU.add).then_inc(g_rows, 1)
            e.wait_ge(g_rows, 13)
            V.tensor_tensor_scan(r["L"], D["restart"][:, :], r["l"], 0.0, ALU.mult, ALU.add).then_inc(g_rows, 1)
            e.wait_ge(g_rows, 14)
            V.tensor_tensor_scan(r["m"], r["l"], r["i"], FAR, ALU.add, ALU.max).then_inc(g_rows, 1)
            e.wait_ge(g_rows, 15)
            V.tensor_copy(D["mprev"][:, 1:], chunks(r["m"])[:, 0:CHUNKS - 1, P - 1])
            V.tensor_tensor(r["a"], r["i"], r["L"], ALU.subtract)
            V.tensor_tensor(r["b"], r["L"], r["m"], ALU.subtract).then_inc(g_rows, 1)
            e.wait_ge(g_rows, 16)
            V.tensor_tensor(chunks(r["i"]), chunks(r["a"]), chunks(r["b"])[:, :, P - 1:P].to_broadcast([P, CHUNKS, P]), ALU.add)
            V.tensor_tensor(chunks(r["f"]), chunks(r["b"]), D["mprev"][:, :, None].to_broadcast([P, CHUNKS, P]),
                            ALU.add).then_inc(g_rows, 1)
            e.wait_ge(g_rows, 20)
            at = 20
            for x, parts in (("a", "a3"), ("b", "b3")):
                for k in range(2):
                    V.tensor_copy(r["part"], r[x]).then_inc(g_rows, 1)
                    at += 1
                    e.wait_ge(g_rows, at)
                    V.scalar_tensor_tensor(r[parts] if k else r[x], r["part"], D["later"][:, k:k + 1], r[x], ALU.mult,
                                           ALU.add).then_inc(g_rows, 1)
                    at += 1
                    e.wait_ge(g_rows, at)
            for n, dst in enumerate(("WT", "RT", "eT")):
                for half in range(2):
                    e.wait_ge(g_turn, 2 * n + half + 1)
                    last = V.tensor_scalar(D[dst][:, half * 4 * NB * MH:(half + 1) * 4 * NB * MH].rearrange("p (c b h) -> p c b h", c=4, b=NB),
                                         banks[2 * n + half][:, :].rearrange("p (c b x) -> p c b x", c=4, b=NB)[:, :, :, 0:MH],
                                         1e-6 if dst == "eT" else 0.0, None, ALU.add)
            e.wait_ge(g_turn, 6 + 2 * NB)
            V.tensor_copy(D["decay"][:, :].rearrange("p (c x) -> p x c", c=CHUNKS),
                          banks[6][:, 0:2 * NB * CHUNKS].rearrange("p (x c) -> p x c", c=CHUNKS)).then_inc(g_const, 1)
            e.wait_ge(g_const, 4)

            def pre(c, par, k):
                if k == 0:
                    if not first(c):
                        e.wait_ge(g_e, c * NB - NB)
                        e.wait_ge(g_vk, c * NB - NB)
                    V.tensor_copy(D["ac"][:, par, :], D["a3"][:, bass.ds(c * P, P)])
                    V.tensor_copy(D["xc"][:, par, :].rearrange("p (b t) -> p b t", b=NB),
                                  D["xT"][:, :].rearrange("p (b t) -> p b t", b=NB)[:, :, bass.ds(c * P, P)]).then_inc(g_xc, 1)

            def mid(c, par, b):
                u, k, n = c * NB + b, b % 2, MH * MV1
                e.wait_ge(g_oT, u + 1)
                V.tensor_tensor(D["um"][:, k, :].rearrange("p (g h d) -> p g h d", g=2, h=4),
                                SB[1][:, 2 * P:2 * P + n].rearrange("p (g h d) -> p g h d", g=2, h=4),
                                D["blocks"][:, None, :, None].to_broadcast([P, 2, 4, MV1]), ALU.mult).then_inc(g_um, 1)

            def scores(c, par, b):
                u, k = c * NB + b, b % 2
                e.wait_ge(g_D, u + 1)
                e.wait_ge(g_s, u + 1)
                e.wait_ge(g_o, u + 1)
                for r in range(4):
                    C_ = D["D"][:, k, r * 2 * P:(r + 1) * 2 * P]
                    last = V.tensor_tensor(C_, C_, SB[r][:, 0:2 * P], ALU.mult)
                last.then_inc(g_c, 1)

            def back(c, par, b):
                u, k, n = c * NB + b, b % 2, MH * MV1
                bank = OB
                e.wait_ge(g_o, u + (CREDIT + 1))
                V.tensor_tensor(D["t1"][:, k, :].rearrange("p (h d) -> p h d", h=MH),
                                bank[:, 2 * P:2 * P + n].rearrange("p (h d) -> p h d", h=MH),
                                D["RT"][:, bass.ds(c * (NB * MH) + b * MH, MH), None].to_broadcast([P, MH, MV1]),
                                ALU.mult).then_inc(g_t, 1)
                e.wait_ge(g_t, u + 1)
                V.tensor_tensor(D["T"][:, par, b, :, :], D["t1"][:, k, :].rearrange("p (h d) -> p h d", h=MH),
                                bank[:, 0:2 * P].rearrange("p (h d) -> p h d", h=MH)[:, :, 0:MV1], ALU.add).then_inc(g_T, 1)
                e.wait_ge(g_um, u + 1)
                e.wait_ge(g_state, u + 1)
                for g in range(2):
                    last = V.scalar_tensor_tensor(D["S"][:, b, g, :], D["S"][:, b, g, :],
                                                  D["decay"][:, bass.ds(c * (2 * NB) + (g * NB + b), 1)],
                                                  D["um"][:, k, g * 4 * MV1:(g + 1) * 4 * MV1], ALU.mult, ALU.add)
                last.then_inc(g_state, 1)

            def post(c, par, piece):
                T = D["T"][:, par, :, :, :]
                of_h = [P, NB, MH, MV]
                n, h, mu, hc = D["n"][:, :, :], D["h"][:, :, :, :], D["mu"][:, :, :], D["hc"][:, :, :, :]

                def steps(at, *todo):
                    for k, ins in enumerate(todo):
                        if k:
                            e.wait_ge(g_post, c * POSTS + (at + k))
                        ins().then_inc(g_post, 1)

                if piece == 0:
                    e.wait_ge(g_T, c * NB + (NB + CREDIT))
                    e.wait_ge(g_y, c)
                    steps(0, lambda: V.scalar_tensor_tensor(n, T[:, :, :, MV], -1.0, T[:, :, :, MV], ALU.mult, ALU.max),
                          lambda: V.scalar_tensor_tensor(n, n, 1e-6,
                                                         D["eT"][:, bass.ds(c * (NB * MH), NB * MH)].rearrange("p (b h) -> p b h", h=MH),
                                                         ALU.add, ALU.max),
                          lambda: V.reciprocal(n, n),
                          lambda: V.tensor_tensor(h, T[:, :, :, 0:MV], D["n"][:, :, :, None].to_broadcast(of_h), ALU.mult),
                          lambda: V.reduce_sum(mu, h, AX.X),
                          lambda: V.scalar_tensor_tensor(hc, D["mu"][:, :, :, None].to_broadcast(of_h), -1.0 / MV, h, ALU.mult,
                                                         ALU.add))
                elif piece == 1:
                    e.wait_ge(g_sq, c + 1)
                    steps(6, lambda: V.reduce_sum(mu, D["sq"][:, :, :, :], AX.X),
                          lambda: V.tensor_scalar(D["var"][:, :, :], mu, 1.0 / MV, 1e-6, ALU.mult, ALU.add))
                elif piece == 2:
                    e.wait_ge(g_pow, c + 1)
                    if not first(c):
                        e.wait_ge(g_b0, y_fill(c - 1) + 1)
                    V.tensor_tensor(D["y"][:, :, :].rearrange("p b (h d) -> p b h d", d=MV), D["hw"][:, :, :, :],
                                    D["rstd"][:, :, :, None].to_broadcast(of_h), ALU.mult).then_inc(g_y, 1)
                elif piece == 3:
                    e.wait_ge(g_b0, y_fill(c) + 1)
                    of_c = lambda n: D[n][:, :].rearrange("p (b t) -> p b t", b=NB)[:, :, bass.ds(c * P, P)]
                    V.tensor_tensor(of_c("xT"), TB[:, :].rearrange("p (b t) -> p b t", b=NB), of_c("gate"),
                                    ALU.mult).then_inc(g_b0used, 1)

            ml_order(e.Fori, pre, nothing, mid, scores, back, post)
            for i in range(NSUP):
                e.wait_ge(g_down, i + 1)
                at = slice(i * SUP, (i + 1) * SUP)
                V.tensor_tensor(X[:, at, :], X[:, at, :], banks[2 + i % 2][:, :].rearrange("p (k c) -> p k c", k=SUP),
                                ALU.add).then_inc(g_add, 1)

        def pre_fill(c, k):
            return c * 4 + k if isinstance(c, int) and c < 2 else c * 5 + (k - 2)

        def y_fill(c):
            return 38 + c - 6 if isinstance(c, int) and c > 5 else c * 5 + 12

        def fills_before(c, b):
            if isinstance(c, int) and c < 2:
                return [4, 4, 6, 7][b] if c == 0 else 8
            if isinstance(c, int):
                return pre_fill(c + 1, 0)
            return c * 5 + 2 if b == 0 else c * 5 + 3 + [0, 2, 3][b - 1]

        def ml_pool(e, ln0):
            D = ml
            nc.gpsimd.memset(D["causal"][:, :], 0.0).then_inc(g_pconst, 1)
            e.wait_ge(g_pconst, 1)
            nc.gpsimd.affine_select(out=D["causal"][:, :], in_=D["causal"][:, :], compare_op=ALU.is_ge, fill=FAR,
                                    base=0, pattern=[[1, P]], channel_multiplier=-1).then_inc(g_pconst, 1)

            def stage(s, i, b, par):
                if s == 0:
                    ln_pool(e, i + ln0)
            pipeline(e.Fori, 3, stage)
            e.wait_ge(g_rows, 28)
            e.wait_ge(g_const, 4)

            def pre(c, par, k):
                if k == 0:
                    if not first(c):
                        e.wait_ge(g_e, c * NB - NB)
                    nc.gpsimd.tensor_tensor(D["bm"][:, par, :, :],
                                            D["b3"][:, None, bass.ds(c * P, P)].to_broadcast([P, MH, P]),
                                            D["ind"][:, :, None].to_broadcast([P, MH, P]), ALU.mult).then_inc(g_bm, 1)

            def weights(c, par, b):
                u, k = c * NB + b, b % 2
                e.wait_ge(g_vkused, u + 1)
                e.wait_ge(g_o, u + 1)
                nc.gpsimd.tensor_tensor(D["kw"][:, k, :, 0:MQK], D["k"][:, k, :].rearrange("p (h d) -> p h d", d=MQK),
                                        D["WT"][:, bass.ds(c * (NB * MH) + b * MH, MH), None].to_broadcast([P, MH, MQK]),
                                        ALU.mult).then_inc(g_kw, 1)

            def post(c, par, piece):
                if piece == 1:
                    e.wait_ge(g_y, c)
                    e.wait_ge(g_post, c * POSTS + (6 ))
                    nc.gpsimd.tensor_tensor(D["hw"][:, :, :, :], D["hc"][:, :, :, :],
                                            ml_norm_w[:, None, :].to_broadcast([P, NB, C]).rearrange("p b (h d) -> p b h d", d=MV),
                                            ALU.mult)
                    e.wait_ge(g_post, c * POSTS + (8 ))
                    nc.gpsimd.tensor_tensor(D["rstd"][:, :, :], D["var"][:, :, :],
                                            minus_half[:, 0:NB * MH].rearrange("p (b h) -> p b h", h=MH), ALU.pow).then_inc(g_pow, 1)

            ml_order(e.Fori, pre, weights, nothing, nothing, nothing, post)

        def ml_scalar(e, ln0):
            D = ml

            def stage(s, i, b, par):
                if s == 1:
                    e.wait_ge(xn_turned, i + (ln0 + 1))
                    xT = D["xT"][:, bass.ds(b * NT, NT)].rearrange("p (j s) -> p s j", s=SPB)[:, par * SUP:(par + 1) * SUP, :]
                    nc.scalar.activation(xT, banks[4][:, :].rearrange("p (s j) -> p s j", s=SUP), ACT.Copy).then_inc(xT_ready, 1)
                elif s == 2:
                    e.wait_ge(g_open, i + 1)
                    gate = D["gate"][:, bass.ds(b * NT, NT)].rearrange("p (j s) -> p s j", s=SPB)[:, par * SUP:(par + 1) * SUP, :]
                    nc.scalar.activation(gate, banks[5 + par][:, :].rearrange("p (s j) -> p s j", s=SUP), ACT.Sigmoid).then_inc(g_opened, 1)
            nc.scalar.preload_act_table(ACT.Sigmoid)
            pipeline(e.Fori, 3, stage)
            e.wait_ge(g_bias, 2)
            n = 0
            for k, name in ((1, "f"), (0, "i")):
                for half in range(2):
                    n += 1
                    e.wait_ge(g_gate, n)
                    nc.scalar.activation(D[name][:, half * W:(half + 1) * W], banks[n - 1][:, :], ACT.Tanh, scale=1.0 / GATE_CAP,
                                         bias=D["bcols"][:, k:k + 1]).then_inc(g_rows, 1)
            for at, dst, src, fn, scale, bias in ((6, "e", "f", ACT.Abs, 1.0, 0.0), (7, "e", "e", ACT.Exp, -1.0, 0.0),
                                                  (8, "u", "e", ACT.Identity, 1.0, 1.0), (9, "l", "u", ACT.Ln, 1.0, 0.0),
                                                  (17, "i", "i", ACT.Exp, 1.0, 0.0), (17, "f", "f", ACT.Exp, 1.0, 0.0),
                                                  (17, "e", "m", ACT.Exp, -1.0, 0.0)):
                e.wait_ge(g_rows, at)
                nc.scalar.activation(D[dst][:, :], D[src][:, :], fn, scale=scale, bias=bias).then_inc(g_rows, 1)

            def pre(c, par, k):
                e.wait_ge(g_b0, pre_fill(c, k) + 1)
                if not first(c):
                    e.wait_ge(g_o, c * NB + (CREDIT - NB))
                dst = D["qT" if k % 2 == 0 else "kT"][:, par, k // 2, :]
                nc.scalar.activation(dst, TB[:, :], ACT.Copy, scale=1.0 if k % 2 == 0 else SCALE).then_inc(g_b0used, 1)

            def weights(c, par, b):
                u, k = c * NB + b, b % 2
                e.wait_ge(g_e, u + 1)
                e.wait_ge(g_o, u + 1)
                for g in range(2):
                    last = nc.scalar.activation(D["D"][:, k, g * W:(g + 1) * W], EB[g][:, :], ACT.Exp)
                last.then_inc(g_D, 1)
                e.wait_ge(g_vk, u + 1)
                nc.scalar.activation(D["v1"][:, k, :, 0:MV], TB[:, 0:C].rearrange("p (h d) -> p h d", d=MV), ACT.Copy)
                nc.scalar.activation(D["k"][:, k, :], TB[:, C:C + MH * MQK], ACT.Copy, scale=SCALE).then_inc(g_vkused, 1)

            def mid(c, par, b):
                u, k = c * NB + b, b % 2
                e.wait_ge(g_oT, u + 1)
                e.wait_ge(g_o, u + 1)
                nc.scalar.activation(D["oT"][:, k, :], SB[0][:, 2 * P:4 * P], ACT.Copy).then_inc(g_oTused, 1)

            def post(c, par, piece):
                if piece == 0:
                    e.wait_ge(g_post, c * POSTS + (6 ))
                    nc.scalar.activation(D["sq"][:, :, :, :], D["hc"][:, :, :, :], ACT.Square).then_inc(g_sq, 1)

            e.wait_ge(g_const, 4)
            ml_order(e.Fori, pre, weights, mid, nothing, nothing, post)

        def ml_tensor(e, ln0):
            D = ml
            e.wait_ge(g_const, 2)
            nc.tensor.transpose(banks[7][:, 0:2], D["brows"][:, :], ident[0:2, 0:2]).then_inc(g_bias, 1)

            def stage(s, i, b, par):
                if s == 1:
                    e.wait_ge(xT_ready, i + ln0)
                    ln_tensor(e, i + ln0, banks[4])
                elif s == 2:
                    e.wait_ge(xT_ready, i + (ln0 + 1))
                    e.wait_ge(g_opened, max(i - 1, 0) if isinstance(i, int) else i - 1)
                    xT = D["xT"][:, bass.ds(b * NT, NT)].rearrange("p (j s) -> p s j", s=SPB)[:, par * SUP:(par + 1) * SUP, :]
                    nc.tensor.matmul(banks[5 + par][:, :].rearrange("p (s j) -> p s j", s=SUP), ml_o_w[:, :], xT, start=True,
                                     stop=True).then_inc(g_open, 1)
            pipeline(e.Fori, 3, stage)
            e.wait_ge(xT_ready, ln0 + NSUP)
            n = 0
            for k in (1, 0):
                for half in range(2):
                    for b in range(NB):
                        last = nc.tensor.matmul(banks[n][32 * b:32 * (b + 1), :], D["if_pad"][:, k, :],
                                                D["xT"][:, b * NT + half * W:b * NT + (half + 1) * W], start=True, stop=True)
                    last.then_inc(g_gate, 1)
                    n += 1
            e.wait_ge(g_rows, 20)
            for n, src in enumerate("ife"):
                for half in range(2):
                    for k in range(4):
                        last = nc.tensor.transpose(banks[2 * n + half][:, k * P:(k + 1) * P],
                                                   D[src][:, (half * 4 + k) * P:(half * 4 + k + 1) * P], ident[:, :])
                    last.then_inc(g_turn, 1)
            for g in range(2):
                for b in range(NB):
                    at = (g * NB + b) * CHUNKS
                    last = nc.tensor.matmul(banks[6][:, at:at + CHUNKS], D["heads"][32 * b:32 * (b + 1), g, :],
                                            D["f"][32 * b:32 * (b + 1), :].rearrange("p (c t) -> p c t", t=P)[:, :, P - 1],
                                            start=True, stop=True)
                    last.then_inc(g_turn, 1)
                    e.wait_ge(g_turn, 6 + g * NB + b + 1)
            e.wait_ge(g_const, 4)
            e.wait_ge(g_pconst, 2)

            def pre(c, par, k):
                e.wait_ge(g_xc, c + 1)
                if not first(c):
                    e.wait_ge(g_vkused, c * NB + ((0, 0, 1, 2)[k] + 2 - NB))
                if not (first(c) and k == 0):
                    e.wait_ge(g_b0used, pre_fill(c, k))
                nc.tensor.matmul(TB[:, :], D["qk_pad"][:, k % 2, k // 2, :], D["xc"][:, par, :], start=True,
                                 stop=True).then_inc(g_b0, 1)

            def weights(c, par, b):
                u = c * NB + b
                rows, cols = slice(32 * b, 32 * (b + 1)), slice(b * P, (b + 1) * P)
                e.wait_ge(g_bm, c + 1)
                e.wait_ge(g_D, u)
                for g in range(2):
                    dst = EB[g][:, :].rearrange("p (h s) -> p h s", h=4)
                    nc.tensor.matmul(dst, D["ac"][rows, par, :], D["ind"][rows, g * 4:(g + 1) * 4, None].to_broadcast([32, 4, P]),
                                     start=True, stop=False)
                    nc.tensor.matmul(dst, D["ones"][rows, :], D["bm"][rows, par, g * 4:(g + 1) * 4, :], start=False, stop=False)
                    last = nc.tensor.matmul(dst, identb[:, :], D["causal"][:, None, :].to_broadcast([P, 4, P]), start=False, stop=True)
                last.then_inc(g_e, 1)
                e.wait_ge(g_vkused, u)
                e.wait_ge(g_b0used, fills_before(c, b))
                nc.tensor.matmul(TB[:, 0:C + MH * MQK], D["xc"][:, par, cols], ml_vk_w[:, :], start=True,
                                 stop=True).then_inc(g_vk, 1)

            def scores(c, par, b):
                u = c * NB + b
                cols = slice(b * P, (b + 1) * P)
                e.wait_ge(g_c, u + CREDIT)
                if b == 0:
                    e.wait_ge(g_b0used, pre_fill(c, 3) + 1)
                for pair in ((2, 3), (0, 1)):
                    if pair[0] == 0:
                        e.wait_ge(g_oTused, u)
                        e.wait_ge(g_um, u)
                    for g, r in ((g, r) for g in range(2) for r in pair):
                        at = slice(32 * r, 32 * r + MQK)
                        last = nc.tensor.matmul(SB[r][:, g * P:(g + 1) * P], D["kT"][at, par, g, cols],
                                                D["qT"][at, par, g, cols], start=True, stop=True)
                last.then_inc(g_s, 1)

            def mid(c, par, b):
                u, k, n = c * NB + b, b % 2, MH * MV1
                e.wait_ge(g_c, u + (CREDIT + 1))
                e.wait_ge(g_vkused, u + 1)
                for h in range(MH):
                    r, g = h % 4, h // 4
                    nc.tensor.matmul(SB[0][32 * r:32 * (r + 1), (2 + g) * P:(3 + g) * P], D["v1"][:, k, h, :],
                                     D["D"][:, k, (r * 2 + g) * P:(r * 2 + g + 1) * P], start=True, stop=True)
                e.wait_ge(g_kw, u + 1)
                for g in range(2):
                    last = nc.tensor.matmul(SB[1][:, 2 * P + g * 4 * MV1:2 * P + (g + 1) * 4 * MV1],
                                            D["kw"][:, k, g * 4:(g + 1) * 4, :].rearrange("p h d -> p (h d)"),
                                            D["v1"][:, k, g * 4:(g + 1) * 4, 0:MV1], start=True, stop=True)
                last.then_inc(g_oT, 1)

            def back(c, par, b):
                u, k = c * NB + b, b % 2
                cols = slice(b * P, (b + 1) * P)
                e.wait_ge(g_T, u + CREDIT)
                e.wait_ge(g_state, u + 1)
                for g in range(2):
                    nc.tensor.matmul(OB[:, 2 * P + g * 4 * MV1:2 * P + (g + 1) * 4 * MV1], D["qT"][:, par, g, cols], D["S"][:, b, g, :],
                                     start=True, stop=True)
                e.wait_ge(g_oTused, u + 1)
                for g in range(2):
                    last = nc.tensor.transpose(OB[:, g * P:(g + 1) * P], D["oT"][:, k, g * P:(g + 1) * P], ident[:, :])
                last.then_inc(g_o, 1)

            def post(c, par, piece):
                if piece == 3:
                    e.wait_ge(g_y, c + 1)
                    e.wait_ge(g_b0used, y_fill(c))
                    e.wait_ge(g_vkused, CHUNKS * NB if isinstance(c, int) and c > 5 else c * NB + (2 * NB + 1))
                    for b in range(NB):
                        last = nc.tensor.transpose(TB[:, b * P:(b + 1) * P], D["y"][:, b, :], ident[:, :])
                    last.then_inc(g_b0, 1)

            ml_order(e.Fori, pre, weights, mid, scores, back, post)
            e.wait_ge(g_b0used, y_fill(CHUNKS - 1) + 1)
            for i in range(NSUP):
                b, half = divmod(i, 2)
                if i >= 2:
                    e.wait_ge(g_add, i - 1)
                for k in range(SUP):
                    last = nc.tensor.matmul(banks[2 + i % 2][:, k * C:(k + 1) * C],
                                            D["xT"][:, b * NT:(b + 1) * NT].rearrange("p (j s) -> p s j", s=SPB)[:, half * SUP + k, :],
                                            ml_down_w[:, :], start=True, stop=True)
                last.then_inc(g_down, 1)


        def run(e, name):
            mlps = []
            ln = 0
            for k, phase in enumerate(order):
                if k:
                    e.wait_ge(phase_done, 4 * k)
                if phase in ("ffn0", "ffn1"):
                    kind = int(phase[-1])
                    {"vector": mlp_vector, "scalar": mlp_scalar, "gpsimd": mlp_pool, "tensor": mlp_tensor}[name](
                        e, Mlp(kind, mlps), ln)
                    mlps.append(kind)
                else:
                    PARTS[phase][name](e, ln)
                if phase != "setup":
                    ln += NSUP
                e.drain().then_inc(phase_done, 1)

        PARTS = {"setup": {"vector": lambda e, n: setup_vector(e), "scalar": lambda e, n: setup_scalar(e),
                           "gpsimd": lambda e, n: setup_pool(e), "tensor": lambda e, n: setup_tensor(e)}}
        PARTS["lin"] = {"vector": lin_vector, "scalar": lin_scalar, "gpsimd": lin_pool, "tensor": lin_tensor}
        PARTS["rnn"] = {"vector": rnn_vector, "scalar": rnn_scalar, "gpsimd": rnn_pool, "tensor": rnn_tensor}
        PARTS["ssm"] = {"vector": ssm_vector, "scalar": ssm_scalar, "gpsimd": ssm_pool, "tensor": ssm_tensor}
        PARTS["mlstm"] = {"vector": ml_vector, "scalar": ml_scalar, "gpsimd": ml_pool, "tensor": ml_tensor}

        block = ctx.enter_context(nc.Block())

        @block.sync
        def _(e):
            setup_sync(e)
            e.wait_ge(x_loaded, 16 * NB)
            e.wait_ge(phase_done, 4 * len(order))
            for b in range(NB):
                e.dma_start(out[b].rearrange("(j s) c -> j s c", s=SPB), X[:, b * SPB:(b + 1) * SPB, :]).then_inc(stored, 16)
            e.wait_ge(stored, 16 * NB)

        @block.vector
        def _(e):
            for s in (m_upused, m_h, g_c, g_T):
                e.sem_inc(s, CREDIT)
            e.sem_inc(g_state, NB)
            e.sem_inc(s_scan, RING)
            run(e, "vector")

        @block.scalar
        def _(e):
            for s in (m_silu, m_wbs):
                e.sem_inc(s, CREDIT)
            e.sem_inc(s_da, RING)
            run(e, "scalar")

        @block.gpsimd
        def _(e):
            e.sem_inc(m_hl, CREDIT)
            e.sem_inc(s_dbu, RING)
            run(e, "gpsimd")

        @block.tensor
        def _(e):
            e.sem_inc(m_down, CREDIT)
            e.sem_inc(g_o, CREDIT)
            e.sem_inc(s_acc, RING)
            run(e, "tensor")


_INS = ['L0_attn_a_x', 'L0_attn_a_qkv_w', 'L0_attn_a_qkv_b', 'L0_attn_a_proj_w', 'L0_attn_a_proj_b', 'L0_attn_b_W_A', 'L0_attn_b_W_B', 'L0_attn_b_W_C', 'L0_ffn_Wr', 'L0_ffn_br', 'L0_ffn_Wg_s', 'L0_ffn_bg_s', 'L0_ffn_Wu_s', 'L0_ffn_bu_s', 'L0_ffn_Wd_s', 'L0_ffn_bd_s', 'L0_ffn_Wg', 'L0_ffn_bg', 'L0_ffn_Wu', 'L0_ffn_bu', 'L0_ffn_Wd', 'L0_ffn_bd', 'L1_attn_a_norm_scale', 'L1_attn_a_in_w', 'L1_attn_a_in_b', 'L1_attn_a_conv_w', 'L1_attn_a_conv_b', 'L1_attn_a_xproj_w', 'L1_attn_a_dt_w', 'L1_attn_a_dt_b', 'L1_attn_a_A_log', 'L1_attn_a_D', 'L1_attn_a_out_w', 'L1_attn_a_out_b', 'L1_attn_b_Wq', 'L1_attn_b_Wk', 'L1_attn_b_Wv', 'L1_attn_b_Wo', 'L1_attn_b_Wi', 'L1_attn_b_bi', 'L1_attn_b_Wf', 'L1_attn_b_bf', 'L1_attn_b_outnorm_w', 'L1_attn_b_Wdown', 'L1_ffn_gate_w', 'L1_ffn_w1', 'L1_ffn_w2', 'L1_ffn_w3', 'L1_ffn_w1s', 'L1_ffn_w2s', 'L1_ffn_w3s']


def kernel(**inputs):
    import numpy as _np
    import concourse.bacc as _bacc
    from concourse import mybir as _mybir
    from concourse.bass_utils import run_bass_kernel_spmd as _run

    nc = _bacc.Bacc("TRN2", target_bir_lowering=False, num_devices=1)
    arrays, aps = {}, {}
    for name in _INS:
        a = _np.ascontiguousarray(inputs[name])
        arrays[f"in_{name}"] = a
        aps[name] = nc.dram_tensor(f"in_{name}", a.shape, _mybir.dt.from_np(a.dtype), kind="ExternalInput").ap()
    out = nc.dram_tensor("out", (NB, NT, C), _mybir.dt.float32, kind="ExternalOutput").ap()
    build(nc, aps, out)
    r = _run(nc, [arrays], core_ids=[0])
    return r.results[0]["out"]
```
